# Optimizing a Trainium2 kernel written in Bass

```python
import numpy as np
import jax
import jax.numpy as jnp

def _softmax(x, axis=-1):
    return jax.nn.softmax(x, axis=axis)

def _gelu(x):
    return jax.nn.gelu(x, approximate=True)

def _silu(x):
    return jax.nn.silu(x)

def _sigmoid(x):
    return jax.nn.sigmoid(x)

def _layernorm(x, axis=-1, eps=1e-05):
    m = jnp.mean(x, axis=axis, keepdims=True)
    v = jnp.var(x, axis=axis, keepdims=True)
    return (x - m) / jnp.sqrt(v + eps)

def _scatter_add(tgt, idx, src, axis=0):
    return tgt.at[idx].add(src)

def _segment_sum(src, seg, n):
    return jax.ops.segment_sum(src, seg, n)
kernel_name = 'mk_cond_resid_d4_seqx_r4_fe799a'

def setup_inputs(seed: int=0):
    np.random.seed(seed)
    _w = jnp.asarray

    def _rec_inputs():
        import jax
        import jax.numpy as jnp
        _rk = jax.random.key(seed)
        x = -0.000125 + 0.9999 * jax.random.normal(jax.random.fold_in(_rk, 1), (128, 64, 256), jnp.float32)
        _lenS = 64 - jax.random.randint(jax.random.fold_in(_rk, 7), (128,), 0, max(1, 64 // 4) + 1, jnp.int32)
        _lenS2 = 64 - jax.random.randint(jax.random.fold_in(_rk, 8), (128,), 0, max(1, 64 // 4) + 1, jnp.int32)
        cond_512 = 0.00782532 + 1.00527 * jax.random.normal(jax.random.fold_in(_rk, 11), (128, 128), jnp.float32)
        itok_BxS_0_999 = jax.random.randint(jax.random.fold_in(_rk, 12), (128, 64), 0, 250, jnp.int32)
        itok_BxS_0_4 = jax.random.randint(jax.random.fold_in(_rk, 13), (128, 64), 0, 5, jnp.int32)
        cond_64 = 0.0990542 + 1.04422 * jax.random.normal(jax.random.fold_in(_rk, 15), (128, 64), jnp.float32)
        fside_Bx32_0 = -0.136436 + 0.990155 * jax.random.normal(jax.random.fold_in(_rk, 16), (128, 32), jnp.float32)
        _validS = jnp.arange(64)[None, :] < _lenS[:, None]
        _validS2 = jnp.arange(64)[None, :] < _lenS2[:, None]
        _causal = jnp.tril(jnp.ones((64, 64), dtype=bool))
        mask_BxS_ik0 = jnp.where(jnp.broadcast_to(_validS[:, :], (128, 64)), 0, 1).astype(jnp.int32)
        return (x, cond_512, itok_BxS_0_999, itok_BxS_0_4, cond_64, fside_Bx32_0, mask_BxS_ik0)
    x, cond_512, itok_BxS_0_999, itok_BxS_0_4, cond_64, fside_Bx32_0, mask_BxS_ik0 = _rec_inputs()

    def _L0_cond_setup():
        import jax, jax.numpy as jnp
        import numpy as np
        IN_DIM = 256
        OUT_DIM = 256
        MU_DIM = 128
        K = 30
        key = jax.random.key(seed)
        k1, k2, k3, k4, k5 = jax.random.split(key, 5)
        B, S = (16, 512)
        x = jax.random.normal(k1, (B, S, IN_DIM), dtype=jnp.float32)
        mu = jax.random.normal(k2, (B, MU_DIM), dtype=jnp.float32)
        W_dec = jax.random.normal(k3, (MU_DIM, (IN_DIM + 1) * K), dtype=jnp.float32) / np.sqrt(MU_DIM)
        b_dec = jax.random.normal(k4, ((IN_DIM + 1) * K,), dtype=jnp.float32) * 0.01
        V = jax.random.normal(k5, (K, OUT_DIM), dtype=jnp.float32) / np.sqrt(K)
        return {'x': x, 'mu': mu, 'W_dec': W_dec, 'b_dec': b_dec, 'V': V}
    _L0_cond_all = _L0_cond_setup()
    _L0_cond_in = {k: v for k, v in _L0_cond_all.items() if k in ('W_dec', 'b_dec', 'V')}
    del _L0_cond_all

    def _L1_cond_setup():
        import jax, jax.numpy as jnp
        import numpy as np
        W_DIM = 128
        CLAMP = 256.0
        key = jax.random.key(seed)
        ks = jax.random.split(key, 6)
        B, L, C = (8, 2048, 256)
        return {'x': jax.random.normal(ks[0], (B, L, C), dtype=jnp.float32), 'w': jax.random.normal(ks[1], (B, W_DIM), dtype=jnp.float32), 'weight': jax.random.normal(ks[2], (C, C), dtype=jnp.float32), 'bias': jax.random.normal(ks[3], (C,), dtype=jnp.float32), 'affine_w': jax.random.normal(ks[4], (C, W_DIM), dtype=jnp.float32), 'affine_b': jnp.ones((C,), dtype=jnp.float32)}
    _L1_cond_all = _L1_cond_setup()
    _L1_cond_in = {k: v for k, v in _L1_cond_all.items() if k in ('weight', 'bias', 'affine_w', 'affine_b')}
    del _L1_cond_all

    def _L2_cond_setup():
        import jax, jax.numpy as jnp
        import numpy as np
        B, S, D, H, C = (8, 1024, 256, 64, 128)
        INIT_RANGE = 0.01
        key = jax.random.key(seed)
        ks = jax.random.split(key, 6)
        return {'hidden_states': jax.random.normal(ks[0], (B, S, D), dtype=jnp.float32), 'conditions': jax.random.normal(ks[1], (B, C), dtype=jnp.float32), 'down_project': jax.random.normal(ks[2], (D, H), dtype=jnp.float32) * INIT_RANGE, 'down_gamma': jax.random.normal(ks[3], (C, H), dtype=jnp.float32), 'down_beta': jnp.zeros((C, H), dtype=jnp.float32), 'up_project': jax.random.normal(ks[4], (H, D), dtype=jnp.float32) * INIT_RANGE, 'up_gamma': jax.random.normal(ks[5], (C, D), dtype=jnp.float32), 'up_beta': jnp.zeros((C, D), dtype=jnp.float32)}
    _L2_cond_all = _L2_cond_setup()
    _L2_cond_in = {k: v for k, v in _L2_cond_all.items() if k in ('down_project', 'down_gamma', 'down_beta', 'up_project', 'up_gamma', 'up_beta')}
    del _L2_cond_all

    def _L3_cond_setup():
        import jax, jax.numpy as jnp
        import numpy as np
        EPS = 1e-05

        def _ln(x, g, b):
            m = jnp.mean(x, axis=-1, keepdims=True)
            v = jnp.mean((x - m) ** 2, axis=-1, keepdims=True)
            return (x - m) * jax.lax.rsqrt(v + EPS) * g + b

        def _mlp_ln(s, W1, b1, W2, b2, g, b):
            h = jax.nn.silu(s @ W1 + b1) @ W2 + b2
            return _ln(h, g, b)
        key = jax.random.key(seed)
        B, S, D = (4, 512, 256)
        MEM, NOI, RES = (128, 64, 32)
        ks = jax.random.split(key, 40)
        ki = iter(range(40))

        def nrm(shape, scale=0.02):
            return jax.random.normal(ks[next(ki)], shape, jnp.float32) * scale

        def gamma(shape):
            return jnp.ones(shape, jnp.float32) + nrm(shape)
        inp = {'x': jax.random.normal(ks[next(ki)], (B, S, D), jnp.float32), 'pathway_ids': jax.random.randint(ks[next(ki)], (B, S), 0, 250), 'compartment_ids': jax.random.randint(ks[next(ki)], (B, S), 0, 5), 'time_steps': jax.random.randint(ks[next(ki)], (B, S), 0, 5), 'scale_type': jax.random.randint(ks[next(ki)], (B, S), 0, 3), 'memory_state': jax.random.normal(ks[next(ki)], (B, MEM), jnp.float32), 'noise_state': jax.random.normal(ks[next(ki)], (B, NOI), jnp.float32), 'resource_state': jax.random.normal(ks[next(ki)], (B, RES), jnp.float32), 'pw_g': gamma((250, D)), 'pw_b': nrm((250, D)), 'cp_g': gamma((5, D)), 'cp_b': nrm((5, D)), 'tm_g': gamma((5, D)), 'tm_b': nrm((5, D)), 'ms_g': gamma((3, D)), 'ms_b': nrm((3, D)), 'mem_W1': nrm((MEM, D)), 'mem_b1': jnp.zeros((D,)), 'mem_W2': nrm((D, D)), 'mem_b2': jnp.zeros((D,)), 'mem_g': gamma((D,)), 'mem_be': jnp.zeros((D,)), 'noi_W1': nrm((NOI, D)), 'noi_b1': jnp.zeros((D,)), 'noi_W2': nrm((D, D)), 'noi_b2': jnp.zeros((D,)), 'noi_g': gamma((D,)), 'noi_be': jnp.zeros((D,)), 'res_W1': nrm((RES, D)), 'res_b1': jnp.zeros((D,)), 'res_W2': nrm((D, D)), 'res_b2': jnp.zeros((D,)), 'res_g': gamma((D,)), 'res_be': jnp.zeros((D,)), 'int_W1': nrm((6 * D, D)), 'int_b1': jnp.zeros((D,)), 'int_W2': nrm((D, D)), 'int_b2': jnp.zeros((D,)), 'int_g': gamma((D,)), 'int_be': jnp.zeros((D,)), 'aw': jnp.ones((6,), jnp.float32) / 6.0}
        return inp
    _L3_cond_all = _L3_cond_setup()
    _L3_cond_in = {k: v for k, v in _L3_cond_all.items() if k in ('pw_g', 'pw_b', 'cp_g', 'cp_b', 'tm_g', 'tm_b', 'ms_g', 'ms_b', 'mem_W1', 'mem_b1', 'mem_W2', 'mem_b2', 'mem_g', 'mem_be', 'noi_W1', 'noi_b1', 'noi_W2', 'noi_b2', 'noi_g', 'noi_be', 'res_W1', 'res_b1', 'res_W2', 'res_b2', 'res_g', 'res_be', 'int_W1', 'int_b1', 'int_W2', 'int_b2', 'int_g', 'int_be', 'aw')}
    del _L3_cond_all
    return {'x': x, 'cond_512': cond_512, 'itok_BxS_0_999': itok_BxS_0_999, 'itok_BxS_0_4': itok_BxS_0_4, 'cond_64': cond_64, 'fside_Bx32_0': fside_Bx32_0, 'mask_BxS_ik0': mask_BxS_ik0, 'L0_cond_W_dec': _L0_cond_in['W_dec'], 'L0_cond_b_dec': _L0_cond_in['b_dec'], 'L0_cond_V': _L0_cond_in['V'], 'L1_cond_weight': _L1_cond_in['weight'], 'L1_cond_bias': _L1_cond_in['bias'], 'L1_cond_affine_w': _L1_cond_in['affine_w'], 'L1_cond_affine_b': _L1_cond_in['affine_b'], 'L2_cond_down_project': _L2_cond_in['down_project'], 'L2_cond_down_gamma': _L2_cond_in['down_gamma'], 'L2_cond_down_beta': _L2_cond_in['down_beta'], 'L2_cond_up_project': _L2_cond_in['up_project'], 'L2_cond_up_gamma': _L2_cond_in['up_gamma'], 'L2_cond_up_beta': _L2_cond_in['up_beta'], 'L3_cond_pw_g': _L3_cond_in['pw_g'], 'L3_cond_pw_b': _L3_cond_in['pw_b'], 'L3_cond_cp_g': _L3_cond_in['cp_g'], 'L3_cond_cp_b': _L3_cond_in['cp_b'], 'L3_cond_tm_g': _L3_cond_in['tm_g'], 'L3_cond_tm_b': _L3_cond_in['tm_b'], 'L3_cond_ms_g': _L3_cond_in['ms_g'], 'L3_cond_ms_b': _L3_cond_in['ms_b'], 'L3_cond_mem_W1': _L3_cond_in['mem_W1'], 'L3_cond_mem_b1': _L3_cond_in['mem_b1'], 'L3_cond_mem_W2': _L3_cond_in['mem_W2'], 'L3_cond_mem_b2': _L3_cond_in['mem_b2'], 'L3_cond_mem_g': _L3_cond_in['mem_g'], 'L3_cond_mem_be': _L3_cond_in['mem_be'], 'L3_cond_noi_W1': _L3_cond_in['noi_W1'], 'L3_cond_noi_b1': _L3_cond_in['noi_b1'], 'L3_cond_noi_W2': _L3_cond_in['noi_W2'], 'L3_cond_noi_b2': _L3_cond_in['noi_b2'], 'L3_cond_noi_g': _L3_cond_in['noi_g'], 'L3_cond_noi_be': _L3_cond_in['noi_be'], 'L3_cond_res_W1': _L3_cond_in['res_W1'], 'L3_cond_res_b1': _L3_cond_in['res_b1'], 'L3_cond_res_W2': _L3_cond_in['res_W2'], 'L3_cond_res_b2': _L3_cond_in['res_b2'], 'L3_cond_res_g': _L3_cond_in['res_g'], 'L3_cond_res_be': _L3_cond_in['res_be'], 'L3_cond_int_W1': _L3_cond_in['int_W1'], 'L3_cond_int_b1': _L3_cond_in['int_b1'], 'L3_cond_int_W2': _L3_cond_in['int_W2'], 'L3_cond_int_b2': _L3_cond_in['int_b2'], 'L3_cond_int_g': _L3_cond_in['int_g'], 'L3_cond_int_be': _L3_cond_in['int_be'], 'L3_cond_aw': _L3_cond_in['aw']}

def reference(x, cond_512, itok_BxS_0_999, itok_BxS_0_4, cond_64, fside_Bx32_0, mask_BxS_ik0, L0_cond_W_dec, L0_cond_b_dec, L0_cond_V, L1_cond_weight, L1_cond_bias, L1_cond_affine_w, L1_cond_affine_b, L2_cond_down_project, L2_cond_down_gamma, L2_cond_down_beta, L2_cond_up_project, L2_cond_up_gamma, L2_cond_up_beta, L3_cond_pw_g, L3_cond_pw_b, L3_cond_cp_g, L3_cond_cp_b, L3_cond_tm_g, L3_cond_tm_b, L3_cond_ms_g, L3_cond_ms_b, L3_cond_mem_W1, L3_cond_mem_b1, L3_cond_mem_W2, L3_cond_mem_b2, L3_cond_mem_g, L3_cond_mem_be, L3_cond_noi_W1, L3_cond_noi_b1, L3_cond_noi_W2, L3_cond_noi_b2, L3_cond_noi_g, L3_cond_noi_be, L3_cond_res_W1, L3_cond_res_b1, L3_cond_res_W2, L3_cond_res_b2, L3_cond_res_g, L3_cond_res_be, L3_cond_int_W1, L3_cond_int_b1, L3_cond_int_W2, L3_cond_int_b2, L3_cond_int_g, L3_cond_int_be, L3_cond_aw):
    import jax
    import jax.numpy as jnp

    def _L0_cond_ref(x, mu, W_dec, b_dec, V):
        import jax, jax.numpy as jnp
        import numpy as np
        IN_DIM = 256
        OUT_DIM = 256
        MU_DIM = 128
        K = 30
        B = mu.shape[0]
        U = (mu @ W_dec + b_dec).reshape(B, IN_DIM + 1, K)
        param = jnp.einsum('bik,kj->bij', U, V)
        weight = param[:, :-1, :]
        bias = param[:, -1, :]
        out = jnp.einsum('bsd,bde->bse', x, weight)
        out = out + bias[:, None, :]
        return out

    def _L1_cond_ref(x, w, weight, bias, affine_w, affine_b):
        import jax, jax.numpy as jnp
        import numpy as np
        W_DIM = 128
        CLAMP = 256.0
        B, L, C = x.shape
        gain = 1.0 / np.sqrt(W_DIM).astype(np.float32)
        styles = w @ (affine_w * gain).T + affine_b
        ws = weight[None, :, :] * styles[:, None, :]
        dcoefs = jax.lax.rsqrt(jnp.sum(ws * ws, axis=2) + 1e-08)
        xm = x * styles[:, None, :]
        y = jnp.einsum('blc,oc->blo', xm, weight)
        y = y * dcoefs[:, None, :]
        y = jnp.clip(y + bias, -CLAMP, CLAMP)
        return y

    def _L2_cond_ref(hidden_states, conditions, down_project, down_gamma, down_beta, up_project, up_gamma, up_beta):
        import jax, jax.numpy as jnp
        import numpy as np
        B, S, D, H, C = (8, 1024, 256, 64, 128)
        INIT_RANGE = 0.01
        dg = conditions @ down_gamma
        db = conditions @ down_beta
        ug = conditions @ up_gamma
        ub = conditions @ up_beta
        w_down = down_project[None, :, :] * dg[:, None, :] + db[:, None, :]
        down = jnp.einsum('bsd,bdh->bsh', hidden_states, w_down)
        act = jax.nn.relu(down)
        w_up = up_project[None, :, :] * ug[:, None, :] + ub[:, None, :]
        up = jnp.einsum('bsh,bhd->bsd', act, w_up)
        return up + hidden_states

    def _L3_cond_ref(x, pathway_ids, compartment_ids, time_steps, scale_type, memory_state, noise_state, resource_state, pw_g, pw_b, cp_g, cp_b, tm_g, tm_b, ms_g, ms_b, mem_W1, mem_b1, mem_W2, mem_b2, mem_g, mem_be, noi_W1, noi_b1, noi_W2, noi_b2, noi_g, noi_be, res_W1, res_b1, res_W2, res_b2, res_g, res_be, int_W1, int_b1, int_W2, int_b2, int_g, int_be, aw):
        import jax, jax.numpy as jnp
        import numpy as np
        EPS = 1e-05

        def _ln(x, g, b):
            m = jnp.mean(x, axis=-1, keepdims=True)
            v = jnp.mean((x - m) ** 2, axis=-1, keepdims=True)
            return (x - m) * jax.lax.rsqrt(v + EPS) * g + b

        def _mlp_ln(s, W1, b1, W2, b2, g, b):
            h = jax.nn.silu(s @ W1 + b1) @ W2 + b2
            return _ln(h, g, b)
        h = _ln(x, pw_g[pathway_ids], pw_b[pathway_ids])
        h = _ln(h, cp_g[compartment_ids], cp_b[compartment_ids])
        t = _ln(x, tm_g[time_steps], tm_b[time_steps])
        m = x + _mlp_ln(memory_state, mem_W1, mem_b1, mem_W2, mem_b2, mem_g, mem_be)[:, None, :]
        n = x + _mlp_ln(noise_state, noi_W1, noi_b1, noi_W2, noi_b2, noi_g, noi_be)[:, None, :]
        r = x + _mlp_ln(resource_state, res_W1, res_b1, res_W2, res_b2, res_g, res_be)[:, None, :]
        s = _ln(x, ms_g[scale_type], ms_b[scale_type])
        w = jax.nn.softmax(aw)
        cat = jnp.concatenate([w[0] * h, w[1] * t, w[2] * m, w[3] * n, w[4] * r, w[5] * s], axis=-1)
        return _mlp_ln(cat, int_W1, int_b1, int_W2, int_b2, int_g, int_be)
    x = x + _L0_cond_ref(x, cond_512, L0_cond_W_dec, L0_cond_b_dec, L0_cond_V)
    x = x + _L1_cond_ref(x, cond_512, L1_cond_weight, L1_cond_bias, L1_cond_affine_w, L1_cond_affine_b)
    x = x + _L2_cond_ref(x, cond_512, L2_cond_down_project, L2_cond_down_gamma, L2_cond_down_beta, L2_cond_up_project, L2_cond_up_gamma, L2_cond_up_beta)
    x = x + _L3_cond_ref(x, itok_BxS_0_999, itok_BxS_0_4, itok_BxS_0_4, mask_BxS_ik0, cond_512, cond_64, fside_Bx32_0, L3_cond_pw_g, L3_cond_pw_b, L3_cond_cp_g, L3_cond_cp_b, L3_cond_tm_g, L3_cond_tm_b, L3_cond_ms_g, L3_cond_ms_b, L3_cond_mem_W1, L3_cond_mem_b1, L3_cond_mem_W2, L3_cond_mem_b2, L3_cond_mem_g, L3_cond_mem_be, L3_cond_noi_W1, L3_cond_noi_b1, L3_cond_noi_W2, L3_cond_noi_b2, L3_cond_noi_g, L3_cond_noi_be, L3_cond_res_W1, L3_cond_res_b1, L3_cond_res_W2, L3_cond_res_b2, L3_cond_res_g, L3_cond_res_be, L3_cond_int_W1, L3_cond_int_b1, L3_cond_int_W2, L3_cond_int_b2, L3_cond_int_g, L3_cond_int_be, L3_cond_aw)
    return x

_drawn_inputs = setup_inputs


def setup_inputs(seed=0):
    import zlib

    import numpy as np

    out = dict(_drawn_inputs(seed))
    spreads = {'L1_cond_affine_b': (1.0, 0.2),
     'L2_cond_down_beta': (0.0, 0.1),
     'L2_cond_up_beta': (0.0, 0.1),
     'L3_cond_mem_b1': (0.0, 0.8),
     'L3_cond_mem_b2': (0.0, 0.8),
     'L3_cond_mem_be': (0.0, 0.8),
     'L3_cond_noi_b1': (0.0, 0.8),
     'L3_cond_noi_b2': (0.0, 0.8),
     'L3_cond_noi_be': (0.0, 0.8),
     'L3_cond_res_b1': (0.0, 0.8),
     'L3_cond_res_b2': (0.0, 0.8),
     'L3_cond_res_be': (0.0, 0.8),
     'L3_cond_int_b1': (0.0, 0.8),
     'L3_cond_int_b2': (0.0, 0.8),
     'L3_cond_int_be': (0.0, 0.8),
     'L3_cond_aw': (0.1666666716337204, 0.6)}
    factors = {'cond_64': 8.0,
     'fside_Bx32_0': 8.0,
     'L0_cond_b_dec': 6.016,
     'L1_cond_bias': 8.0,
     'L2_cond_down_project': 2.89,
     'L2_cond_down_gamma': 2.842,
     'L2_cond_up_gamma': 2.678,
     'L3_cond_pw_g': 8.0,
     'L3_cond_pw_b': 8.0,
     'L3_cond_cp_g': 8.0,
     'L3_cond_cp_b': 8.0,
     'L3_cond_tm_g': 8.0,
     'L3_cond_tm_b': 8.0,
     'L3_cond_ms_g': 8.0,
     'L3_cond_ms_b': 8.0,
     'L3_cond_mem_W1': 8.0,
     'L3_cond_mem_W2': 8.0,
     'L3_cond_mem_g': 8.0,
     'L3_cond_noi_W1': 8.0,
     'L3_cond_noi_W2': 8.0,
     'L3_cond_noi_g': 8.0,
     'L3_cond_res_W1': 8.0,
     'L3_cond_res_W2': 8.0,
     'L3_cond_res_g': 8.0,
     'L3_cond_int_W1': 8.0,
     'L3_cond_int_W2': 8.0,
     'L3_cond_int_g': 8.0}
    for name, (base, spread) in spreads.items():
        noise = np.random.default_rng([zlib.crc32(name.encode()), seed]).standard_normal(out[name].shape)
        drawn = base * np.exp(spread * noise) if base else spread * noise
        out[name] = jnp.asarray(drawn.astype(out[name].dtype))
    for name, factor in factors.items():
        out[name] = (out[name] * factor).astype(out[name].dtype)
    return out
```

```python
from contextlib import ExitStack

import numpy as np
import concourse.bass as bass
from concourse import mybir

F32 = mybir.dt.float32
BF16 = mybir.dt.bfloat16
I32 = mybir.dt.int32
ACT = mybir.ActivationFunctionType
ALU = mybir.AluOpType
AX = mybir.AxisListType

B, S, D = 128, 64, 256
P = 128
ROWS = B * S
KB = D // P
CH = 512
NCH = ROWS // CH
CB = CH // S
CT = CH // P
RK = 30
MU = 128
HID = 64
NPW, NCP, NMS = 250, 5, 3
PIECES = 3
CLS = PIECES * (NCP + NMS)
BRW = PIECES * CB
EPS = 1e-5
DEMOD_EPS = 1e-8
CLAMP = 256.0
PRO = 4
LAG_A, LAG_B, LAG_C = 1, 2, 3


class Chunk:

    def __init__(self, n, half, ring):
        self.n, self.half, self.ring = n, half, ring

    def valid(self):
        return not isinstance(self.n, int) or 0 <= self.n < NCH


def wait(eng, sem, value):
    if not isinstance(value, int) or value > 0:
        eng.wait_ge(sem, value)


def settle(eng, sem):
    eng.sem_inc(sem, 1)


def run_slots(eng, order):
    def slot(base, half, k):
        for stage, lag in order:
            d = k - lag
            c = Chunk(base + d, half + (d - d % 2) // 2, d % 2)
            if c.valid():
                stage(eng, c)
    for n in range(PRO):
        slot(0, 0, n)
    with eng.Fori(PRO // 2, NCH // 2) as i:
        for k in range(2):
            slot(2 * i, i, k)
    for n in range(NCH, NCH + LAG_C):
        slot(0, 0, n)


def setup(nc, k):
    t = k["t"]
    nets = (("mem", MU), ("noi", 64), ("res", 32))
    with ExitStack() as ctx:
        def sb(name, shape, dt=F32):
            return ctx.enter_context(nc.sbuf_tensor("set_" + name, shape, dt))

        def sem(name):
            return ctx.enter_context(nc.semaphore("set_" + name))

        width = (D + 1) * RK
        wdec = sb("wdec", [MU, width])
        bdec = sb("bdec", [P, KB, RK])
        bdec_u = sb("bdec_u", [RK, 1])
        aff = sb("aff", [MU, D])
        aff_b = sb("aff_b", [P, KB])
        u_all = sb("u_all", [P, KB, B, RK])
        style2 = sb("style2", [P, KB, B])
        wsq = sb("wsq", [P, KB, D])
        dm = [sb(f"dm{n}", [P, KB, B]) for n in range(5)]
        dgb = sb("dgb", [MU, P])
        ugb = sb("ugb", [MU, 2 * D])
        ugub_row = sb("ugub_row", [B, 2 * D])
        aw = sb("aw", [P, 6])
        aw_s = [sb(f"aw_s{n}", [P, 6]) for n in range(2)]
        aw_c = [sb(f"aw_c{n}", [P, 1]) for n in range(3)]
        st = {n: sb(n + "_st", [w, B]) for n, w in nets[1:]}
        st["mem"] = k["mu_t"]
        w1n = {n: sb(n + "_w1", [w, D]) for n, w in nets}
        b1n = sb("b1n", [P, 3, KB])
        w2n = sb("w2n", [P, 3, KB, D])
        rown = sb("rown", [P, 3, 3, D])
        hid = sb("hid", [P, 3, KB, B])
        mo = [sb(f"mo{n}", [P, 3, D]) for n in range(3)]
        mo_bn = sb("mo_bn", [P, 3, 6])
        mo_mv = sb("mo_mv", [P, 3, 2])
        mo_ve = sb("mo_ve", [P, 3])
        mo_r = sb("mo_r", [P, 3])
        mo_t = sb("mo_t", [P, 3, KB, B])
        cls_t = sb("cls_t", [P, 3, KB, CLS])
        tab = [sb(f"tab{n}", [CLS, 4 * D]) for n in range(3)]
        tab_p = [sb(f"tab_p{n}", [CLS, 4 * D], BF16) for n in range(3)]
        rowb = [sb(f"rowb{n}", [B, D]) for n in range(3)]
        rowb_p = sb("rowb_p", [B, PIECES, D], BF16)
        b2f = [sb(f"b2f{n}", [PIECES, D]) for n in range(3)]
        b2p = [sb(f"b2p{n}", [PIECES, D], BF16) for n in range(3)]
        eye3 = sb("eye3", [PIECES, PIECES])

        (d_mu, d_aff, d_l1, d_w1, d_net, d_const, d_ug, d_dec0, d_dec1, d_tab, d_fin) = (
            sem(n) for n in "d_mu d_aff d_l1 d_w1 d_net d_const d_ug d_dec0 d_dec1 d_tab d_fin".split())
        (z_tab, z_pool, m_pre, m_dc, m_hid, m_mo, m_mot, m_row, m_cls, m_dec) = (
            sem(n) for n in "z_tab z_pool m_pre m_dc m_hid m_mo m_mot m_row m_cls m_dec".split())
        (c_style, c_ug, c_dc, c_hid, c_exp, c_mot, v_st2, v_dca, v_aw, v_w1, v_mve, v_mo, v_rowb, v_dec,
         v_chain, v_ugub, g_ve, g_r) = (
            sem(n) for n in ("c_style c_ug c_dc c_hid c_exp c_mot v_st2 v_dca v_aw v_w1 v_mve v_mo v_rowb v_dec "
                             "v_chain v_ugub g_ve g_r").split())
        ps_a, ps_b, ps_c, ps_d = k["ps_a"], k["ps_b"], k["ps_c"], k["ps_d"]
        flat_c = ps_c[:, :, :].rearrange("p k n -> p (k n)")
        rows_d = k["rows_of"](ps_d)

        def feat(ap, blocks=KB):
            return ap.rearrange("(k p) n -> p k n", p=P)

        def row(ap):
            return ap.rearrange("(o n) -> o n", o=1)

        block = ctx.enter_context(nc.Block())
        counts = {}

        @block.sync
        def _(eng):
            def load(s, dst, src):
                eng.dma_start(dst, src).then_inc(s, 16)
                counts[s.name] = counts.get(s.name, 0) + 16
            load(d_mu, k["mu_t"][:, :], t["cond_t"])
            load(d_aff, aff[:, :], t["aff_t"])
            load(d_aff, aff_b[:, :], t["aff_b"])
            load(d_ug, dgb[:, 0:HID], t["down_gamma"])
            load(d_ug, dgb[:, HID:P], t["down_beta"])
            load(d_ug, ugb[:, 0:D], t["up_gamma"])
            load(d_ug, ugb[:, D:2 * D], t["up_beta"])
            half = P * RK
            load(d_dec0, wdec[:, 0:half], t["W_dec"][:, 0:half])
            load(d_dec0, bdec[:, :, :], t["b_dec"][0:D * RK].rearrange("(k p r) -> p k r", k=KB, p=P))
            load(d_dec0, bdec_u[:, :], t["b_dec"][D * RK:width].rearrange("(r o) -> r o", o=1))
            load(d_dec1, wdec[:, half:width], t["W_dec"][:, half:width])
            load(d_l1, k["l1_w"][:, :, :], feat(t["l1_wt"]))
            load(d_l1, k["l1_b"][:, :], t["l1_b"])
            for n in range(2):
                load(d_const, k["onehot"][n][CLS:CLS + BRW, :], t["entry_rows"])
            load(d_fin, k["v_sb"][:, :], t["V"])
            load(d_fin, k["down_w"][:, :, 0:HID], feat(t["down_p"]))
            for h in range(2):
                load(d_fin, k["up_rep"][h * HID:(h + 1) * HID, :], t["up_p"])
            load(d_fin, k["b1"][:, :], t["int_b1"])
            load(d_fin, k["w2"][:, :, :], feat(t["int_W2"]))
            load(d_fin, k["ln_g"][:, :], row(t["int_g"]).broadcast_to([P, D]))
            load(d_fin, k["ln_be"][:, :], row(t["int_be"]).broadcast_to([P, D]))
            load(d_fin, k["pw_idx"][:, :], t["itok_t"])
            eng.wait_ge(v_ugub, 1)
            load(d_fin, k["ugub_d"], ugub_row[:, :])
            eng.wait_ge(v_rowb, 1)
            load(d_fin, k["row_d"], rowb_p[:, :, :])
            eng.wait_ge(v_dec, 2 * ((RK + 3) // 4))
            for c in range(KB):
                load(d_fin, k["u_d"][:, :, c].rearrange("n p b r -> p n (b r)"),
                     u_all[:, c].rearrange("p (n b) r -> p n (b r)", b=CB))
            eng.wait_ge(d_fin, counts[d_fin.name])

        @block.scalar
        def _(eng):
            def load(s, dst, src):
                eng.dma_start(dst, src).then_inc(s, 16)
                counts[s.name] = counts.get(s.name, 0) + 16
            load(d_w1, k["w1"][:, :, :], t["int_W1"].rearrange("(k p) n -> p k n", p=P))
            load(d_w1, aw[:, :], row(t["aw"]).broadcast_to([P, 6]))
            for n, (net, w) in enumerate(nets):
                if net != "mem":
                    load(d_net, st[net][:, :], t[net + "_t"])
                load(d_net, w1n[net][:, :], t[net + "_W1"])
                load(d_net, b1n[:, n, :], t[net + "_b1"])
                load(d_net, w2n[:, n, :, :], feat(t[net + "_W2"]))
                for m, what in enumerate(("b2", "g", "be")):
                    load(d_net, rown[:, n, m, :], row(t[f"{net}_{what}"]).broadcast_to([P, D]))
            load(d_const, k["ident"][:, :], t["ident"])
            load(d_const, k["two_i"][:, :], t["two_i"])
            load(d_const, k["cls_id"][:, :], t["cls_id"])
            load(d_const, k["piece_mask"][:, :], t["piece_mask"])
            load(d_const, eye3[:, :], t["ident"][0:PIECES, 0:PIECES])
            load(d_const, b2f[0][:, :], row(t["int_b2"]).broadcast_to([PIECES, D]))
            eng.wait_ge(z_tab, 1)
            for e in range(PIECES):
                lo = e * NCP
                load(d_tab, tab[0][lo:lo + NCP, 0:D], t["cp_g"])
                load(d_tab, tab[0][lo:lo + NCP, D:2 * D], t["tm_g"])
                load(d_tab, cls_t[:, 0, :, lo:lo + NCP], feat(t["cp_bt"]))
                load(d_tab, cls_t[:, 1, :, lo:lo + NCP], feat(t["tm_bt"]))
                lo = PIECES * NCP + e * NMS
                load(d_tab, tab[0][lo:lo + NMS, 2 * D:3 * D], t["ms_g"])
                load(d_tab, cls_t[:, 2, :, lo:lo + NMS], feat(t["ms_bt"]))
            eng.wait_ge(m_pre, 1)
            eng.wait_ge(d_aff, 32)
            for o in range(KB):
                m = eng.activation(k["style"][:, o, :], ps_a[:, 0, o * P:(o + 1) * P], ACT.Identity,
                                   bias=aff_b[:, o:o + 1], scale=float(np.float32(1.0) / np.sqrt(np.float32(MU))))
            m.then_inc(c_style, 1)
            eng.activation(k["dgdb"][:, :], ps_a[:, 0, 2 * P:3 * P], ACT.Copy)
            eng.activation(ugub_row[:, :], ps_a[:, 1, :], ACT.Copy).then_inc(v_ugub, 1)
            eng.wait_ge(v_dca, 1)
            eng.activation(dm[1][:, :, :], dm[0][:, :, :], ACT.Sqrt).then_inc(c_dc, 1)
            eng.wait_ge(v_aw, 1)
            eng.activation(aw_s[1][:, :], aw_s[0][:, :], ACT.Exp).then_inc(c_exp, 1)
            eng.wait_ge(m_hid, 1)
            eng.wait_ge(d_net, 16 * 20)
            for n in range(3):
                for o in range(KB):
                    j = n * KB + o
                    m = eng.activation(hid[:, n, o, :], flat_c[:, j * P:(j + 1) * P], ACT.Silu,
                                       bias=b1n[:, n, o:o + 1])
            m.then_inc(c_hid, 1)
            eng.wait_ge(m_mot, 1)
            eng.activation(mo_t[:, :, :, :], flat_c[:, 0:3 * KB * P].rearrange(
                "p (n k b) -> p n k b", n=3, k=KB), ACT.Copy).then_inc(c_mot, 1)

        @block.tensor
        def _(eng):
            mu = k["mu_t"][:, :]
            eng.wait_ge(d_mu, 16)
            eng.wait_ge(d_aff, 32)
            eng.wait_ge(d_ug, 64)
            for o in range(KB):
                eng.matmul(ps_a[:, 0, o * P:(o + 1) * P], aff[:, o * P:(o + 1) * P], mu, start=True, stop=True)
            eng.matmul(ps_a[:, 0, 2 * P:3 * P], dgb[:, :], mu, start=True, stop=True)
            eng.matmul(ps_a[:, 1, :], mu, ugb[:, :], start=True, stop=True).then_inc(m_pre, 1)
            eng.wait_ge(d_net, 16 * 20)
            for n, (net, _) in enumerate(nets):
                for o in range(KB):
                    j = n * KB + o
                    m = eng.matmul(flat_c[:, j * P:(j + 1) * P], w1n[net][:, o * P:(o + 1) * P], st[net][:, :],
                                   start=True, stop=True)
            m.then_inc(m_hid, 1)
            eng.wait_ge(v_st2, 1)
            for o in range(KB):
                for c in range(KB):
                    m = eng.matmul(ps_b[:, 0, o * P:(o + 1) * P], wsq[:, c, o * P:(o + 1) * P], style2[:, c, :],
                                   start=c == 0, stop=c == KB - 1)
            m.then_inc(m_dc, 1)
            eng.wait_ge(c_hid, 1)
            for n in range(3):
                for c in range(KB):
                    m = eng.matmul(rows_d[:, n, :], hid[:, n, c, :], w2n[:, n, c, :], start=c == 0, stop=c == KB - 1)
            m.then_inc(m_mo, 1)
            eng.wait_ge(v_w1, 1)
            eng.wait_ge(d_tab, 16 * 18)
            for n, first in enumerate((0, 2, 10)):
                for c in range(KB):
                    m = eng.matmul(ps_b[0:CLS, 1, 0:D], cls_t[:, n, c, :], k["w1"][:, first + c, :],
                                   start=n + c == 0, stop=n == 2 and c == KB - 1)
            m.then_inc(m_cls, 1)
            eng.wait_ge(v_mo, 1)
            eng.wait_ge(d_const, 16 * 8)
            for n in range(3):
                for c in range(KB):
                    j = n * KB + c
                    m = eng.transpose(flat_c[:, j * P:(j + 1) * P], mo[0][:, n, c * P:(c + 1) * P], k["ident"][:, :])
            m.then_inc(m_mot, 1)
            eng.wait_ge(c_mot, 1)
            eng.wait_ge(v_dca, 1)
            for n in range(3):
                for c in range(KB):
                    m = eng.matmul(ps_b[:, 0, D:2 * D], mo_t[:, n, c, :], k["w1"][:, 4 + 2 * n + c, :],
                                   start=n + c == 0, stop=n == 2 and c == KB - 1)
            m.then_inc(m_row, 1)
            w = wdec[:, :].rearrange("m (i r) -> m r i", r=RK)
            banks = (ps_a[:, 0, :], ps_a[:, 1, :], ps_d[:, 0, :], ps_d[:, 1, :])
            eng.wait_ge(d_dec0, 48)
            eng.wait_ge(v_ugub, 1)
            eng.wait_ge(v_mo, 1)
            n = 0
            for c in range(KB):
                if c:
                    eng.wait_ge(d_dec1, 16)
                for r0 in range(0, RK, 4):
                    if n >= 4:
                        eng.wait_ge(v_dec, n - 3)
                    for r in range(r0, min(r0 + 4, RK)):
                        m = eng.matmul(banks[n % 4][:, (r - r0) * B:(r - r0 + 1) * B], w[:, r, c * P:(c + 1) * P],
                                       mu, start=True, stop=True)
                    m.then_inc(m_dec, 1)
                    n += 1
            eng.wait_ge(v_dec, n - 3)
            eng.matmul(banks[n % 4][0:RK, 0:B], w[:, :, D], mu, start=True, stop=True).then_inc(m_dec, 1)

        @block.gpsimd
        def _(eng):
            eng.memset(tab[0][:, :], 0.0).then_inc(z_pool, 1)
            eng.memset(cls_t[:, :, :, :], 0.0).then_inc(z_pool, 1)
            eng.wait_ge(z_pool, 2)
            eng.sem_inc(z_tab, 1)
            eng.memset(k["mhalf"][:, :], -0.5).then_inc(z_pool, 1)
            eng.memset(k["ones3"][:, :], 1.0).then_inc(z_pool, 1)
            eng.memset(k["down_w"][:, :, HID:P], 1.0).then_inc(z_pool, 1)
            eng.memset(k["act_bd"][:, :, :], 0.0).then_inc(z_pool, 1)
            eng.wait_ge(v_mve, 1)
            eng.wait_ge(z_pool, 6)
            eng.tensor_scalar(mo_ve[:, :], mo_mv[:, :, 1], EPS, 1.0, ALU.add, ALU.mult).then_inc(g_ve, 1)
            eng.wait_ge(g_ve, 1)
            eng.tensor_tensor(mo_r[:, :], mo_ve[:, :], k["mhalf"][:, 0:3], ALU.pow).then_inc(g_r, 1)

        @block.vector
        def _(eng):
            done = [0]

            def link(ins):
                done[0] += 1
                ins.then_inc(v_chain, 1)
                eng.wait_ge(v_chain, done[0])

            def split(src, r1, r2, p1, p2, p3):
                link(eng.tensor_copy(p1, src))
                link(eng.tensor_tensor(r1, src, p1, ALU.subtract))
                link(eng.tensor_copy(p2, r1))
                link(eng.tensor_tensor(r2, r1, p2, ALU.subtract))
                link(eng.tensor_copy(p3, r2))

            def pick(out, r1, p1, p2, p3, masks):
                link(eng.tensor_scalar(r1, p1, masks[:, 0:1], None, ALU.mult))
                link(eng.scalar_tensor_tensor(r1, p2, masks[:, 1:2], r1, ALU.mult, ALU.add))
                return eng.scalar_tensor_tensor(out, p3, masks[:, 2:3], r1, ALU.mult, ALU.add)

            eng.wait_ge(d_l1, 32)
            eng.tensor_tensor(wsq[:, :, :], k["l1_w"][:, :, :], k["l1_w"][:, :, :], ALU.mult)
            eng.wait_ge(c_style, 1)
            eng.tensor_tensor(style2[:, :, :], k["style"][:, :, :], k["style"][:, :, :], ALU.mult).then_inc(v_st2, 1)
            eng.wait_ge(d_w1, 32)
            link(eng.reduce_max(aw_c[0][:, :], aw[:, :], AX.X))
            eng.tensor_scalar(aw_s[0][:, :], aw[:, :], aw_c[0][:, 0:1], None, ALU.subtract).then_inc(v_aw, 1)
            eng.wait_ge(m_dc, 1)
            link(eng.tensor_scalar(dm[0][:, :, :], ps_b[:, 0, 0:KB * P].rearrange("p (k b) -> p k b", k=KB),
                                   DEMOD_EPS, None, ALU.add))
            eng.sem_inc(v_dca, 1)
            eng.wait_ge(c_dc, 1)
            link(eng.reciprocal(dm[2][:, :, :], dm[1][:, :, :]))
            link(eng.tensor_tensor(dm[3][:, :, :], dm[0][:, :, :], dm[2][:, :, :], ALU.mult))
            link(eng.tensor_tensor(dm[4][:, :, :], dm[3][:, :, :], dm[2][:, :, :], ALU.mult))
            link(eng.tensor_scalar(dm[3][:, :, :], dm[4][:, :, :], -0.5, 1.5, ALU.mult, ALU.add))
            eng.tensor_tensor(k["dcoef"][:, :, :], dm[2][:, :, :], dm[3][:, :, :], ALU.mult)
            eng.wait_ge(c_exp, 1)
            link(eng.reduce_sum(aw_c[1][:, :], aw_s[1][:, :], AX.X))
            link(eng.reciprocal(aw_c[2][:, :], aw_c[1][:, :]))
            link(eng.tensor_scalar(aw_s[0][:, :], aw_s[1][:, :], aw_c[2][:, 0:1], None, ALU.mult))
            for n in range(6):
                part = k["w1"][:, 2 * n:2 * n + 2, :]
                last = eng.tensor_scalar(part, part, aw_s[0][:, n:n + 1], None, ALU.mult)
            link(last)
            eng.sem_inc(v_w1, 1)
            link(eng.tensor_tensor(k["w1x"][:, :, :], k["w1"][:, 4:6, :], k["w1"][:, 6:8, :], ALU.add))
            link(eng.tensor_tensor(k["w1x"][:, :, :], k["w1x"][:, :, :], k["w1"][:, 8:10, :], ALU.add))
            eng.wait_ge(m_mo, 1)
            eng.wait_ge(d_net, 16 * 20)
            link(eng.tensor_tensor(mo[1][:, :, :], rows_d[:, 0:3, :], rown[:, :, 0, :], ALU.add))
            for n in range(3):
                last = eng.bn_stats(mo_bn[:, n, :], mo[1][:, n, :])
            link(last)
            for n in range(3):
                last = eng.bn_aggr(mo_mv[:, n, :], mo_bn[:, n, :])
            last.then_inc(v_mve, 1)
            eng.wait_ge(g_r, 1)
            for n in range(3):
                last = eng.tensor_scalar(mo[2][:, n, :], mo[1][:, n, :], mo_mv[:, n, 0:1], mo_r[:, n:n + 1],
                                         ALU.subtract, ALU.mult)
            link(last)
            link(eng.tensor_tensor(mo[1][:, :, :], mo[2][:, :, :], rown[:, :, 1, :], ALU.mult))
            eng.tensor_tensor(mo[0][:, :, :], mo[1][:, :, :], rown[:, :, 2, :], ALU.add).then_inc(v_mo, 1)
            eng.wait_ge(m_cls, 1)
            eng.wait_ge(d_tab, 16 * 18)
            eng.wait_ge(d_const, 16 * 8)
            link(eng.tensor_copy(tab[0][:, 3 * D:4 * D], ps_b[0:CLS, 1, 0:D]))
            pieces = [p[:, :] for p in tab_p]
            split(tab[0][:, :], tab[1][:, :], tab[2][:, :], *pieces)
            link(pick(k["gain_tab"][:, :], tab[1][:, 0:3 * D], *(p[:, 0:3 * D] for p in pieces), k["piece_mask"]))
            for n in range(2):
                last = pick(k["shift"][n][0:CLS, :], tab[1][:, 3 * D:4 * D], *(p[:, 3 * D:4 * D] for p in pieces),
                            k["piece_mask"])
                link(last)
            pieces = [p[:, :] for p in b2p]
            split(b2f[0][:, :], b2f[1][:, :], b2f[2][:, :], *pieces)
            link(pick(k["b2_row"][:, :], b2f[1][:, :], *pieces, eye3))
            eng.wait_ge(m_row, 1)
            link(eng.tensor_copy(rowb[0][:, :], ps_b[:, 0, D:2 * D]))
            split(rowb[0][:, :], rowb[1][:, :], rowb[2][:, :], *(rowb_p[:, e, :] for e in range(PIECES)))
            eng.sem_inc(v_rowb, 1)
            banks = (ps_a[:, 0, :], ps_a[:, 1, :], ps_d[:, 0, :], ps_d[:, 1, :])
            eng.wait_ge(d_dec0, 48)
            n = 0
            for c in range(KB):
                for r0 in range(0, RK, 4):
                    w = min(4, RK - r0)
                    eng.wait_ge(m_dec, n + 1)
                    bias = bdec[:, c, r0:r0 + w].unsqueeze(2).broadcast_to([P, w, B])
                    eng.tensor_tensor(u_all[:, c, :, r0:r0 + w].rearrange("p b r -> p r b"),
                                      banks[n % 4][:, 0:w * B].rearrange("p (r b) -> p r b", b=B), bias,
                                      ALU.add).then_inc(v_dec, 1)
                    n += 1
            eng.wait_ge(m_dec, n + 1)
            link(eng.tensor_scalar(k["ub_t"][:, :], banks[n % 4][0:RK, 0:B], bdec_u[:, 0:1], None, ALU.add))


def conditioned_residuals(nc, t):
    ctx = ExitStack()
    with ctx:
        def sb(name, shape, dt=F32):
            return ctx.enter_context(nc.sbuf_tensor(name, shape, dt))

        def sem(name):
            return ctx.enter_context(nc.semaphore(name))

        ps_a, ps_b, ps_c, ps_d = (
            ctx.enter_context(nc.psum_tensor(f"ps_{n}", [P, KB, CH], F32)) for n in "abcd")

        def rows_of(ps):
            return ps[:, :, :].rearrange("p k (u d) -> p (k u) d", d=D)

        ident = sb("ident", [P, P])
        two_i = sb("two_i", [P, P])
        mhalf = sb("mhalf", [P, CT])
        cls_id = sb("cls_id", [CLS, 1])
        piece_mask = sb("piece_mask", [CLS, PIECES])
        mu_t = sb("mu_t", [MU, B])
        ub_t = sb("ub_t", [RK, B])
        v_sb = sb("v_sb", [RK, D])
        style = sb("style", [P, KB, B])
        dcoef = sb("dcoef", [P, KB, B])
        l1_w = sb("l1_w", [P, KB, D])
        l1_b = sb("l1_b", [P, KB])
        down_w = sb("down_w", [P, KB, P])
        dgdb = sb("dgdb", [P, B])
        up_rep = sb("up_rep", [P, D])
        w1 = sb("w1", [P, 12, D])
        w1x = sb("w1x", [P, KB, D])
        b1 = sb("b1", [P, KB])
        w2 = sb("w2", [P, KB, D])
        b2_row = sb("b2_row", [PIECES, D], BF16)
        ones3 = sb("ones3", [PIECES, P], BF16)
        ln_g = sb("ln_g", [P, D])
        ln_be = sb("ln_be", [P, D])
        gain_tab = sb("gain_tab", [CLS, 3 * D], BF16)
        pw_idx = sb("pw_idx", [P, ROWS // P], I32)

        ugub_d = nc.dram_tensor("ugub_scratch", (B, 2 * D), F32, kind="Internal").ap()
        u_d = nc.dram_tensor("u_scratch", (NCH, P, KB, CB, RK), F32, kind="Internal").ap()
        row_d = nc.dram_tensor("row_scratch", (B, PIECES, D), BF16, kind="Internal").ap()

        onehot = [sb(f"onehot{r}", [CLS + BRW, CH], BF16) for r in range(2)]
        shift = [sb(f"shift{r}", [CLS + BRW, D], BF16) for r in range(2)]
        act_bd = sb("act_bd", [P, CT, P])

        setup(nc, locals())

        x_in = [sb(f"x_in{r}", [P, CT, D]) for r in range(2)]
        u_ch = [sb(f"u_ch{r}", [P, KB, CB, RK]) for r in range(2)]
        ugub = [sb(f"ugub{r}", [P, CT, 2 * D]) for r in range(2)]
        idx_ch = [sb(f"idx_ch{r}", [CLS, CH], I32) for r in range(2)]
        pw_rows = [sb(f"pw_rows{r}", [P, CT, 2 * D]) for r in range(2)]
        gidx = [sb(f"gidx{r}", [P, CT], I32) for r in range(2)]
        x_t = sb("x_t", [P, KB, CH])
        t_t = sb("t_t", [RK, CH])
        x1_t = sb("x1_t", [P, KB, CH])
        xm_t = sb("xm_t", [P, KB, CH])
        l1_u = sb("l1_u", [P, KB, CH])
        x2_t = sb("x2_t", [P, KB, CH])
        dn_u = sb("dn_u", [HID, CH])
        dn_v = sb("dn_v", [HID, CH])
        dn = sb("dn", [HID, CH])
        w_up = sb("w_up", [P, CT, D])
        x3 = sb("x3", [P, CT, D])
        x3be = [sb(f"x3be{r}", [P, CT, D]) for r in range(2)]
        xhat = sb("xhat", [P, CT, D])
        h1 = sb("h1", [P, CT, D])
        x3_t = sb("x3_t", [P, KB, CH])
        xh_t = sb("xh_t", [P, KB, CH])
        hh_t = sb("hh_t", [P, KB, CH])
        tm_t = sb("tm_t", [P, KB, CH])
        ms_t = sb("ms_t", [P, KB, CH])
        h_t = sb("h_t", [P, KB, CH])
        act_t = sb("act_t", [P, KB, CH])
        y_out = [sb(f"y_out{r}", [P, CT, D]) for r in range(2)]
        bn = {k: sb(f"bn_{k}", [P, CT, 6]) for k in "xhy"}
        mv = {k: sb(f"mv_{k}", [P, CT, 2]) for k in "xhy"}
        ve = {k: sb(f"ve_{k}", [P, CT]) for k in "xhy"}
        rstd = {k: sb(f"rstd_{k}", [P, CT]) for k in "xhy"}


        s_x = [sem(f"s_x{r}") for r in range(2)]
        s_u = [sem(f"s_u{r}") for r in range(2)]
        s_ug = [sem(f"s_ug{r}") for r in range(2)]
        s_idx = [sem(f"s_idx{r}") for r in range(2)]
        s_row = [sem(f"s_row{r}") for r in range(2)]
        s_pw = [sem(f"s_pw{r}") for r in range(2)]
        s_idle = sem("s_idle")
        s_store = [sem(f"s_store{r}") for r in range(2)]
        p_xt, p_t, p_x1, p_l1, p_dn, p_up, p_x3t, p_xht, p_tm, p_ms, p_hht, p_cp, p_w1, p_w2 = (
            sem("p_" + n) for n in "xt t x1 l1 dn up x3t xht tm ms hht cp w1 w2".split())
        a_xt, a_relu, a_x3, a_x3t, a_xht, a_hht, a_silu = (
            sem("a_" + n) for n in "xt relu x3 x3t xht hht silu".split())
        (v_t, v_x1, v_l1u, v_l1v, v_x2, v_dnu, v_dn, v_bnx, v_mvx, v_xhat, v_bnh, v_mvh, v_hhat,
         v_tm, v_ms, v_h, v_bny, v_mvy, v_y1, v_y) = (
            sem("v_" + n) for n in
            "t x1 l1u l1v x2 dnu dn bnx mvx xhat bnh mvh hhat tm ms h bny mvy y1 y".split())
        (g_gidx, g_oh, g_xm, g_vex, g_rx, g_h1m, g_h1, g_veh, g_rh, g_upm, g_up, g_x3be, g_vey,
         g_ry) = (sem("g_" + n) for n in
                  "gidx oh xm vex rx h1m h1 veh rh upm up x3be vey ry".split())

        x_d = t["x"].rearrange("(c k p) d -> c p k d", k=CT, p=P)
        out_d = t["out"].rearrange("(c k p) d -> c p k d", k=CT, p=P)
        ug_d = ugub_d.rearrange("(c k h) d -> c h k d", k=CT, h=2)
        tok_d = t["itok4"].rearrange("(c o n) -> c o n", o=1, n=CH)
        mask_d = t["mask"].rearrange("(c o n) -> c o n", o=1, n=CH)
        rowc_d = row_d.rearrange("(c b) e d -> c (b e) d", b=CB)

        def one(ap, c):
            return ap[c.n]

        def cols(table, c):
            k = table.shape[1]
            return table[:, :, bass.ds(c.n * CB, CB)].unsqueeze(3).broadcast_to([P, k, CB, S])

        def by_entry(ap):
            return ap.rearrange("p k (b s) -> p k b s", s=S)

        def load(eng, c):
            r = c.ring
            wait(eng, p_xt, c.n - 1)
            eng.dma_start(x_in[r][:, :, :], one(x_d, c)).then_inc(s_x[r], 16)
            wait(eng, p_t, c.n - 1)
            eng.dma_start(u_ch[r][:, :, :, :],
                          one(u_d, c)).then_inc(s_u[r], 16)
            wait(eng, g_up, c.n - 1)
            for h in range(2):
                src = one(ug_d, c)[h:h + 1].broadcast_to([HID, CT, 2 * D])
                eng.dma_start(ugub[r][h * HID:(h + 1) * HID, :, :], src).then_inc(s_ug[r], 16)
            wait(eng, g_oh, c.n - 1)
            ncp = PIECES * NCP
            eng.dma_start(idx_ch[r][0:ncp, :], one(tok_d, c).broadcast_to([ncp, CH])).then_inc(s_idx[r], 16)
            eng.dma_start(idx_ch[r][ncp:CLS, :],
                          one(mask_d, c).broadcast_to([CLS - ncp, CH])).then_inc(s_idx[r], 16)
            wait(eng, p_w1, c.n - 1)
            eng.dma_start(shift[r][CLS:CLS + BRW, :], one(rowc_d, c)).then_inc(s_row[r], 16)

        def store(eng, c):
            wait(eng, v_y, c.n + 1)
            eng.dma_start(one(out_d, c), y_out[c.ring][:, :, :]).then_inc(s_store[c.ring], 16)

        def pe_xt(eng, c):
            wait(eng, s_x[c.ring], 16 * (c.half + 1))
            wait(eng, v_l1u, c.n)
            for k in range(KB):
                for j in range(CT):
                    m = eng.transpose(ps_a[:, k, j * P:(j + 1) * P],
                                      x_in[c.ring][:, j, k * P:(k + 1) * P], ident[:, :])
            m.then_inc(p_xt, 1)

        def pe_t(eng, c):
            wait(eng, a_xt, c.n + 1)
            wait(eng, s_u[c.ring], 16 * (c.half + 1))
            for b in range(CB):
                for k in range(KB):
                    m = eng.matmul(ps_a[0:RK, 0, b * S:(b + 1) * S], u_ch[c.ring][:, k, b, :],
                                   x_t[:, k, b * S:(b + 1) * S], start=k == 0, stop=k == KB - 1)
            m.then_inc(p_t, 1)

        def pe_x1(eng, c):
            wait(eng, v_t, c.n + 1)
            for k in range(KB):
                m = eng.matmul(ps_a[:, k, :], v_sb[:, k * P:(k + 1) * P], t_t[:, :], start=True, stop=True)
            m.then_inc(p_x1, 1)

        def pe_l1(eng, c):
            wait(eng, v_x1, c.n + 1)
            wait(eng, g_xm, c.n + 1)
            for o in range(KB):
                for k in range(KB):
                    m = eng.matmul(ps_a[:, o, :], l1_w[:, k, o * P:(o + 1) * P], xm_t[:, k, :],
                                   start=k == 0, stop=k == KB - 1)
            m.then_inc(p_l1, 1)

        def pe_dn(eng, c):
            wait(eng, v_x2, c.n + 1)
            wait(eng, v_ms, c.n)
            for k in range(KB):
                m = eng.matmul(ps_b[:, 0, :], down_w[:, k, :], x2_t[:, k, :], start=k == 0, stop=k == KB - 1)
            m.then_inc(p_dn, 1)

        def pe_up(eng, c):
            wait(eng, a_relu, c.n + 1)
            wait(eng, v_dn, c.n + 1)
            wait(eng, g_up, c.n + 1)
            out = rows_of(ps_b)
            for j in range(CT):
                eng.matmul(out[:, j, :], act_bd[:, j, :], w_up[:, j, :], start=True, stop=False)
                for k in range(KB):
                    m = eng.matmul(out[:, j, k * P:(k + 1) * P], x2_t[:, k, j * P:(j + 1) * P],
                                   two_i[:, :], start=False, stop=k == KB - 1)
            m.then_inc(p_up, 1)

        def transposes(eng, out, src):
            for k in range(KB):
                for j in range(CT):
                    m = eng.transpose(out[:, k, j * P:(j + 1) * P], src[:, j, k * P:(k + 1) * P], ident[:, :])
            return m

        def pe_xhat(eng, c):
            wait(eng, a_x3, c.n + 1)
            transposes(eng, ps_b, x3).then_inc(p_x3t, 1)
            wait(eng, v_xhat, c.n + 1)
            wait(eng, v_h, c.n)
            transposes(eng, ps_c, xhat).then_inc(p_xht, 1)

        def gains(eng, out, c, first):
            for k in range(KB):
                m = eng.matmul(out[:, k, :], gain_tab[:, first + k * P:first + (k + 1) * P],
                               onehot[c.ring][0:CLS, :], start=True, stop=True)
            return m

        def pe_gains(eng, c):
            wait(eng, g_oh, c.n + 1)
            wait(eng, a_xht, c.n + 1)
            gains(eng, ps_c, c, D).then_inc(p_tm, 1)
            wait(eng, a_x3t, c.n + 1)
            gains(eng, ps_b, c, 2 * D).then_inc(p_ms, 1)

        def pe_hhat(eng, c):
            wait(eng, v_hhat, c.n + 1)
            wait(eng, v_y1, c.n)
            transposes(eng, ps_d, h1).then_inc(p_hht, 1)

        def pe_cp(eng, c):
            wait(eng, v_tm, c.n + 1)
            gains(eng, ps_c, c, 0).then_inc(p_cp, 1)

        def pe_w1(eng, c):
            wait(eng, a_hht, c.n + 1)
            wait(eng, v_ms, c.n + 1)
            wait(eng, a_x3t, c.n + 1)
            wait(eng, s_row[c.ring], 16 * (c.half + 1))
            parts = ((w1x, 0, x3_t), (w1, 2, tm_t), (w1, 10, ms_t), (w1, 0, h_t))
            for o in range(KB):
                cut = slice(o * P, (o + 1) * P)
                eng.matmul(ps_d[:, o, :], shift[c.ring][:, cut], onehot[c.ring][:, :], start=True, stop=False)
                for w, first, act in parts[:3]:
                    for k in range(KB):
                        eng.matmul(ps_d[:, o, :], w[:, first + k, cut], act[:, k, :], start=False, stop=False)
                if o == 0:
                    wait(eng, v_h, c.n + 1)
                for k in range(KB):
                    m = eng.matmul(ps_d[:, o, :], w1[:, k, cut], h_t[:, k, :], start=False, stop=k == KB - 1)
            m.then_inc(p_w1, 1)

        def pe_w2(eng, c):
            wait(eng, a_silu, c.n + 1)
            out = rows_of(ps_d)
            for j in range(CT):
                eng.matmul(out[:, j, :], ones3[:, :], b2_row[:, :], start=True, stop=False)
                for k in range(KB):
                    m = eng.matmul(out[:, j, :], act_t[:, k, j * P:(j + 1) * P], w2[:, k, :],
                                   start=False, stop=k == KB - 1)
            m.then_inc(p_w2, 1)

        def act_xt(eng, c):
            wait(eng, p_xt, c.n + 1)
            wait(eng, v_x1, c.n)
            eng.activation(x_t[:, :, :], ps_a[:, :, :], ACT.Copy).then_inc(a_xt, 1)

        def act_relu(eng, c):
            wait(eng, v_dn, c.n + 1)
            wait(eng, p_up, c.n)
            d = dn[:, :].rearrange("h (k e s) -> h k e s", e=2, s=S)
            eng.activation(act_bd[0:HID, :, 0:S], d[:, :, 0, :], ACT.Relu)
            eng.activation(act_bd[HID:P, :, S:P], d[:, :, 1, :], ACT.Relu).then_inc(a_relu, 1)

        def act_x3(eng, c):
            wait(eng, p_up, c.n + 1)
            wait(eng, p_x3t, c.n)
            wait(eng, v_xhat, c.n)
            wait(eng, g_x3be, c.n)
            eng.activation(x3[:, :, :], rows_of(ps_b), ACT.Copy).then_inc(a_x3, 1)

        def act_x3t(eng, c):
            wait(eng, p_x3t, c.n + 1)
            wait(eng, p_w1, c.n)
            eng.activation(x3_t[:, :, :], ps_b[:, :, :], ACT.Copy).then_inc(a_x3t, 1)
            wait(eng, p_xht, c.n + 1)
            wait(eng, v_ms, c.n)
            eng.activation(xh_t[:, :, :], ps_c[:, :, :], ACT.Copy).then_inc(a_xht, 1)

        def act_hht(eng, c):
            wait(eng, p_hht, c.n + 1)
            wait(eng, v_h, c.n)
            eng.activation(hh_t[:, :, :], ps_d[:, :, :], ACT.Copy).then_inc(a_hht, 1)

        def act_silu(eng, c):
            wait(eng, p_w1, c.n + 1)
            wait(eng, p_w2, c.n)
            for k in range(KB):
                m = eng.activation(act_t[:, k, :], ps_d[:, k, :], ACT.Silu, bias=b1[:, k:k + 1])
            m.then_inc(a_silu, 1)

        def v_down(eng, c):
            wait(eng, p_dn, c.n + 1)
            wait(eng, a_relu, c.n)
            def half(ap):
                return ap.rearrange("p (b s) -> p b s", s=S)
            def dtab(lo):
                return dgdb[lo:lo + HID, bass.ds(c.n * CB, CB)].unsqueeze(2).broadcast_to([HID, CB, S])
            eng.tensor_tensor(half(dn_u[:, :]), half(ps_b[0:HID, 0, :]), dtab(0), ALU.mult)
            eng.tensor_tensor(half(dn_v[:, :]), half(ps_b[HID:P, 0, :]), dtab(HID), ALU.mult).then_inc(v_dnu, 1)
            eng.wait_ge(v_dnu, c.n + 1)
            eng.tensor_tensor(dn[:, :], dn_u[:, :], dn_v[:, :], ALU.add).then_inc(v_dn, 1)

        def v_tadd(eng, c):
            wait(eng, p_t, c.n + 1)
            wait(eng, p_x1, c.n)
            ub = ub_t[:, bass.ds(c.n * CB, CB)].unsqueeze(2).broadcast_to([RK, CB, S])
            eng.tensor_tensor(t_t[:, :].rearrange("p (b s) -> p b s", s=S),
                              ps_a[0:RK, 0, :].rearrange("p (b s) -> p b s", s=S), ub, ALU.add).then_inc(v_t, 1)

        def v_hprod(eng, c):
            wait(eng, a_hht, c.n + 1)
            wait(eng, p_cp, c.n + 1)
            wait(eng, p_w1, c.n)
            eng.tensor_tensor(h_t[:, :, :], ps_c[:, :, :], hh_t[:, :, :], ALU.mult).then_inc(v_h, 1)

        def v_x1add(eng, c):
            wait(eng, p_x1, c.n + 1)
            wait(eng, g_xm, c.n)
            wait(eng, v_x2, c.n)
            eng.tensor_tensor(x1_t[:, :, :], ps_a[:, :, :], x_t[:, :, :], ALU.add).then_inc(v_x1, 1)

        def stats(eng, c, k, src, s_bn, s_mv):
            for j in range(CT):
                m = eng.bn_stats(bn[k][:, j, :], src[:, j, :])
            m.then_inc(s_bn, 1)
            eng.wait_ge(s_bn, c.n + 1)
            settle(eng, s_idle)
            for j in range(CT):
                m = eng.bn_aggr(mv[k][:, j, :], bn[k][:, j, :])
            m.then_inc(s_mv, 1)

        def normalise(eng, k, out, src):
            for j in range(CT):
                m = eng.tensor_scalar(out[:, j, :], src[:, j, :], mv[k][:, j, 0:1], rstd[k][:, j:j + 1],
                                      ALU.subtract, ALU.mult)
            return m

        def v_xstat(eng, c):
            wait(eng, a_x3, c.n + 1)
            wait(eng, g_vex, c.n)
            stats(eng, c, "x", x3, v_bnx, v_mvx)

        def v_xnorm(eng, c):
            wait(eng, g_rx, c.n + 1)
            wait(eng, p_xht, c.n)
            wait(eng, g_h1m, c.n)
            normalise(eng, "x", xhat, x3).then_inc(v_xhat, 1)

        def v_hstat(eng, c):
            wait(eng, g_h1, c.n + 1)
            stats(eng, c, "h", h1, v_bnh, v_mvh)

        def v_hnorm(eng, c):
            wait(eng, g_rh, c.n + 1)
            normalise(eng, "h", h1, h1).then_inc(v_hhat, 1)

        def v_l1(eng, c):
            wait(eng, p_l1, c.n + 1)
            eng.tensor_tensor(by_entry(l1_u[:, :, :]), by_entry(ps_a[:, :, :]), cols(dcoef, c),
                              ALU.mult).then_inc(v_l1u, 1)
            eng.wait_ge(v_l1u, c.n + 1)
            for k in range(KB):
                m = eng.tensor_scalar(l1_u[:, k, :], l1_u[:, k, :], l1_b[:, k:k + 1], CLAMP, ALU.add, ALU.min)
            m.then_inc(v_l1v, 1)
            eng.wait_ge(v_l1v, c.n + 1)
            wait(eng, p_up, c.n)
            eng.scalar_tensor_tensor(x2_t[:, :, :], l1_u[:, :, :], -CLAMP, x1_t[:, :, :],
                                     ALU.max, ALU.add).then_inc(v_x2, 1)

        def v_gprod(eng, c):
            wait(eng, a_xht, c.n + 1)
            wait(eng, p_w1, c.n)
            wait(eng, p_tm, c.n + 1)
            eng.tensor_tensor(tm_t[:, :, :], ps_c[:, :, :], xh_t[:, :, :], ALU.mult).then_inc(v_tm, 1)
            wait(eng, p_ms, c.n + 1)
            eng.tensor_tensor(ms_t[:, :, :], ps_b[:, :, :], xh_t[:, :, :], ALU.mult).then_inc(v_ms, 1)

        def v_final(eng, c):
            wait(eng, p_w2, c.n + 1)
            out = rows_of(ps_d)
            stats(eng, c, "y", out, v_bny, v_mvy)
            eng.wait_ge(v_mvy, c.n + 1)
            wait(eng, s_store[c.ring], 16 * c.half)
            for j in range(CT):
                m = eng.scalar_tensor_tensor(y_out[c.ring][:, j, :], out[:, j, :], mv["y"][:, j, 0:1], ln_g[:, :],
                                             ALU.subtract, ALU.mult)
            m.then_inc(v_y1, 1)
            eng.wait_ge(v_y1, c.n + 1)
            wait(eng, g_ry, c.n + 1)
            wait(eng, g_x3be, c.n + 1)
            for j in range(CT):
                m = eng.scalar_tensor_tensor(y_out[c.ring][:, j, :], y_out[c.ring][:, j, :], rstd["y"][:, j:j + 1],
                                             x3be[c.ring][:, j, :], ALU.mult, ALU.add)
            m.then_inc(v_y, 1)

        def g_gather(eng, c):
            wait(eng, g_h1, c.n - 1)
            wait(eng, s_pw[c.ring], 16 * CT * c.half)
            eng.tensor_copy(gidx[c.ring][:, :], pw_idx[:, bass.ds(c.n * CT, CT)]).then_inc(g_gidx, 1)
            eng.wait_ge(g_gidx, c.n + 1)
            settle(eng, s_idle)
            for j in range(CT):
                eng.indirect_dma_start(
                    pw_rows[c.ring][:, j, :], None, t["pw"],
                    bass.IndirectOffsetOnAxis(ap=gidx[c.ring][:, j:j + 1], axis=0)).then_inc(s_pw[c.ring], 16)

        def g_onehot(eng, c):
            wait(eng, s_idx[c.ring], 32 * (c.half + 1))
            wait(eng, p_w1, c.n - 1)
            settle(eng, s_idle)
            eng.tensor_scalar(onehot[c.ring][0:CLS, :], idx_ch[c.ring][:, :], cls_id[:, 0:1], None,
                              ALU.is_equal).then_inc(g_oh, 1)

        def g_style(eng, c):
            wait(eng, v_x1, c.n + 1)
            wait(eng, p_l1, c.n)
            eng.tensor_tensor(by_entry(xm_t[:, :, :]), by_entry(x1_t[:, :, :]), cols(style, c),
                              ALU.mult).then_inc(g_xm, 1)

        def root(eng, c, k, s_mv, s_ve, s_r):
            wait(eng, s_mv, c.n + 1)
            settle(eng, s_idle)
            eng.tensor_scalar(ve[k][:, :], mv[k][:, :, 1], EPS, 1.0, ALU.add, ALU.mult).then_inc(s_ve, 1)
            eng.wait_ge(s_ve, c.n + 1)
            eng.tensor_tensor(rstd[k][:, :], ve[k][:, :], mhalf[:, :], ALU.pow).then_inc(s_r, 1)

        def g_rootx(eng, c):
            wait(eng, v_xhat, c.n)
            root(eng, c, "x", v_mvx, g_vex, g_rx)

        def g_h(eng, c):
            wait(eng, v_xhat, c.n + 1)
            wait(eng, s_pw[c.ring], 16 * CT * (c.half + 1))
            wait(eng, p_hht, c.n)
            eng.tensor_tensor(h1[:, :, :], xhat[:, :, :], pw_rows[c.ring][:, :, 0:D], ALU.mult).then_inc(g_h1m, 1)
            eng.wait_ge(g_h1m, c.n + 1)
            eng.tensor_tensor(h1[:, :, :], h1[:, :, :], pw_rows[c.ring][:, :, D:2 * D], ALU.add).then_inc(g_h1, 1)

        def g_rooth(eng, c):
            root(eng, c, "h", v_mvh, g_veh, g_rh)

        def g_wup(eng, c):
            wait(eng, s_ug[c.ring], 32 * (c.half + 1))
            wait(eng, p_up, c.n)
            eng.tensor_tensor(w_up[:, :, :], up_rep[:, :].unsqueeze(1).broadcast_to([P, CT, D]), ugub[c.ring][:, :, 0:D], ALU.mult).then_inc(g_upm, 1)
            eng.wait_ge(g_upm, c.n + 1)
            eng.tensor_tensor(w_up[:, :, :], w_up[:, :, :], ugub[c.ring][:, :, D:2 * D], ALU.add).then_inc(g_up, 1)

        def g_res(eng, c):
            wait(eng, a_x3, c.n + 1)
            wait(eng, v_y, c.n - 1)
            eng.tensor_tensor(x3be[c.ring][:, :, :], x3[:, :, :], ln_be[:, :].unsqueeze(1).broadcast_to([P, CT, D]), ALU.add).then_inc(g_x3be, 1)

        def g_rooty(eng, c):
            wait(eng, v_y, c.n)
            root(eng, c, "y", v_mvy, g_vey, g_ry)

        block = ctx.enter_context(nc.Block())

        @block.sync
        def _(eng):
            run_slots(eng, [(load, 0), (store, LAG_C)])
            for r in range(2):
                eng.wait_ge(s_store[r], 16 * NCH // 2)

        @block.tensor
        def _(eng):
            run_slots(eng, [(pe_xt, LAG_A), (pe_hhat, LAG_C), (pe_dn, LAG_B), (pe_t, LAG_A), (pe_cp, LAG_C),
                            (pe_up, LAG_B), (pe_x1, LAG_A), (pe_w1, LAG_C), (pe_xhat, LAG_B),
                            (pe_l1, LAG_A), (pe_gains, LAG_B), (pe_w2, LAG_C)])

        @block.scalar
        def _(eng):
            run_slots(eng, [(act_xt, LAG_A), (act_hht, LAG_C), (act_relu, LAG_B), (act_x3, LAG_B),
                            (act_silu, LAG_C), (act_x3t, LAG_B)])

        @block.vector
        def _(eng):
            run_slots(eng, [(v_down, LAG_B), (v_tadd, LAG_A), (v_hprod, LAG_C), (v_x1add, LAG_A),
                            (v_xstat, LAG_B), (v_xnorm, LAG_B), (v_hstat, LAG_B), (v_hnorm, LAG_B),
                            (v_l1, LAG_A), (v_gprod, LAG_B), (v_final, LAG_C)])

        @block.gpsimd
        def _(eng):
            run_slots(eng, [(g_gather, LAG_A), (g_onehot, LAG_B), (g_style, LAG_A), (g_rootx, LAG_B),
                            (g_h, LAG_B), (g_rooth, LAG_B), (g_res, LAG_B), (g_wup, LAG_A),
                            (g_rooty, LAG_C)])


def kernel(**inputs):
    import numpy as np
    import ml_dtypes
    import concourse.bacc as bacc
    from concourse import mybir
    from concourse.bass_utils import run_bass_kernel_spmd

    a = {n: np.asarray(v) for n, v in inputs.items()}
    lay = np.ascontiguousarray

    def by_block(v):
        return lay(v.reshape(KB, P).T)

    ncls = PIECES * (NCP + NMS)
    cls_id = np.concatenate([np.tile(np.arange(NCP), PIECES), np.tile(np.arange(NMS), PIECES)])
    piece = np.concatenate([np.repeat(np.arange(PIECES), NCP), np.repeat(np.arange(PIECES), NMS)])
    entry = np.repeat(np.arange(CB), PIECES)
    arrays = {
        "ident": np.eye(P, dtype=np.float32),
        "two_i": 2 * np.eye(P, dtype=np.float32),
        "cls_id": cls_id.astype(np.float32).reshape(ncls, 1),
        "piece_mask": (piece[:, None] == np.arange(PIECES)[None, :]).astype(np.float32),
        "entry_rows": (entry[:, None] == np.repeat(np.arange(CB), S)[None, :]).astype(ml_dtypes.bfloat16),
    }
    arrays.update({
        "x": a["x"].reshape(ROWS, D),
        "cond_t": lay(a["cond_512"].T),
        "noi_t": lay(a["cond_64"].T),
        "res_t": lay(a["fside_Bx32_0"].T),
        "itok_t": lay(a["itok_BxS_0_999"].reshape(ROWS // P, P).T),
        "itok4": a["itok_BxS_0_4"].reshape(ROWS),
        "mask": a["mask_BxS_ik0"].reshape(ROWS),
        "W_dec": a["L0_cond_W_dec"], "b_dec": a["L0_cond_b_dec"], "V": a["L0_cond_V"],
        "l1_wt": lay(a["L1_cond_weight"].T), "l1_b": by_block(a["L1_cond_bias"]),
        "aff_t": lay(a["L1_cond_affine_w"].T), "aff_b": by_block(a["L1_cond_affine_b"]),
        "down_p": a["L2_cond_down_project"], "down_gamma": a["L2_cond_down_gamma"],
        "down_beta": a["L2_cond_down_beta"], "up_p": a["L2_cond_up_project"],
        "up_gamma": a["L2_cond_up_gamma"], "up_beta": a["L2_cond_up_beta"],
        "pw": lay(np.concatenate([a["L3_cond_pw_g"], a["L3_cond_pw_b"]], axis=1)),
        "cp_g": a["L3_cond_cp_g"], "cp_bt": lay(a["L3_cond_cp_b"].T),
        "tm_g": a["L3_cond_tm_g"], "tm_bt": lay(a["L3_cond_tm_b"].T),
        "ms_g": a["L3_cond_ms_g"], "ms_bt": lay(a["L3_cond_ms_b"].T),
        "aw": a["L3_cond_aw"],
    })
    for net in ("mem", "noi", "res", "int"):
        for part in ("W1", "b1", "W2", "b2", "g", "be"):
            v = a[f"L3_cond_{net}_{part}"]
            arrays[f"{net}_{part}"] = by_block(v) if part == "b1" else v

    nc = bacc.Bacc("TRN2", target_bir_lowering=False, num_devices=1)
    t, placed = {}, {}
    for name, v in arrays.items():
        v = lay(v)
        placed["in_" + name] = v
        t[name] = nc.dram_tensor("in_" + name, v.shape, mybir.dt.from_np(v.dtype), kind="ExternalInput").ap()
    t["out"] = nc.dram_tensor("out", (ROWS, D), mybir.dt.float32, kind="ExternalOutput").ap()
    conditioned_residuals(nc, t)
    r = run_bass_kernel_spmd(nc, [placed], core_ids=[0])
    return r.results[0]["out"].reshape(B, S, D)
```

```python
from contextlib import ExitStack

import numpy as np
import concourse.bass as bass
from concourse import mybir

F32 = mybir.dt.float32
F32R = mybir.dt.float32r
BF16 = mybir.dt.bfloat16
I32 = mybir.dt.int32
ACT = mybir.ActivationFunctionType
ALU = mybir.AluOpType
AX = mybir.AxisListType

B, S, D = 128, 64, 256
P = 128
ROWS = B * S
KB = D // P
CH = 512
NCH = ROWS // CH
CB = CH // S
CT = CH // P
RK = 30
MU = 128
HID = 64
NPW, NCP, NMS = 250, 5, 3
PIECES = 3
CLS = PIECES * (NCP + NMS)
BRW = PIECES * CB
EPS = 1e-5
DEMOD_EPS = 1e-8
CLAMP = 256.0
LAG_A, LAG_B, LAG_C, LAG_D = 1, 2, 3, 4


class Chunk:

    def __init__(self, n, half, ring):
        self.n, self.half, self.ring = n, half, ring

    def valid(self):
        return not isinstance(self.n, int) or 0 <= self.n < NCH


def wait(eng, sem, value):
    if not isinstance(value, int) or value > 0:
        eng.wait_ge(sem, value)


def settle(eng, sem):
    eng.sem_inc(sem, 1)


def run_slots(eng, order):
    last = max(lag for _, lag in order)
    fill = last + 2 - last % 2
    def slot(base, half, k):
        for stage, lag in order:
            d = k - lag
            c = Chunk(base + d, half + (d - d % 2) // 2, d % 2)
            if c.valid():
                stage(eng, c)
    for n in range(fill):
        slot(0, 0, n)
    with eng.Fori(fill // 2, NCH // 2) as i:
        for k in range(2):
            slot(2 * i, i, k)
    for n in range(NCH, NCH + last):
        slot(0, 0, n)


def setup(nc, k):
    t = k["t"]
    nets = (("mem", MU), ("noi", 64), ("res", 32))
    with ExitStack() as ctx:
        def sb(name, shape, dt=F32):
            return ctx.enter_context(nc.sbuf_tensor("set_" + name, shape, dt))

        def sem(name):
            return ctx.enter_context(nc.semaphore("set_" + name))

        width = (D + 1) * RK
        wdec = sb("wdec", [MU, width])
        bdec = sb("bdec", [P, KB, RK])
        bdec_u = sb("bdec_u", [RK, 1])
        aff = sb("aff", [MU, D])
        aff_b = sb("aff_b", [P, KB])
        u_all = sb("u_all", [P, KB, B, RK])
        style2 = sb("style2", [P, KB, B])
        wsq = sb("wsq", [P, KB, D])
        l1_w = sb("l1_w", [P, KB, D])
        down_w = sb("down_w", [P, KB, P])
        w1 = sb("w1", [P, 12, D])
        w1x = sb("w1x", [P, KB, D])
        w2 = sb("w2", [P, KB, D])
        two_i = sb("two_i", [P, P])
        dm = [sb(f"dm{n}", [P, KB, B]) for n in range(5)]
        dgb = sb("dgb", [MU, P])
        ugb = sb("ugb", [MU, 2 * D])
        ugub_row = sb("ugub_row", [B, 2 * D])
        aw = sb("aw", [P, 6])
        aw_s = [sb(f"aw_s{n}", [P, 6]) for n in range(2)]
        aw_c = [sb(f"aw_c{n}", [P, 1]) for n in range(3)]
        st = {n: sb(n + "_st", [w, B]) for n, w in nets[1:]}
        st["mem"] = k["mu_t"]
        w1n = {n: sb(n + "_w1", [w, D]) for n, w in nets}
        b1n = sb("b1n", [P, 3, KB])
        w2n = sb("w2n", [P, 3, KB, D])
        rown = sb("rown", [P, 3, 3, D])
        hid = sb("hid", [P, 3, KB, B])
        mo = [sb(f"mo{n}", [P, 3, D]) for n in range(3)]
        mo_bn = sb("mo_bn", [P, 3, 6])
        mo_mv = sb("mo_mv", [P, 3, 2])
        mo_ve = sb("mo_ve", [P, 3])
        mo_r = sb("mo_r", [P, 3])
        mo_t = sb("mo_t", [P, 3, KB, B])
        cls_t = sb("cls_t", [P, 3, KB, CLS])
        tab = [sb(f"tab{n}", [CLS, 4 * D]) for n in range(3)]
        tab_p = [sb(f"tab_p{n}", [CLS, 4 * D], BF16) for n in range(3)]
        rowb = [sb(f"rowb{n}", [B, D]) for n in range(3)]
        rowb_p = sb("rowb_p", [B, PIECES, D], BF16)
        b2f = [sb(f"b2f{n}", [PIECES, D]) for n in range(3)]
        b2p = [sb(f"b2p{n}", [PIECES, D], BF16) for n in range(3)]
        eye3 = sb("eye3", [PIECES, PIECES])

        (d_mu, d_aff, d_l1, d_w1, d_net, d_const, d_ug, d_dec0, d_dec1, d_tab, d_fin, d_wts) = (
            sem(n) for n in "d_mu d_aff d_l1 d_w1 d_net d_const d_ug d_dec0 d_dec1 d_tab d_fin d_wts".split())
        (z_tab, z_pool, m_pre, m_dc, m_hid, m_mo, m_mot, m_row, m_cls, m_dec) = (
            sem(n) for n in "z_tab z_pool m_pre m_dc m_hid m_mo m_mot m_row m_cls m_dec".split())
        (c_style, c_ug, c_dc, c_hid, c_exp, c_mot, v_st2, v_dca, v_aw, v_w1, v_mve, v_mo, v_rowb, v_dec,
         v_chain, v_ugub, g_ve, g_r) = (
            sem(n) for n in ("c_style c_ug c_dc c_hid c_exp c_mot v_st2 v_dca v_aw v_w1 v_mve v_mo v_rowb v_dec "
                             "v_chain v_ugub g_ve g_r").split())
        ps_a, ps_b, ps_c, ps_d = k["ps_a"], k["ps_b"], k["ps_c"], k["ps_d"]
        flat_c = ps_c[:, :, :].rearrange("p k n -> p (k n)")
        rows_d = k["rows_of"](ps_d)

        def feat(ap, blocks=KB):
            return ap.rearrange("(k p) n -> p k n", p=P)

        def row(ap):
            return ap.rearrange("(o n) -> o n", o=1)

        block = ctx.enter_context(nc.Block())
        counts = {}

        @block.sync
        def _(eng):
            def load(s, dst, src):
                eng.dma_start(dst, src).then_inc(s, 16)
                counts[s.name] = counts.get(s.name, 0) + 16
            load(d_mu, k["mu_t"][:, :], t["cond_t"])
            load(d_aff, aff[:, :], t["aff_t"])
            load(d_aff, aff_b[:, :], t["aff_b"])
            load(d_ug, dgb[:, 0:HID], t["down_gamma"])
            load(d_ug, dgb[:, HID:P], t["down_beta"])
            load(d_ug, ugb[:, 0:D], t["up_gamma"])
            load(d_ug, ugb[:, D:2 * D], t["up_beta"])
            half = P * RK
            load(d_dec0, wdec[:, 0:half], t["W_dec"][:, 0:half])
            load(d_dec0, bdec[:, :, :], t["b_dec"][0:D * RK].rearrange("(k p r) -> p k r", k=KB, p=P))
            load(d_dec0, bdec_u[:, :], t["b_dec"][D * RK:width].rearrange("(r o) -> r o", o=1))
            load(d_dec1, wdec[:, half:width], t["W_dec"][:, half:width])
            load(d_l1, l1_w[:, :, :], feat(t["l1_wt"]))
            load(d_l1, k["l1_b"][:, :], t["l1_b"])
            for n in range(2):
                load(d_const, k["onehot"][n][CLS:CLS + BRW, :], t["entry_rows"])
            load(d_fin, k["v_sb"][:, :], t["V"])
            load(d_wts, down_w[:, :, 0:HID], feat(t["down_p"]))
            for h in range(2):
                load(d_fin, k["up_rep"][h * HID:(h + 1) * HID, :], t["up_p"])
            load(d_fin, k["b1"][:, :], t["int_b1"])
            load(d_wts, w2[:, :, :], feat(t["int_W2"]))
            load(d_fin, k["ln_g"][:, :], row(t["int_g"]).broadcast_to([P, D]))
            load(d_fin, k["ln_be"][:, :], row(t["int_be"]).broadcast_to([P, D]))
            load(d_fin, k["pw_idx"][:, :], t["itok_t"])
            eng.wait_ge(v_ugub, 1)
            load(d_fin, k["ugub_d"], ugub_row[:, :])
            eng.wait_ge(v_rowb, 1)
            load(d_fin, k["row_d"], rowb_p[:, :, :])
            eng.wait_ge(v_dec, 2 * ((RK + 3) // 4))
            for c in range(KB):
                load(d_fin, k["u_d"][:, :, c].rearrange("n p b r -> p n (b r)"),
                     u_all[:, c].rearrange("p (n b) r -> p n (b r)", b=CB))
            eng.wait_ge(d_fin, counts[d_fin.name])

        @block.scalar
        def _(eng):
            def load(s, dst, src):
                eng.dma_start(dst, src).then_inc(s, 16)
                counts[s.name] = counts.get(s.name, 0) + 16
            load(d_w1, w1[:, :, :], t["int_W1"].rearrange("(k p) n -> p k n", p=P))
            load(d_w1, aw[:, :], row(t["aw"]).broadcast_to([P, 6]))
            for n, (net, w) in enumerate(nets):
                if net != "mem":
                    load(d_net, st[net][:, :], t[net + "_t"])
                load(d_net, w1n[net][:, :], t[net + "_W1"])
                load(d_net, b1n[:, n, :], t[net + "_b1"])
                load(d_net, w2n[:, n, :, :], feat(t[net + "_W2"]))
                for m, what in enumerate(("b2", "g", "be")):
                    load(d_net, rown[:, n, m, :], row(t[f"{net}_{what}"]).broadcast_to([P, D]))
            load(d_const, k["ident"][:, :], t["ident"])
            load(d_const, two_i[:, :], t["two_i"])
            load(d_const, k["cls_neg"][:, :], t["cls_neg"])
            load(d_const, k["piece_mask"][:, :], t["piece_mask"])
            load(d_const, eye3[:, :], t["ident"][0:PIECES, 0:PIECES])
            load(d_const, b2f[0][:, :], row(t["int_b2"]).broadcast_to([PIECES, D]))
            eng.wait_ge(z_tab, 1)
            for e in range(PIECES):
                lo = e * NCP
                load(d_tab, tab[0][lo:lo + NCP, 0:D], t["cp_g"])
                load(d_tab, tab[0][lo:lo + NCP, D:2 * D], t["tm_g"])
                load(d_tab, cls_t[:, 0, :, lo:lo + NCP], feat(t["cp_bt"]))
                load(d_tab, cls_t[:, 1, :, lo:lo + NCP], feat(t["tm_bt"]))
                lo = PIECES * NCP + e * NMS
                load(d_tab, tab[0][lo:lo + NMS, 2 * D:3 * D], t["ms_g"])
                load(d_tab, cls_t[:, 2, :, lo:lo + NMS], feat(t["ms_bt"]))
            eng.wait_ge(m_pre, 1)
            eng.wait_ge(d_aff, 32)
            for o in range(KB):
                m = eng.activation(k["style"][:, o, :], ps_a[:, 0, o * P:(o + 1) * P], ACT.Identity,
                                   bias=aff_b[:, o:o + 1], scale=float(np.float32(1.0) / np.sqrt(np.float32(MU))))
            m.then_inc(c_style, 1)
            eng.activation(k["dgdb"][:, :], ps_a[:, 0, 2 * P:3 * P], ACT.Copy)
            eng.activation(ugub_row[:, :], ps_a[:, 1, :], ACT.Copy).then_inc(v_ugub, 1)
            eng.wait_ge(v_dca, 1)
            eng.activation(dm[1][:, :, :], dm[0][:, :, :], ACT.Sqrt).then_inc(c_dc, 1)
            eng.wait_ge(v_aw, 1)
            eng.activation(aw_s[1][:, :], aw_s[0][:, :], ACT.Exp).then_inc(c_exp, 1)
            eng.wait_ge(m_hid, 1)
            eng.wait_ge(d_net, 16 * 20)
            for n in range(3):
                for o in range(KB):
                    j = n * KB + o
                    m = eng.activation(hid[:, n, o, :], flat_c[:, j * P:(j + 1) * P], ACT.Silu,
                                       bias=b1n[:, n, o:o + 1])
            m.then_inc(c_hid, 1)
            eng.wait_ge(m_mot, 1)
            eng.activation(mo_t[:, :, :, :], flat_c[:, 0:3 * KB * P].rearrange(
                "p (n k b) -> p n k b", n=3, k=KB), ACT.Copy).then_inc(c_mot, 1)

        @block.tensor
        def _(eng):
            mu = k["mu_t"][:, :]
            eng.wait_ge(d_mu, 16)
            eng.wait_ge(d_aff, 32)
            eng.wait_ge(d_ug, 64)
            for o in range(KB):
                eng.matmul(ps_a[:, 0, o * P:(o + 1) * P], aff[:, o * P:(o + 1) * P], mu, start=True, stop=True)
            eng.matmul(ps_a[:, 0, 2 * P:3 * P], dgb[:, :], mu, start=True, stop=True)
            eng.matmul(ps_a[:, 1, :], mu, ugb[:, :], start=True, stop=True).then_inc(m_pre, 1)
            eng.wait_ge(d_net, 16 * 20)
            for n, (net, _) in enumerate(nets):
                for o in range(KB):
                    j = n * KB + o
                    m = eng.matmul(flat_c[:, j * P:(j + 1) * P], w1n[net][:, o * P:(o + 1) * P], st[net][:, :],
                                   start=True, stop=True)
            m.then_inc(m_hid, 1)
            eng.wait_ge(v_st2, 1)
            for o in range(KB):
                for c in range(KB):
                    m = eng.matmul(ps_b[:, 0, o * P:(o + 1) * P], wsq[:, c, o * P:(o + 1) * P], style2[:, c, :],
                                   start=c == 0, stop=c == KB - 1)
            m.then_inc(m_dc, 1)
            eng.wait_ge(c_hid, 1)
            for n in range(3):
                for c in range(KB):
                    m = eng.matmul(rows_d[:, n, :], hid[:, n, c, :], w2n[:, n, c, :], start=c == 0, stop=c == KB - 1)
            m.then_inc(m_mo, 1)
            eng.wait_ge(v_w1, 1)
            eng.wait_ge(d_tab, 16 * 18)
            for n, first in enumerate((0, 2, 10)):
                for c in range(KB):
                    m = eng.matmul(ps_b[0:CLS, 1, 0:D], cls_t[:, n, c, :], w1[:, first + c, :],
                                   start=n + c == 0, stop=n == 2 and c == KB - 1)
            m.then_inc(m_cls, 1)
            eng.wait_ge(v_mo, 1)
            eng.wait_ge(d_const, 16 * 8)
            for n in range(3):
                for c in range(KB):
                    j = n * KB + c
                    m = eng.transpose(flat_c[:, j * P:(j + 1) * P], mo[0][:, n, c * P:(c + 1) * P], k["ident"][:, :])
            m.then_inc(m_mot, 1)
            eng.wait_ge(c_mot, 1)
            eng.wait_ge(v_dca, 1)
            for n in range(3):
                for c in range(KB):
                    m = eng.matmul(ps_b[:, 0, D:2 * D], mo_t[:, n, c, :], w1[:, 4 + 2 * n + c, :],
                                   start=n + c == 0, stop=n == 2 and c == KB - 1)
            m.then_inc(m_row, 1)
            w = wdec[:, :].rearrange("m (i r) -> m r i", r=RK)
            banks = (ps_a[:, 0, :], ps_a[:, 1, :], ps_d[:, 0, :], ps_d[:, 1, :])
            eng.wait_ge(d_dec0, 48)
            eng.wait_ge(v_ugub, 1)
            eng.wait_ge(v_mo, 1)
            n = 0
            for c in range(KB):
                if c:
                    eng.wait_ge(d_dec1, 16)
                for r0 in range(0, RK, 4):
                    if n >= 4:
                        eng.wait_ge(v_dec, n - 3)
                    for r in range(r0, min(r0 + 4, RK)):
                        m = eng.matmul(banks[n % 4][:, (r - r0) * B:(r - r0 + 1) * B], w[:, r, c * P:(c + 1) * P],
                                       mu, start=True, stop=True)
                    m.then_inc(m_dec, 1)
                    n += 1
            eng.wait_ge(v_dec, n - 3)
            eng.matmul(banks[n % 4][0:RK, 0:B], w[:, :, D], mu, start=True, stop=True).then_inc(m_dec, 1)

        @block.gpsimd
        def _(eng):
            eng.memset(tab[0][:, :], 0.0).then_inc(z_pool, 1)
            eng.memset(cls_t[:, :, :, :], 0.0).then_inc(z_pool, 1)
            eng.wait_ge(z_pool, 2)
            eng.sem_inc(z_tab, 1)
            eng.memset(k["mhalf"][:, :], -0.5).then_inc(z_pool, 1)
            eng.memset(k["ones3"][:, :], 1.0).then_inc(z_pool, 1)
            eng.memset(down_w[:, :, HID:P], 1.0).then_inc(z_pool, 1)
            eng.memset(k["act_bd"][:, :, :], 0.0).then_inc(z_pool, 1)
            eng.wait_ge(v_mve, 1)
            eng.wait_ge(z_pool, 6)
            eng.tensor_scalar(mo_ve[:, :], mo_mv[:, :, 1], EPS, 1.0, ALU.add, ALU.mult).then_inc(g_ve, 1)
            eng.wait_ge(g_ve, 1)
            eng.tensor_tensor(mo_r[:, :], mo_ve[:, :], k["mhalf"][:, 0:3], ALU.pow).then_inc(g_r, 1)

        @block.vector
        def _(eng):
            done = [0]

            def link(ins):
                done[0] += 1
                ins.then_inc(v_chain, 1)
                eng.wait_ge(v_chain, done[0])

            def split(src, r1, r2, p1, p2, p3):
                link(eng.tensor_copy(p1, src))
                link(eng.tensor_tensor(r1, src, p1, ALU.subtract))
                link(eng.tensor_copy(p2, r1))
                link(eng.tensor_tensor(r2, r1, p2, ALU.subtract))
                link(eng.tensor_copy(p3, r2))

            def pick(out, r1, p1, p2, p3, masks):
                link(eng.tensor_scalar(r1, p1, masks[:, 0:1], None, ALU.mult))
                link(eng.scalar_tensor_tensor(r1, p2, masks[:, 1:2], r1, ALU.mult, ALU.add))
                return eng.scalar_tensor_tensor(out, p3, masks[:, 2:3], r1, ALU.mult, ALU.add)

            eng.wait_ge(d_l1, 32)
            eng.tensor_tensor(wsq[:, :, :], l1_w[:, :, :], l1_w[:, :, :], ALU.mult)
            eng.wait_ge(c_style, 1)
            eng.tensor_tensor(style2[:, :, :], k["style"][:, :, :], k["style"][:, :, :], ALU.mult).then_inc(v_st2, 1)
            eng.wait_ge(d_w1, 32)
            link(eng.reduce_max(aw_c[0][:, :], aw[:, :], AX.X))
            eng.tensor_scalar(aw_s[0][:, :], aw[:, :], aw_c[0][:, 0:1], None, ALU.subtract).then_inc(v_aw, 1)
            eng.wait_ge(m_dc, 1)
            link(eng.tensor_scalar(dm[0][:, :, :], ps_b[:, 0, 0:KB * P].rearrange("p (k b) -> p k b", k=KB),
                                   DEMOD_EPS, None, ALU.add))
            eng.sem_inc(v_dca, 1)
            eng.wait_ge(c_dc, 1)
            link(eng.reciprocal(dm[2][:, :, :], dm[1][:, :, :]))
            link(eng.tensor_tensor(dm[3][:, :, :], dm[0][:, :, :], dm[2][:, :, :], ALU.mult))
            link(eng.tensor_tensor(dm[4][:, :, :], dm[3][:, :, :], dm[2][:, :, :], ALU.mult))
            link(eng.tensor_scalar(dm[3][:, :, :], dm[4][:, :, :], -0.5, 1.5, ALU.mult, ALU.add))
            eng.tensor_tensor(k["dcoef"][:, :, :], dm[2][:, :, :], dm[3][:, :, :], ALU.mult)
            eng.wait_ge(c_exp, 1)
            link(eng.reduce_sum(aw_c[1][:, :], aw_s[1][:, :], AX.X))
            link(eng.reciprocal(aw_c[2][:, :], aw_c[1][:, :]))
            link(eng.tensor_scalar(aw_s[0][:, :], aw_s[1][:, :], aw_c[2][:, 0:1], None, ALU.mult))
            for n in range(6):
                part = w1[:, 2 * n:2 * n + 2, :]
                last = eng.tensor_scalar(part, part, aw_s[0][:, n:n + 1], None, ALU.mult)
            link(last)
            eng.sem_inc(v_w1, 1)
            link(eng.tensor_tensor(w1x[:, :, :], w1[:, 4:6, :], w1[:, 6:8, :], ALU.add))
            link(eng.tensor_tensor(w1x[:, :, :], w1x[:, :, :], w1[:, 8:10, :], ALU.add))
            eng.wait_ge(m_mo, 1)
            eng.wait_ge(d_net, 16 * 20)
            link(eng.tensor_tensor(mo[1][:, :, :], rows_d[:, 0:3, :], rown[:, :, 0, :], ALU.add))
            for n in range(3):
                last = eng.bn_stats(mo_bn[:, n, :], mo[1][:, n, :])
            link(last)
            for n in range(3):
                last = eng.bn_aggr(mo_mv[:, n, :], mo_bn[:, n, :])
            last.then_inc(v_mve, 1)
            eng.wait_ge(g_r, 1)
            for n in range(3):
                last = eng.tensor_scalar(mo[2][:, n, :], mo[1][:, n, :], mo_mv[:, n, 0:1], mo_r[:, n:n + 1],
                                         ALU.subtract, ALU.mult)
            link(last)
            link(eng.tensor_tensor(mo[1][:, :, :], mo[2][:, :, :], rown[:, :, 1, :], ALU.mult))
            eng.tensor_tensor(mo[0][:, :, :], mo[1][:, :, :], rown[:, :, 2, :], ALU.add).then_inc(v_mo, 1)
            def halves(hi, lo, src):
                link(eng.tensor_copy(hi, src))
                eng.tensor_tensor(lo, src, hi.bitcast(F32), ALU.subtract)
            eng.wait_ge(d_wts, 32)
            eng.wait_ge(z_pool, 5)
            halves(k["l1_w_h"][:, :, :], k["l1_w_l"][:, :, :], l1_w[:, :, :])
            halves(k["down_w_h"][:, :, :], k["down_w_l"][:, :, :], down_w[:, :, :])
            halves(k["w2_h"][:, :, :], k["w2_l"][:, :, :], w2[:, :, :])
            for first, src in ((0, w1[:, 0:4, :]), (4, w1x[:, :, :]), (6, w1[:, 10:12, :])):
                n = src.shape[1]
                halves(k["w1_h"][:, first:first + n, :], k["w1_l"][:, first:first + n, :], src)
            eng.wait_ge(m_cls, 1)
            eng.wait_ge(d_tab, 16 * 18)
            eng.wait_ge(d_const, 16 * 8)
            eng.tensor_copy(k["two_i"][:, :], two_i[:, :])
            link(eng.tensor_copy(tab[0][:, 3 * D:4 * D], ps_b[0:CLS, 1, 0:D]))
            pieces = [p[:, :] for p in tab_p]
            split(tab[0][:, :], tab[1][:, :], tab[2][:, :], *pieces)
            link(pick(k["gain_tab"][:, :], tab[1][:, 0:3 * D], *(p[:, 0:3 * D] for p in pieces), k["piece_mask"]))
            for n in range(2):
                last = pick(k["shift"][n][0:CLS, :], tab[1][:, 3 * D:4 * D], *(p[:, 3 * D:4 * D] for p in pieces),
                            k["piece_mask"])
                link(last)
            pieces = [p[:, :] for p in b2p]
            split(b2f[0][:, :], b2f[1][:, :], b2f[2][:, :], *pieces)
            link(pick(k["b2_row"][:, :], b2f[1][:, :], *pieces, eye3))
            eng.wait_ge(m_row, 1)
            link(eng.tensor_copy(rowb[0][:, :], ps_b[:, 0, D:2 * D]))
            split(rowb[0][:, :], rowb[1][:, :], rowb[2][:, :], *(rowb_p[:, e, :] for e in range(PIECES)))
            eng.sem_inc(v_rowb, 1)
            banks = (ps_a[:, 0, :], ps_a[:, 1, :], ps_d[:, 0, :], ps_d[:, 1, :])
            eng.wait_ge(d_dec0, 48)
            n = 0
            for c in range(KB):
                for r0 in range(0, RK, 4):
                    w = min(4, RK - r0)
                    eng.wait_ge(m_dec, n + 1)
                    bias = bdec[:, c, r0:r0 + w].unsqueeze(2).broadcast_to([P, w, B])
                    eng.tensor_tensor(u_all[:, c, :, r0:r0 + w].rearrange("p b r -> p r b"),
                                      banks[n % 4][:, 0:w * B].rearrange("p (r b) -> p r b", b=B), bias,
                                      ALU.add).then_inc(v_dec, 1)
                    n += 1
            eng.wait_ge(m_dec, n + 1)
            link(eng.tensor_scalar(k["ub_t"][:, :], banks[n % 4][0:RK, 0:B], bdec_u[:, 0:1], None, ALU.add))


def conditioned_residuals(nc, t):
    ctx = ExitStack()
    with ctx:
        def sb(name, shape, dt=F32):
            return ctx.enter_context(nc.sbuf_tensor(name, shape, dt))

        def sem(name):
            return ctx.enter_context(nc.semaphore(name))

        ps_a, ps_b, ps_c, ps_d = (
            ctx.enter_context(nc.psum_tensor(f"ps_{n}", [P, KB, CH], F32)) for n in "abcd")

        def rows_of(ps):
            return ps[:, :, :].rearrange("p k (u d) -> p (k u) d", d=D)

        ident = sb("ident", [P, P])
        two_i = sb("two_i", [P, P], F32R)
        mhalf = sb("mhalf", [P, CT])
        cls_neg = sb("cls_neg", [CLS, 1])
        piece_mask = sb("piece_mask", [CLS, PIECES])
        mu_t = sb("mu_t", [MU, B])
        ub_t = sb("ub_t", [RK, B])
        v_sb = sb("v_sb", [RK, D])
        style = sb("style", [P, KB, B])
        dcoef = sb("dcoef", [P, KB, B])
        l1_w_h, l1_w_l = (sb(f"l1_w_{e}", [P, KB, D], F32R) for e in "hl")
        l1_b = sb("l1_b", [P, KB])
        down_w_h, down_w_l = (sb(f"down_w_{e}", [P, KB, P], F32R) for e in "hl")
        dgdb = sb("dgdb", [P, B])
        up_rep = sb("up_rep", [P, D])
        w1_h, w1_l = (sb(f"w1_{e}", [P, 8, D], F32R) for e in "hl")
        b1 = sb("b1", [P, KB])
        w2_h, w2_l = (sb(f"w2_{e}", [P, KB, D], F32R) for e in "hl")
        b2_row = sb("b2_row", [PIECES, D], BF16)
        ones3 = sb("ones3", [PIECES, P], BF16)
        ln_g = sb("ln_g", [P, D])
        ln_be = sb("ln_be", [P, D])
        gain_tab = sb("gain_tab", [CLS, 3 * D], BF16)
        pw_idx = sb("pw_idx", [P, ROWS // P], I32)

        ugub_d = nc.dram_tensor("ugub_scratch", (B, 2 * D), F32, kind="Internal").ap()
        u_d = nc.dram_tensor("u_scratch", (NCH, P, KB, CB, RK), F32, kind="Internal").ap()
        row_d = nc.dram_tensor("row_scratch", (B, PIECES, D), BF16, kind="Internal").ap()

        onehot = [sb(f"onehot{r}", [CLS + BRW, CH], BF16) for r in range(2)]
        shift = [sb(f"shift{r}", [CLS + BRW, D], BF16) for r in range(2)]
        act_bd = sb("act_bd", [P, CT, P])

        setup(nc, locals())

        x_t = [sb(f"x_t{r}", [P, KB, CH]) for r in range(2)]
        u_ch = [sb(f"u_ch{r}", [P, KB, CB, RK]) for r in range(2)]
        ugub = sb("ugub", [P, CT, 2 * D])
        idx_ch = [sb(f"idx_ch{r}", [CLS, CH], I32) for r in range(2)]
        pw_rows = [sb(f"pw_rows{r}", [P, CT, 2 * D]) for r in range(2)]
        gidx = [sb(f"gidx{r}", [P, CT], I32) for r in range(2)]
        oh_sq = sb("oh_sq", [CLS, CH], BF16)
        t_t = sb("t_t", [RK, CH])
        x1_t = sb("x1_t", [P, KB, CH])
        xm_t = sb("xm_t", [P, KB, CH])
        xm_t_h, xm_t_l = (sb(f"xm_t_{e}", [P, KB, CH], F32R) for e in "hl")
        l1_u = xm_t
        x2_t = x1_t
        x2_t_h, x2_t_l = (sb(f"x2_t_{e}", [P, KB, CH], F32R) for e in "hl")
        dn_u = sb("dn_u", [HID, CH])
        dn_v = sb("dn_v", [HID, CH])
        dn = sb("dn", [HID, CH])
        w_up = sb("w_up", [P, CT, D])
        x3 = sb("x3", [P, CT, D])
        x3be = [sb(f"x3be{r}", [P, CT, D]) for r in range(2)]
        xhat = sb("xhat", [P, CT, D])
        h1 = sb("h1", [P, CT, D])
        x3_t_h, x3_t_l = (sb(f"x3_t_{e}", [P, KB, CH], F32R) for e in "hl")
        xh_t = sb("xh_t", [P, KB, CH])
        hh_t = sb("hh_t", [P, KB, CH])
        tm_t = sb("tm_t", [P, KB, CH])
        tm_t_h, tm_t_l = (sb(f"tm_t_{e}", [P, KB, CH], F32R) for e in "hl")
        ms_t = sb("ms_t", [P, KB, CH])
        ms_t_h, ms_t_l = (sb(f"ms_t_{e}", [P, KB, CH], F32R) for e in "hl")
        h_t = tm_t
        h_t_h, h_t_l = (sb(f"h_t_{e}", [P, KB, CH], F32R) for e in "hl")
        act_t = hh_t
        act_t_h, act_t_l = (sb(f"act_t_{e}", [P, KB, CH], F32R) for e in "hl")
        y_out = [sb(f"y_out{r}", [P, CT, D]) for r in range(2)]
        bn = {k: sb(f"bn_{k}", [P, CT, 6]) for k in "xhy"}
        mv = {k: sb(f"mv_{k}", [P, CT, 2]) for k in "xhy"}
        ve = {k: sb(f"ve_{k}", [P, CT]) for k in "xhy"}
        rstd = {k: sb(f"rstd_{k}", [P, CT]) for k in "xhy"}
        nb = {k: sb(f"nb_{k}", [P, CT]) for k in "xh"}


        s_x = [sem(f"s_x{r}") for r in range(2)]
        s_u = [sem(f"s_u{r}") for r in range(2)]
        s_ug = sem("s_ug")
        s_idx = [sem(f"s_idx{r}") for r in range(2)]
        s_row = [sem(f"s_row{r}") for r in range(2)]
        s_pw = [sem(f"s_pw{r}") for r in range(2)]
        s_idle = sem("s_idle")
        s_store = [sem(f"s_store{r}") for r in range(2)]
        (p_t, p_x1, p_l1, p_dn, p_up, p_x3t, p_xht, p_tm, p_ms, p_hht, p_cp, p_w1x, p_w1t, p_w1m, p_w1, p_w2) = (
            sem("p_" + n) for n in "t x1 l1 dn up x3t xht tm ms hht cp w1x w1t w1m w1 w2".split())
        (a_relu, a_x3, a_x3h, a_xht, a_hht, a_silu, a_silh, a_xmh, a_x2h, a_tmh, a_msh, a_hh, a_sq, a_oh, a_xhat, a_hhat) = (
            sem("a_" + n) for n in "relu x3 x3h xht hht silu silh xmh x2h tmh msh hh sq oh xhat hhat".split())
        (v_t, v_x1, v_l1u, v_l1v, v_x2, v_dnu, v_dn, v_bnx, v_mvx, v_xnb, v_bnh, v_mvh, v_hnb,
         v_tm, v_ms, v_h, v_bny, v_mvy, v_y1, v_y, v_xml, v_x2l, v_x3l, v_hl, v_sill) = (
            sem("v_" + n) for n in
            "t x1 l1u l1v x2 dnu dn bnx mvx xnb bnh mvh hnb tm ms h bny mvy y1 y "
            "xml x2l x3l hl sill".split())
        (g_gidx, g_xm, g_vex, g_rx, g_h1m, g_h1, g_veh, g_rh, g_upm, g_up, g_x3be, g_vey,
         g_ry, g_tml, g_msl) = (sem("g_" + n) for n in
                  "gidx xm vex rx h1m h1 veh rh upm up x3be vey ry tml msl".split())

        x_d = t["x_t"].rearrange("(k p) (c n) -> c p k n", p=P, n=CH)
        out_d = t["out"].rearrange("(c k p) d -> c p k d", k=CT, p=P)
        ug_d = ugub_d.rearrange("(c k h) d -> c h k d", k=CT, h=2)
        tok_d = t["itok4"].rearrange("(c o n) -> c o n", o=1, n=CH)
        mask_d = t["mask"].rearrange("(c o n) -> c o n", o=1, n=CH)
        rowc_d = row_d.rearrange("(c b) e d -> c (b e) d", b=CB)

        def one(ap, c):
            return ap[c.n]

        def cols(table, c):
            k = table.shape[1]
            return table[:, :, bass.ds(c.n * CB, CB)].unsqueeze(3).broadcast_to([P, k, CB, S])

        def by_entry(ap):
            return ap.rearrange("p k (b s) -> p k b s", s=S)

        def load(eng, c):
            r = c.ring
            wait(eng, v_x1, c.n - 1)
            eng.dma_start(x_t[r][:, :, :], one(x_d, c)).then_inc(s_x[r], 16)
            wait(eng, p_t, c.n - 1)
            eng.dma_start(u_ch[r][:, :, :, :],
                          one(u_d, c)).then_inc(s_u[r], 16)
            wait(eng, a_sq, c.n - 1)
            ncp = PIECES * NCP
            eng.dma_start(idx_ch[r][0:ncp, :], one(tok_d, c).broadcast_to([ncp, CH])).then_inc(s_idx[r], 16)
            eng.dma_start(idx_ch[r][ncp:CLS, :],
                          one(mask_d, c).broadcast_to([CLS - ncp, CH])).then_inc(s_idx[r], 16)

        def load_shift(eng, c):
            wait(eng, p_w1, c.n - 1)
            eng.dma_start(shift[c.ring][CLS:CLS + BRW, :], one(rowc_d, c)).then_inc(s_row[c.ring], 16)

        def load_up(eng, c):
            wait(eng, g_up, c.n)
            for h in range(2):
                src = one(ug_d, c)[h:h + 1].broadcast_to([HID, CT, 2 * D])
                eng.dma_start(ugub[h * HID:(h + 1) * HID, :, :], src).then_inc(s_ug, 16)

        def store(eng, c):
            wait(eng, v_y, c.n + 1)
            eng.dma_start(one(out_d, c), y_out[c.ring][:, :, :]).then_inc(s_store[c.ring], 16)

        def product(eng, out, w, act, first, last):
            (wh, wl), (ah, al) = w, act
            eng.matmul(out, wl, ah, start=first, stop=False)
            eng.matmul(out, wh, al, start=False, stop=False)
            return eng.matmul(out, wh, ah, start=False, stop=last)

        def pe_t(eng, c):
            wait(eng, s_x[c.ring], 16 * (c.half + 1))
            wait(eng, v_l1u, c.n)
            wait(eng, s_u[c.ring], 16 * (c.half + 1))
            for b in range(CB):
                for k in range(KB):
                    m = eng.matmul(ps_a[0:RK, 0, b * S:(b + 1) * S], u_ch[c.ring][:, k, b, :],
                                   x_t[c.ring][:, k, b * S:(b + 1) * S], start=k == 0, stop=k == KB - 1)
            m.then_inc(p_t, 1)

        def pe_x1(eng, c):
            wait(eng, v_t, c.n + 1)
            for k in range(KB):
                m = eng.matmul(ps_a[:, k, :], v_sb[:, k * P:(k + 1) * P], t_t[:, :], start=True, stop=True)
            m.then_inc(p_x1, 1)

        def pe_l1(eng, c):
            wait(eng, v_x1, c.n + 1)
            wait(eng, v_xml, c.n + 1)
            for o in range(KB):
                cut = slice(o * P, (o + 1) * P)
                for k in range(KB):
                    m = product(eng, ps_a[:, o, :], (l1_w_h[:, k, cut], l1_w_l[:, k, cut]),
                                (xm_t_h[:, k, :], xm_t_l[:, k, :]), k == 0, k == KB - 1)
            m.then_inc(p_l1, 1)

        def pe_dn(eng, c):
            wait(eng, v_x2l, c.n + 1)
            wait(eng, v_ms, c.n)
            for k in range(KB):
                m = product(eng, ps_b[:, 0, :], (down_w_h[:, k, :], down_w_l[:, k, :]),
                            (x2_t_h[:, k, :], x2_t_l[:, k, :]), k == 0, k == KB - 1)
            m.then_inc(p_dn, 1)

        def pe_up(eng, c):
            wait(eng, a_relu, c.n + 1)
            wait(eng, v_dn, c.n + 1)
            wait(eng, g_up, c.n + 1)
            out = rows_of(ps_b)
            for j in range(CT):
                eng.matmul(out[:, j, :], act_bd[:, j, :], w_up[:, j, :], start=True, stop=False)
                for k in range(KB):
                    for half in (x2_t_l, x2_t_h):
                        m = eng.matmul(out[:, j, k * P:(k + 1) * P], half[:, k, j * P:(j + 1) * P],
                                       two_i[:, :], start=False, stop=k == KB - 1 and half is x2_t_h)
            m.then_inc(p_up, 1)

        def transposes(eng, out, src):
            for k in range(KB):
                for j in range(CT):
                    m = eng.transpose(out[:, k, j * P:(j + 1) * P], src[:, j, k * P:(k + 1) * P], ident[:, :])
            return m

        def pe_x3t(eng, c):
            wait(eng, a_x3, c.n + 1)
            transposes(eng, ps_b, x3).then_inc(p_x3t, 1)

        def pe_xht(eng, c):
            wait(eng, a_xhat, c.n + 1)
            wait(eng, v_h, c.n)
            transposes(eng, ps_c, xhat).then_inc(p_xht, 1)

        def gains(eng, out, c, first):
            for k in range(KB):
                m = eng.matmul(out[:, k, :], gain_tab[:, first + k * P:first + (k + 1) * P],
                               onehot[c.ring][0:CLS, :], start=True, stop=True)
            return m

        def pe_tm(eng, c):
            wait(eng, a_oh, c.n + 1)
            wait(eng, a_xht, c.n + 1)
            gains(eng, ps_c, c, D).then_inc(p_tm, 1)

        def pe_ms(eng, c):
            wait(eng, a_oh, c.n + 1)
            wait(eng, v_x3l, c.n + 1)
            gains(eng, ps_b, c, 2 * D).then_inc(p_ms, 1)

        def pe_hhat(eng, c):
            wait(eng, a_hhat, c.n + 1)
            wait(eng, v_tm, c.n + 1)
            transposes(eng, ps_c, h1).then_inc(p_hht, 1)

        def pe_cp(eng, c):
            wait(eng, a_hht, c.n + 1)
            gains(eng, ps_c, c, 0).then_inc(p_cp, 1)

        def w1_part(eng, c, first, ah, al, last):
            for o in range(KB):
                cut = slice(o * P, (o + 1) * P)
                for k in range(KB):
                    m = product(eng, ps_d[:, o, :], (w1_h[:, first + k, cut], w1_l[:, first + k, cut]),
                                (ah[:, k, :], al[:, k, :]), False, last and k == KB - 1)
            return m

        def pe_w1_x3(eng, c):
            wait(eng, v_y1, c.n)
            wait(eng, a_oh, c.n + 1)
            wait(eng, s_row[c.ring], 16 * (c.half + 1))
            for o in range(KB):
                eng.matmul(ps_d[:, o, :], shift[c.ring][:, o * P:(o + 1) * P], onehot[c.ring][:, :],
                           start=True, stop=False)
            wait(eng, v_x3l, c.n + 1)
            w1_part(eng, c, 4, x3_t_h, x3_t_l, False).then_inc(p_w1x, 1)

        def pe_w1_tm(eng, c):
            wait(eng, g_tml, c.n + 1)
            w1_part(eng, c, 2, tm_t_h, tm_t_l, False).then_inc(p_w1t, 1)

        def pe_w1_ms(eng, c):
            wait(eng, g_msl, c.n + 1)
            w1_part(eng, c, 6, ms_t_h, ms_t_l, False).then_inc(p_w1m, 1)

        def pe_w1_h(eng, c):
            wait(eng, v_hl, c.n + 1)
            w1_part(eng, c, 0, h_t_h, h_t_l, True).then_inc(p_w1, 1)

        def pe_w2(eng, c):
            wait(eng, v_sill, c.n + 1)
            out = rows_of(ps_d)
            for j in range(CT):
                cut = slice(j * P, (j + 1) * P)
                eng.matmul(out[:, j, :], ones3[:, :], b2_row[:, :], start=True, stop=False)
                for k in range(KB):
                    m = product(eng, out[:, j, :], (act_t_h[:, k, cut], act_t_l[:, k, cut]),
                                (w2_h[:, k, :], w2_l[:, k, :]), False, k == KB - 1)
            m.then_inc(p_w2, 1)

        def act_relu(eng, c):
            wait(eng, v_dn, c.n + 1)
            wait(eng, p_up, c.n)
            d = dn[:, :].rearrange("h (k e s) -> h k e s", e=2, s=S)
            eng.activation(act_bd[0:HID, :, 0:S], d[:, :, 0, :], ACT.Relu)
            eng.activation(act_bd[HID:P, :, S:P], d[:, :, 1, :], ACT.Relu).then_inc(a_relu, 1)

        def act_x3(eng, c):
            wait(eng, p_up, c.n + 1)
            wait(eng, p_x3t, c.n)
            wait(eng, a_xhat, c.n)
            wait(eng, g_x3be, c.n)
            eng.activation(x3[:, :, :], rows_of(ps_b), ACT.Copy).then_inc(a_x3, 1)

        def act_x3t(eng, c):
            wait(eng, p_x3t, c.n + 1)
            wait(eng, p_w1x, c.n)
            eng.activation(x3_t_h[:, :, :], ps_b[:, :, :], ACT.Copy).then_inc(a_x3h, 1)

        def act_xht(eng, c):
            wait(eng, p_xht, c.n + 1)
            wait(eng, v_ms, c.n)
            eng.activation(xh_t[:, :, :], ps_c[:, :, :], ACT.Copy).then_inc(a_xht, 1)

        def act_hht(eng, c):
            wait(eng, p_hht, c.n + 1)
            wait(eng, v_sill, c.n)
            eng.activation(hh_t[:, :, :], ps_c[:, :, :], ACT.Copy).then_inc(a_hht, 1)

        def normalise(eng, k, out, src):
            for j in range(CT):
                m = eng.activation(out[:, j, :], src[:, j, :], ACT.Identity, bias=nb[k][:, j:j + 1],
                                   scale=rstd[k][:, j:j + 1])
            return m

        def act_xnorm(eng, c):
            wait(eng, v_xnb, c.n + 1)
            wait(eng, p_xht, c.n)
            wait(eng, g_h1m, c.n)
            normalise(eng, "x", xhat, x3).then_inc(a_xhat, 1)

        def act_hnorm(eng, c):
            wait(eng, v_hnb, c.n + 1)
            normalise(eng, "h", h1, h1).then_inc(a_hhat, 1)

        def high(out, src, s_src, s_free, s_done):
            def stage(eng, c):
                wait(eng, s_src, c.n + 1)
                wait(eng, s_free, c.n)
                eng.activation(out[:, :, :], src[:, :, :], ACT.Copy).then_inc(s_done, 1)
            return stage

        act_xmh = high(xm_t_h, xm_t, g_xm, p_l1, a_xmh)
        act_x2h = high(x2_t_h, x2_t, v_x2, p_up, a_x2h)
        act_tmh = high(tm_t_h, tm_t, v_tm, p_w1t, a_tmh)
        act_msh = high(ms_t_h, ms_t, v_ms, p_w1m, a_msh)
        act_hh = high(h_t_h, h_t, v_h, p_w1, a_hh)

        def act_silu(eng, c):
            wait(eng, p_w1, c.n + 1)
            wait(eng, v_sill, c.n)
            for k in range(KB):
                m = eng.activation(act_t[:, k, :], ps_d[:, k, :], ACT.Silu, bias=b1[:, k:k + 1])
            m.then_inc(a_silu, 1)

        def act_silh(eng, c):
            wait(eng, p_w2, c.n)
            wait(eng, a_silu, c.n + 1)
            eng.activation(act_t_h[:, :, :], act_t[:, :, :], ACT.Copy).then_inc(a_silh, 1)

        def act_onehot(eng, c):
            wait(eng, s_idx[c.ring], 32 * (c.half + 1))
            eng.activation(oh_sq[:, :], idx_ch[c.ring][:, :], ACT.Square, bias=cls_neg[:, 0:1]).then_inc(a_sq, 1)
            wait(eng, a_sq, c.n + 1)
            wait(eng, p_w1, c.n - 1)
            eng.activation(onehot[c.ring][0:CLS, :], oh_sq[:, :], ACT.Relu, bias=1.0, scale=-1.0).then_inc(a_oh, 1)

        def v_down(eng, c):
            wait(eng, p_dn, c.n + 1)
            wait(eng, a_relu, c.n)
            def half(ap):
                return ap.rearrange("p (b s) -> p b s", s=S)
            def dtab(lo):
                return dgdb[lo:lo + HID, bass.ds(c.n * CB, CB)].unsqueeze(2).broadcast_to([HID, CB, S])
            eng.tensor_tensor(half(dn_u[:, :]), half(ps_b[0:HID, 0, :]), dtab(0), ALU.mult)
            eng.tensor_tensor(half(dn_v[:, :]), half(ps_b[HID:P, 0, :]), dtab(HID), ALU.mult).then_inc(v_dnu, 1)
            eng.wait_ge(v_dnu, c.n + 1)
            eng.tensor_tensor(dn[:, :], dn_u[:, :], dn_v[:, :], ALU.add).then_inc(v_dn, 1)

        def v_tadd(eng, c):
            wait(eng, p_t, c.n + 1)
            wait(eng, p_x1, c.n)
            ub = ub_t[:, bass.ds(c.n * CB, CB)].unsqueeze(2).broadcast_to([RK, CB, S])
            eng.tensor_tensor(t_t[:, :].rearrange("p (b s) -> p b s", s=S),
                              ps_a[0:RK, 0, :].rearrange("p (b s) -> p b s", s=S), ub, ALU.add).then_inc(v_t, 1)

        def v_hprod(eng, c):
            wait(eng, a_hht, c.n + 1)
            wait(eng, p_cp, c.n + 1)
            wait(eng, g_tml, c.n + 1)
            eng.tensor_tensor(h_t[:, :, :], ps_c[:, :, :], hh_t[:, :, :], ALU.mult).then_inc(v_h, 1)

        def v_x1add(eng, c):
            wait(eng, p_x1, c.n + 1)
            wait(eng, v_x2l, c.n)
            eng.tensor_tensor(x1_t[:, :, :], ps_a[:, :, :], x_t[c.ring][:, :, :], ALU.add).then_inc(v_x1, 1)

        def stats(eng, c, k, src, s_bn, s_mv):
            for j in range(CT):
                m = eng.bn_stats(bn[k][:, j, :], src[:, j, :])
            m.then_inc(s_bn, 1)
            eng.wait_ge(s_bn, c.n + 1)
            settle(eng, s_idle)
            for j in range(CT):
                m = eng.bn_aggr(mv[k][:, j, :], bn[k][:, j, :])
            m.then_inc(s_mv, 1)

        def offsets(eng, c, k, s_r, s_nb):
            wait(eng, s_r, c.n + 1)
            eng.scalar_tensor_tensor(nb[k][:, :], mv[k][:, :, 0], -1.0, rstd[k][:, :], ALU.mult, ALU.mult)\
               .then_inc(s_nb, 1)

        def v_xstat(eng, c):
            wait(eng, a_x3, c.n + 1)
            wait(eng, g_vex, c.n)
            stats(eng, c, "x", x3, v_bnx, v_mvx)

        def v_xoff(eng, c):
            wait(eng, a_xhat, c.n)
            offsets(eng, c, "x", g_rx, v_xnb)

        def v_hstat(eng, c):
            wait(eng, g_h1, c.n + 1)
            stats(eng, c, "h", h1, v_bnh, v_mvh)

        def v_hoff(eng, c):
            wait(eng, a_hhat, c.n)
            offsets(eng, c, "h", g_rh, v_hnb)

        def v_l1(eng, c):
            wait(eng, p_l1, c.n + 1)
            eng.tensor_tensor(by_entry(l1_u[:, :, :]), by_entry(ps_a[:, :, :]), cols(dcoef, c),
                              ALU.mult).then_inc(v_l1u, 1)
            eng.wait_ge(v_l1u, c.n + 1)
            for k in range(KB):
                m = eng.tensor_scalar(l1_u[:, k, :], l1_u[:, k, :], l1_b[:, k:k + 1], CLAMP, ALU.add, ALU.min)
            m.then_inc(v_l1v, 1)
            eng.wait_ge(v_l1v, c.n + 1)
            wait(eng, g_xm, c.n + 1)
            eng.scalar_tensor_tensor(x2_t[:, :, :], l1_u[:, :, :], -CLAMP, x1_t[:, :, :],
                                     ALU.max, ALU.add).then_inc(v_x2, 1)

        def v_tmprod(eng, c):
            wait(eng, a_xht, c.n + 1)
            wait(eng, v_hl, c.n)
            wait(eng, p_tm, c.n + 1)
            eng.tensor_tensor(tm_t[:, :, :], ps_c[:, :, :], xh_t[:, :, :], ALU.mult).then_inc(v_tm, 1)

        def v_msprod(eng, c):
            wait(eng, a_xht, c.n + 1)
            wait(eng, g_msl, c.n)
            wait(eng, p_ms, c.n + 1)
            eng.tensor_tensor(ms_t[:, :, :], ps_b[:, :, :], xh_t[:, :, :], ALU.mult).then_inc(v_ms, 1)

        def low(out, src, high_half, s_high, s_free, s_done):
            def stage(eng, c):
                wait(eng, s_high, c.n + 1)
                wait(eng, s_free, c.n)
                eng.tensor_tensor(out[:, :, :], src[:, :, :], high_half[:, :, :].bitcast(F32),
                                  ALU.subtract).then_inc(s_done, 1)
            return stage

        v_xml_ = low(xm_t_l, xm_t, xm_t_h, a_xmh, p_l1, v_xml)
        v_x2l_ = low(x2_t_l, x2_t, x2_t_h, a_x2h, p_up, v_x2l)
        v_x3l_ = low(x3_t_l, ps_b, x3_t_h, a_x3h, p_w1x, v_x3l)
        g_tml_ = low(tm_t_l, tm_t, tm_t_h, a_tmh, p_w1t, g_tml)
        g_msl_ = low(ms_t_l, ms_t, ms_t_h, a_msh, p_w1m, g_msl)
        v_hl_ = low(h_t_l, h_t, h_t_h, a_hh, p_w1, v_hl)
        v_sill_ = low(act_t_l, act_t, act_t_h, a_silh, p_w2, v_sill)

        def v_ystat(eng, c):
            wait(eng, p_w2, c.n + 1)
            stats(eng, c, "y", rows_of(ps_d), v_bny, v_mvy)

        def v_ycentre(eng, c):
            eng.wait_ge(v_mvy, c.n + 1)
            wait(eng, s_store[c.ring], 16 * c.half)
            for j in range(CT):
                m = eng.scalar_tensor_tensor(y_out[c.ring][:, j, :], rows_of(ps_d)[:, j, :], mv["y"][:, j, 0:1],
                                             ln_g[:, :], ALU.subtract, ALU.mult)
            m.then_inc(v_y1, 1)

        def v_ynorm(eng, c):
            wait(eng, v_y1, c.n + 1)
            wait(eng, g_ry, c.n + 1)
            wait(eng, g_x3be, c.n + 1)
            for j in range(CT):
                m = eng.scalar_tensor_tensor(y_out[c.ring][:, j, :], y_out[c.ring][:, j, :], rstd["y"][:, j:j + 1],
                                             x3be[c.ring][:, j, :], ALU.mult, ALU.add)
            m.then_inc(v_y, 1)

        def g_gather(eng, c):
            wait(eng, g_h1, c.n - 1)
            wait(eng, s_pw[c.ring], 16 * CT * c.half)
            eng.tensor_copy(gidx[c.ring][:, :], pw_idx[:, bass.ds(c.n * CT, CT)]).then_inc(g_gidx, 1)
            eng.wait_ge(g_gidx, c.n + 1)
            settle(eng, s_idle)
            for j in range(CT):
                eng.indirect_dma_start(
                    pw_rows[c.ring][:, j, :], None, t["pw"],
                    bass.IndirectOffsetOnAxis(ap=gidx[c.ring][:, j:j + 1], axis=0)).then_inc(s_pw[c.ring], 16)

        def g_style(eng, c):
            wait(eng, v_x1, c.n + 1)
            wait(eng, v_x2, c.n)
            eng.tensor_tensor(by_entry(xm_t[:, :, :]), by_entry(x1_t[:, :, :]), cols(style, c),
                              ALU.mult).then_inc(g_xm, 1)

        def root(eng, c, k, s_mv, s_ve, s_r):
            wait(eng, s_mv, c.n + 1)
            settle(eng, s_idle)
            eng.tensor_scalar(ve[k][:, :], mv[k][:, :, 1], EPS, 1.0, ALU.add, ALU.mult).then_inc(s_ve, 1)
            eng.wait_ge(s_ve, c.n + 1)
            eng.tensor_tensor(rstd[k][:, :], ve[k][:, :], mhalf[:, :], ALU.pow).then_inc(s_r, 1)

        def g_rootx(eng, c):
            wait(eng, a_xhat, c.n)
            root(eng, c, "x", v_mvx, g_vex, g_rx)

        def g_h(eng, c):
            wait(eng, a_xhat, c.n + 1)
            wait(eng, s_pw[c.ring], 16 * CT * (c.half + 1))
            wait(eng, p_hht, c.n)
            eng.tensor_tensor(h1[:, :, :], xhat[:, :, :], pw_rows[c.ring][:, :, 0:D], ALU.mult).then_inc(g_h1m, 1)
            eng.wait_ge(g_h1m, c.n + 1)
            eng.tensor_tensor(h1[:, :, :], h1[:, :, :], pw_rows[c.ring][:, :, D:2 * D], ALU.add).then_inc(g_h1, 1)

        def g_rooth(eng, c):
            root(eng, c, "h", v_mvh, g_veh, g_rh)

        def g_wup(eng, c):
            wait(eng, s_ug, 32 * (c.n + 1))
            wait(eng, p_up, c.n)
            eng.tensor_tensor(w_up[:, :, :], up_rep[:, :].unsqueeze(1).broadcast_to([P, CT, D]), ugub[:, :, 0:D], ALU.mult).then_inc(g_upm, 1)
            eng.wait_ge(g_upm, c.n + 1)
            eng.tensor_tensor(w_up[:, :, :], w_up[:, :, :], ugub[:, :, D:2 * D], ALU.add).then_inc(g_up, 1)

        def g_res(eng, c):
            wait(eng, a_x3, c.n + 1)
            wait(eng, v_y, c.n - 1)
            eng.tensor_tensor(x3be[c.ring][:, :, :], x3[:, :, :], ln_be[:, :].unsqueeze(1).broadcast_to([P, CT, D]), ALU.add).then_inc(g_x3be, 1)

        def g_rooty(eng, c):
            wait(eng, v_y, c.n)
            root(eng, c, "y", v_mvy, g_vey, g_ry)

        block = ctx.enter_context(nc.Block())

        @block.sync
        def _(eng):
            run_slots(eng, [(load, 0), (load_up, 1), (store, 4), (load_shift, 2)])
            for r in range(2):
                eng.wait_ge(s_store[r], 16 * NCH // 2)

        @block.tensor
        def _(eng):
            run_slots(eng, [(pe_tm, 3), (pe_t, 1), (pe_dn, 2), (pe_hhat, 3), (pe_x1, 1), (pe_cp, 3),
                            (pe_up, 2), (pe_w1_x3, 3), (pe_x3t, 2), (pe_w1_tm, 3), (pe_w1_ms, 3), (pe_w1_h, 3),
                            (pe_l1, 1), (pe_xht, 2), (pe_ms, 2), (pe_w2, 3)])

        @block.scalar
        def _(eng):
            run_slots(eng, [(act_x2h, 2), (act_onehot, 2), (act_hnorm, 3), (act_tmh, 3), (act_hht, 3),
                            (act_relu, 2), (act_msh, 3), (act_x3, 2), (act_x3t, 2), (act_xnorm, 2),
                            (act_hh, 3), (act_xmh, 1), (act_silu, 3), (act_silh, 3), (act_xht, 2)])

        @block.vector
        def _(eng):
            run_slots(eng, [(v_ystat, 4), (v_ycentre, 4), (v_x1add, 1), (v_hprod, 3), (v_xstat, 2),
                            (v_xoff, 2), (v_hl_, 3), (v_x3l_, 2), (v_ynorm, 4), (v_xml_, 1), (v_hstat, 2),
                            (v_sill_, 3), (v_l1, 1), (v_msprod, 2), (v_hoff, 2), (v_x2l_, 1), (v_tmprod, 2),
                            (v_tadd, 0), (v_down, 1)])

        @block.gpsimd
        def _(eng):
            run_slots(eng, [(g_gather, 1), (g_rooth, 3), (g_wup, 2), (g_res, 3), (g_tml_, 3), (g_msl_, 3),
                            (g_style, 1), (g_rootx, 2), (g_rooty, 4), (g_h, 2)])


def kernel(**inputs):
    import numpy as np
    import ml_dtypes
    import concourse.bacc as bacc
    from concourse import mybir
    from concourse.bass_utils import run_bass_kernel_spmd

    a = {n: np.asarray(v) for n, v in inputs.items()}
    lay = np.ascontiguousarray

    def by_block(v):
        return lay(v.reshape(KB, P).T)

    ncls = PIECES * (NCP + NMS)
    cls_id = np.concatenate([np.tile(np.arange(NCP), PIECES), np.tile(np.arange(NMS), PIECES)])
    piece = np.concatenate([np.repeat(np.arange(PIECES), NCP), np.repeat(np.arange(PIECES), NMS)])
    entry = np.repeat(np.arange(CB), PIECES)
    arrays = {
        "ident": np.eye(P, dtype=np.float32),
        "two_i": 2 * np.eye(P, dtype=np.float32),
        "cls_neg": -cls_id.astype(np.float32).reshape(ncls, 1),
        "piece_mask": (piece[:, None] == np.arange(PIECES)[None, :]).astype(np.float32),
        "entry_rows": (entry[:, None] == np.repeat(np.arange(CB), S)[None, :]).astype(ml_dtypes.bfloat16),
    }
    arrays.update({
        "x_t": lay(a["x"].reshape(ROWS, D).T),
        "cond_t": lay(a["cond_512"].T),
        "noi_t": lay(a["cond_64"].T),
        "res_t": lay(a["fside_Bx32_0"].T),
        "itok_t": lay(a["itok_BxS_0_999"].reshape(ROWS // P, P).T),
        "itok4": a["itok_BxS_0_4"].reshape(ROWS),
        "mask": a["mask_BxS_ik0"].reshape(ROWS),
        "W_dec": a["L0_cond_W_dec"], "b_dec": a["L0_cond_b_dec"], "V": a["L0_cond_V"],
        "l1_wt": lay(a["L1_cond_weight"].T), "l1_b": by_block(a["L1_cond_bias"]),
        "aff_t": lay(a["L1_cond_affine_w"].T), "aff_b": by_block(a["L1_cond_affine_b"]),
        "down_p": a["L2_cond_down_project"], "down_gamma": a["L2_cond_down_gamma"],
        "down_beta": a["L2_cond_down_beta"], "up_p": a["L2_cond_up_project"],
        "up_gamma": a["L2_cond_up_gamma"], "up_beta": a["L2_cond_up_beta"],
        "pw": lay(np.concatenate([a["L3_cond_pw_g"], a["L3_cond_pw_b"]], axis=1)),
        "cp_g": a["L3_cond_cp_g"], "cp_bt": lay(a["L3_cond_cp_b"].T),
        "tm_g": a["L3_cond_tm_g"], "tm_bt": lay(a["L3_cond_tm_b"].T),
        "ms_g": a["L3_cond_ms_g"], "ms_bt": lay(a["L3_cond_ms_b"].T),
        "aw": a["L3_cond_aw"],
    })
    for net in ("mem", "noi", "res", "int"):
        for part in ("W1", "b1", "W2", "b2", "g", "be"):
            v = a[f"L3_cond_{net}_{part}"]
            arrays[f"{net}_{part}"] = by_block(v) if part == "b1" else v

    nc = bacc.Bacc("TRN2", target_bir_lowering=False, num_devices=1)
    t, placed = {}, {}
    for name, v in arrays.items():
        v = lay(v)
        placed["in_" + name] = v
        t[name] = nc.dram_tensor("in_" + name, v.shape, mybir.dt.from_np(v.dtype), kind="ExternalInput").ap()
    t["out"] = nc.dram_tensor("out", (ROWS, D), mybir.dt.float32, kind="ExternalOutput").ap()
    conditioned_residuals(nc, t)
    r = run_bass_kernel_spmd(nc, [placed], core_ids=[0])
    return r.results[0]["out"].reshape(B, S, D)
```

```python
from contextlib import ExitStack

import numpy as np
import concourse.bass as bass
from concourse import mybir

F32 = mybir.dt.float32
F32R = mybir.dt.float32r
BF16 = mybir.dt.bfloat16
I32 = mybir.dt.int32
ACT = mybir.ActivationFunctionType
ALU = mybir.AluOpType
AX = mybir.AxisListType

B, S, D = 128, 64, 256
P = 128
ROWS = B * S
KB = D // P
CH = 512
NCH = ROWS // CH
CB = CH // S
CT = CH // P
RK = 30
RP = 32
MU = 128
HID = 64
NPW, NCP, NMS = 250, 5, 3
PIECES = 3
CLS = PIECES * (NCP + NMS)
BRW = PIECES * CB
EPS = 1e-5
DEMOD_EPS = 1e-8
CLAMP = 256.0


class Chunk:

    def __init__(self, n, half, ring):
        self.n, self.half, self.ring = n, half, ring

    def valid(self):
        return not isinstance(self.n, int) or 0 <= self.n < NCH


def wait(eng, sem, value):
    if not isinstance(value, int) or value > 0:
        eng.wait_ge(sem, value)


def settle(eng, sem):
    eng.sem_inc(sem, 1)


def run_slots(eng, order):
    last = max(lag for _, lag in order)
    fill = last + 2 - last % 2
    def slot(base, half, k):
        for stage, lag in order:
            d = k - lag
            c = Chunk(base + d, half + (d - d % 2) // 2, d % 2)
            if c.valid():
                stage(eng, c)
    for n in range(fill):
        slot(0, 0, n)
    with eng.Fori(fill // 2, NCH // 2) as i:
        for k in range(2):
            slot(2 * i, i, k)
    for n in range(NCH, NCH + last):
        slot(0, 0, n)


def setup(nc, k):
    t = k["t"]
    with ExitStack() as ctx:
        def sb(name, shape, dt=F32):
            return ctx.enter_context(nc.sbuf_tensor("set_" + name, shape, dt))

        def sem(name):
            return ctx.enter_context(nc.semaphore("set_" + name))

        width = (D + 1) * RK
        cond = sb("cond", [MU, B + D + 2 * HID + 2 * D])
        mu = cond[:, 0:B]
        aff = cond[:, B:B + D]
        dgb = cond[:, B + D:B + D + P]
        ugb = cond[:, B + D + P:B + D + P + 2 * D]
        wdec = sb("wdec", [MU, width])
        bdec = sb("bdec", [P, KB, RK])
        bdec_u = sb("bdec_u", [RK, 1])
        u_all = sb("u_all", [P, KB, B, RK])
        v_rep = sb("v_rep", [3 * RP, D])
        zeros = sb("zeros", [3 * RP, CH])
        style2 = sb("style2", [P, KB, B])
        wsq = sb("wsq", [P, KB, D])
        l1_w = sb("l1_w", [P, KB, D])
        down_w = sb("down_w", [P, KB, P])
        w1 = sb("w1", [P, 12, D])
        w1x = sb("w1x", [P, KB, D])
        w2 = sb("w2", [P, KB, D])
        dm = [sb(f"dm{n}", [P, KB, B]) for n in range(5)]
        ugub_row = sb("ugub_row", [B, 2 * D])
        aw = sb("aw", [P, 6])
        aw_s = [sb(f"aw_s{n}", [P, 6]) for n in range(2)]
        aw_w = sb("aw_w", [P, 6])
        aw_c = [sb(f"aw_c{n}", [P, 1]) for n in range(3)]
        st_nr = sb("st_nr", [64 + 32, B])
        w1_mem = sb("w1_mem", [MU, D])
        w1_nr = sb("w1_nr", [64 + 32, D])
        nets = ((w1_mem, mu, 0, MU), (w1_nr, st_nr, 0, 64), (w1_nr, st_nr, 64, 96))
        w2n = sb("w2n", [P, 3, KB, D])
        rown = sb("rown", [P, 3, 3, D])
        hid = sb("hid", [P, 3, KB, B])
        mo = [sb(f"mo{n}", [P, 3, D]) for n in range(3)]
        mo_bn = sb("mo_bn", [P, 3, 6])
        mo_mv = sb("mo_mv", [P, 3, 2])
        mo_ve = sb("mo_ve", [P, 3])
        mo_r = sb("mo_r", [P, 3])
        mo_t = sb("mo_t", [P, 3, KB, B])
        cls_t = sb("cls_t", [P, 3, KB, CLS])
        cls_const = sb("cls_const", [CLS, 1 + PIECES])
        tab = [sb(f"tab{n}", [CLS, 3 * D]) for n in range(3)]
        tab_p = [sb(f"tab_p{n}", [CLS, 3 * D], BF16) for n in range(3)]
        clsb = [sb(f"clsb{n}", [CLS, D]) for n in range(3)]
        clsb_p = [sb(f"clsb_p{n}", [CLS, D], BF16) for n in range(3)]
        rowb = [sb(f"rowb{n}", [B, D]) for n in range(3)]
        rowb_p = sb("rowb_p", [B, PIECES, D], BF16)
        b2f = [sb(f"b2f{n}", [PIECES, D]) for n in range(3)]
        b2p = [sb(f"b2p{n}", [PIECES, D], BF16) for n in range(3)]

        d_cond, d_net1, d_net2, d_l1, d_bias, d_dec0, d_dec1, d_aw, d_w1, d_gain, d_cls, d_const, d_wts, d_fin = (
            sem("d_" + n) for n in "cond net1 net2 l1 bias dec0 dec1 aw w1 gain cls const wts fin".split())
        (m_pre, m_dc, m_hid, m_mo, m_mot, m_row, m_cls, m_dec) = (
            sem("m_" + n) for n in "pre dc hid mo mot row cls dec".split())
        c_style, c_pre, c_dc, c_hid, c_exp, c_wh, c_w1, c_w1h, c_mot = (
            sem("c_" + n) for n in "style pre dc hid exp wh w1 w1h mot".split())
        v_st2, v_dca, v_rcp, v_aw, v_soft, v_w1x, v_mve, v_mo, v_shift, v_rowb, v_dec, v_chain = (
            sem("v_" + n) for n in "st2 dca rcp aw soft w1x mve mo shift rowb dec chain".split())
        z_tab, z_pool, g_tab, g_r, g_chain = (sem(n) for n in "z_tab z_pool g_tab g_r g_chain".split())
        ps_a, ps_b, ps_c, ps_d = k["ps_a"], k["ps_b"], k["ps_c"], k["ps_d"]
        flat_c = ps_c[:, :, :].rearrange("p k n -> p (k n)")
        rows_b = k["rows_of"](ps_b)
        bias_cols = k["bias_cols"]
        counts = {}

        def feat(ap):
            return ap.rearrange("(k p) n -> p k n", p=P)

        def row(ap):
            return ap.rearrange("(o n) -> o n", o=1)

        def load(eng, s, dst, src):
            eng.dma_start(dst, src).then_inc(s, 16)
            counts[s.name] = counts.get(s.name, 0) + 16

        def loaded(eng, *sems):
            for s in sems:
                eng.wait_ge(s, counts[s.name])

        def chain(eng, s):
            done = [0]
            def link(ins):
                done[0] += 1
                ins.then_inc(s, 1)
                eng.wait_ge(s, done[0])
            return link

        def split(eng, link, src, r1, r2, p1, p2, p3):
            link(eng.tensor_copy(p1, src))
            link(eng.tensor_tensor(r1, src, p1, ALU.subtract))
            link(eng.tensor_copy(p2, r1))
            link(eng.tensor_tensor(r2, r1, p2, ALU.subtract))
            link(eng.tensor_copy(p3, r2))

        def pick(eng, link, out, r1, p1, p2, p3, masks):
            link(eng.tensor_scalar(r1, p1, masks[:, 0:1], None, ALU.mult))
            link(eng.scalar_tensor_tensor(r1, p2, masks[:, 1:2], r1, ALU.mult, ALU.add))
            return eng.scalar_tensor_tensor(out, p3, masks[:, 2:3], r1, ALU.mult, ALU.add)

        w1_parts = ((0, w1[:, 0:4, :]), (4, w1x[:, :, :]), (6, w1[:, 10:12, :]))
        groups = [(c, r, min(r + 4, RK)) for c in range(KB) for r in range(0, RK, 4)]
        banks = (ps_d[:, 0, :], ps_d[:, 1, :], ps_a[:, 0, :], ps_a[:, 1, :])
        per_half = len(groups) // KB

        block = ctx.enter_context(nc.Block())

        @block.sync
        def _(eng):
            load(eng, d_cond, cond[:, :], t["cond_side"])
            load(eng, d_net1, w1_mem[:, :], t["mem_W1"])
            load(eng, d_net1, w1_nr[:, :], t["nr_W1"])
            load(eng, d_net1, st_nr[:, :], t["nr_t"])
            load(eng, d_bias, bias_cols[:, :], t["bias_cols"])
            load(eng, d_l1, l1_w[:, :, :], feat(t["l1_wt"]))
            load(eng, d_aw, aw[:, :], row(t["aw"]).broadcast_to([P, 6]))
            half = P * RK
            load(eng, d_dec0, bdec[:, :, :], t["b_dec"][0:D * RK].rearrange("(k p r) -> p k r", k=KB, p=P))
            load(eng, d_dec0, bdec_u[:, :], t["b_dec"][D * RK:width].rearrange("(r o) -> r o", o=1))
            load(eng, d_dec0, wdec[:, 0:half], t["W_dec"][:, 0:half])
            load(eng, d_net2, w2n[:, :, :, :].rearrange("p n k d -> p (n k) d"), feat(t["nets_W2"]))
            load(eng, d_net2, rown[:, :, :, :].rearrange("p n m d -> p (n m d)"),
                 row(t["nets_rows"]).broadcast_to([P, 9 * D]))
            load(eng, d_dec1, wdec[:, half:width], t["W_dec"][:, half:width])
            load(eng, d_w1, w1[:, :, :], feat(t["int_W1"]))
            load(eng, d_const, k["ident"][:, :], t["ident"])
            load(eng, d_wts, down_w[:, :, 0:HID], feat(t["down_p"]))
            load(eng, d_wts, w2[:, :, :], feat(t["int_W2"]))
            load(eng, d_wts, v_rep[:, :], t["V3"])
            load(eng, d_fin, k["up_rep"][:, :], t["up_p2"])
            load(eng, d_fin, k["ln_gb"][:, :], row(t["int_gb"]).broadcast_to([P, 2 * D]))
            load(eng, d_fin, k["pw_idx"][:, :], t["itok_t"])
            for n in range(2):
                load(eng, d_fin, k["onehot"][n][CLS:CLS + BRW, :], t["entry_rows"])
            eng.wait_ge(c_pre, 1)
            load(eng, d_fin, k["ugub_d"], ugub_row[:, :])
            for c in range(KB):
                eng.wait_ge(v_dec, per_half * (c + 1))
                load(eng, d_fin, k["u_d"][:, :, c].rearrange("n p b r -> p n (b r)"),
                     u_all[:, c].rearrange("p (n b) r -> p n (b r)", b=CB))
            eng.wait_ge(v_rowb, 1)
            load(eng, d_fin, k["row_d"], rowb_p[:, :, :])
            loaded(eng, d_fin)

        @block.gpsimd
        def _(eng):
            link = chain(eng, g_chain)
            eng.memset(tab[0][:, :], 0.0).then_inc(z_tab, 1)
            eng.memset(cls_t[:, :, :, :], 0.0).then_inc(z_tab, 1)
            eng.wait_ge(z_tab, 2)
            ncp = PIECES * NCP
            load(eng, d_gain, cls_const[:, :], t["cls_const"])
            load(eng, d_gain, tab[0][0:ncp, 0:2 * D], t["cptm_g"])
            load(eng, d_gain, tab[0][ncp:CLS, 2 * D:3 * D], t["ms_g"])
            load(eng, d_gain, b2f[0][:, :], row(t["int_b2"]).broadcast_to([PIECES, D]))
            for n in range(2):
                load(eng, d_cls, cls_t[:, n, :, 0:ncp], feat(t[("cp_bt", "tm_bt")[n]]))
            load(eng, d_cls, cls_t[:, 2, :, ncp:CLS], feat(t["ms_bt"]))
            eng.memset(k["mhalf"][:, :], -0.5).then_inc(z_pool, 1)
            eng.memset(k["ones3"][:, :], 1.0).then_inc(z_pool, 1)
            eng.memset(down_w[:, :, HID:P], 1.0).then_inc(z_pool, 1)
            eng.memset(k["act_bd"][:, :, :], 0.0).then_inc(z_pool, 1)
            eng.memset(zeros[:, :], 0.0).then_inc(z_pool, 1)
            loaded(eng, d_gain)
            pieces = [p[:, :] for p in tab_p]
            link(eng.tensor_copy(k["cls_neg"][:, :], cls_const[:, 0:1]))
            split(eng, link, tab[0][:, :], tab[1][:, :], tab[2][:, :], *pieces)
            eng.wait_ge(v_mve, 1)
            eng.wait_ge(z_pool, 5)
            link(eng.tensor_scalar(mo_ve[:, :], mo_mv[:, :, 1], EPS, 1.0, ALU.add, ALU.mult))
            eng.tensor_tensor(mo_r[:, :], mo_ve[:, :], k["mhalf"][:, 0:3], ALU.pow).then_inc(g_r, 1)
            eng.sem_inc(g_tab, 1)
            eng.wait_ge(v_rcp, 1)
            link(eng.tensor_tensor(dm[3][:, :, :], dm[0][:, :, :], dm[2][:, :, :], ALU.mult))
            link(eng.tensor_tensor(dm[4][:, :, :], dm[3][:, :, :], dm[2][:, :, :], ALU.mult))
            link(eng.tensor_scalar(dm[3][:, :, :], dm[4][:, :, :], -0.5, 1.5, ALU.mult, ALU.add))
            eng.tensor_tensor(k["dcoef"][:, :, :], dm[2][:, :, :], dm[3][:, :, :], ALU.mult)
            loaded(eng, d_const)
            pieces = [p[:, :] for p in b2p]
            split(eng, link, b2f[0][:, :], b2f[1][:, :], b2f[2][:, :], *pieces)
            ident = k["ident"]
            link(eng.tensor_scalar(b2f[1][:, :], pieces[0], ident[0:PIECES, 0:1], None, ALU.mult))
            for e in range(1, PIECES):
                link(eng.tensor_scalar(b2f[2][:, :], pieces[e], ident[0:PIECES, e:e + 1], None, ALU.mult))
                out = (b2f[1] if e < PIECES - 1 else k["b2_row"])[:, :]
                link(eng.tensor_tensor(out, b2f[1][:, :], b2f[2][:, :], ALU.add))
            def lower(lo, src, hi):
                eng.tensor_tensor(lo, src, hi.bitcast(F32), ALU.subtract)
            eng.wait_ge(c_wh, 1)
            lower(k["l1_w_l"][:, :, :], l1_w[:, :, :], k["l1_w_h"][:, :, :])
            lower(k["down_w_l"][:, :, :], down_w[:, :, :], k["down_w_h"][:, :, :])
            lower(k["w2_l"][:, :, :], w2[:, :, :], k["w2_h"][:, :, :])
            eng.wait_ge(c_w1h, 1)
            for first, src in w1_parts:
                cut = slice(first, first + src.shape[1])
                lower(k["w1_l"][:, cut, :], src, k["w1_h"][:, cut, :])

        @block.scalar
        def _(eng):
            eng.wait_ge(m_pre, 1)
            loaded(eng, d_bias)
            for o in range(KB):
                m = eng.activation(k["style"][:, o, :], ps_a[:, 0, o * P:(o + 1) * P], ACT.Identity,
                                   bias=bias_cols[:, 2 * KB + o:2 * KB + o + 1],
                                   scale=float(np.float32(1.0) / np.sqrt(np.float32(MU))))
            m.then_inc(c_style, 1)
            eng.activation(k["dgdb"][:, :], ps_a[:, 0, 2 * P:3 * P], ACT.Copy)
            eng.activation(ugub_row[:, :], ps_a[:, 1, :], ACT.Copy).then_inc(c_pre, 1)
            eng.wait_ge(m_hid, 1)
            for j in range(3 * KB):
                m = eng.activation(hid[:, j // KB, j % KB, :], flat_c[:, j * P:(j + 1) * P], ACT.Silu,
                                   bias=bias_cols[:, 3 * KB + j:3 * KB + j + 1])
            m.then_inc(c_hid, 1)
            eng.wait_ge(v_dca, 1)
            eng.activation(dm[1][:, :, :], dm[0][:, :, :], ACT.Sqrt).then_inc(c_dc, 1)
            eng.wait_ge(v_aw, 1)
            eng.activation(aw_s[1][:, :], aw_s[0][:, :], ACT.Exp).then_inc(c_exp, 1)
            loaded(eng, d_w1)
            eng.wait_ge(v_soft, 1)
            for n in range(6):
                part = w1[:, 2 * n:2 * n + 2, :]
                m = eng.activation(part, part, ACT.Copy, scale=aw_w[:, n:n + 1])
            m.then_inc(c_w1, 1)
            loaded(eng, d_l1, d_wts)
            eng.wait_ge(z_pool, 5)
            eng.activation(k["l1_w_h"][:, :, :], l1_w[:, :, :], ACT.Copy)
            eng.activation(k["down_w_h"][:, :, :], down_w[:, :, :], ACT.Copy)
            eng.activation(k["w2_h"][:, :, :], w2[:, :, :], ACT.Copy)
            eng.activation(k["v_st"][:, :], v_rep[:, :], ACT.Copy).then_inc(c_wh, 1)
            eng.activation(k["t_st"][:, :], zeros[:, :], ACT.Copy)
            loaded(eng, d_const)
            eng.wait_ge(c_w1, 1)
            eng.activation(k["two_i"][:, :], k["ident"][:, :], ACT.Copy, scale=2.0)
            eng.wait_ge(m_mot, 1)
            eng.activation(mo_t[:, :, :, :], flat_c[:, 0:3 * KB * P].rearrange(
                "p (n k b) -> p n k b", n=3, k=KB), ACT.Copy).then_inc(c_mot, 1)
            eng.wait_ge(v_w1x, 1)
            for first, src in w1_parts:
                m = eng.activation(k["w1_h"][:, first:first + src.shape[1], :], src, ACT.Copy)
            m.then_inc(c_w1h, 1)
            eng.wait_ge(v_shift, 1)
            eng.activation(k["shift"][1][0:CLS, :], k["shift"][0][0:CLS, :], ACT.Copy)

        @block.tensor
        def _(eng):
            loaded(eng, d_cond)
            for o in range(KB):
                eng.matmul(ps_a[:, 0, o * P:(o + 1) * P], aff[:, o * P:(o + 1) * P], mu, start=True, stop=True)
            eng.matmul(ps_a[:, 0, 2 * P:3 * P], dgb, mu, start=True, stop=True)
            eng.matmul(ps_a[:, 1, :], mu, ugb, start=True, stop=True).then_inc(m_pre, 1)
            loaded(eng, d_net1)
            for n, (w, s, lo, hi) in enumerate(nets):
                for o in range(KB):
                    j = n * KB + o
                    m = eng.matmul(flat_c[:, j * P:(j + 1) * P], w[lo:hi, o * P:(o + 1) * P], s[lo:hi, :],
                                   start=True, stop=True)
            m.then_inc(m_hid, 1)
            eng.wait_ge(v_st2, 1)
            for o in range(KB):
                for c in range(KB):
                    m = eng.matmul(ps_b[:, 0, o * P:(o + 1) * P], wsq[:, c, o * P:(o + 1) * P], style2[:, c, :],
                                   start=c == 0, stop=c == KB - 1)
            m.then_inc(m_dc, 1)
            w = wdec[:, :].rearrange("m (i r) -> m r i", r=RK)

            def decode(first, end):
                for n in range(first, end):
                    c, r0, r1 = groups[n]
                    if n == 2:
                        eng.wait_ge(c_pre, 1)
                    if n >= 4:
                        eng.wait_ge(v_dec, n - 3)
                    for r in range(r0, r1):
                        m = eng.matmul(banks[n % 4][:, (r - r0) * B:(r - r0 + 1) * B], w[:, r, c * P:(c + 1) * P],
                                       mu, start=True, stop=True)
                    m.then_inc(m_dec, 1)

            loaded(eng, d_dec0)
            decode(0, per_half)
            eng.wait_ge(c_hid, 1)
            eng.wait_ge(v_dca, 1)
            loaded(eng, d_net2)
            for n in range(3):
                for c in range(KB):
                    m = eng.matmul(rows_b[:, n, :], hid[:, n, c, :], w2n[:, n, c, :], start=c == 0, stop=c == KB - 1)
            m.then_inc(m_mo, 1)
            loaded(eng, d_dec1)
            decode(per_half, per_half + 4)
            loaded(eng, d_const)
            eng.wait_ge(v_mo, 1)
            for j in range(3 * KB):
                m = eng.transpose(flat_c[:, j * P:(j + 1) * P], mo[0][:, j // KB, j % KB * P:(j % KB + 1) * P],
                                  k["ident"][:, :])
            m.then_inc(m_mot, 1)
            decode(per_half + 4, len(groups))
            n = len(groups)
            eng.wait_ge(v_dec, n - 3)
            eng.matmul(banks[n % 4][0:RK, 0:B], w[:, :, D], mu, start=True, stop=True).then_inc(m_dec, 1)
            eng.wait_ge(c_mot, 1)
            eng.wait_ge(c_w1, 1)
            for n in range(3):
                for c in range(KB):
                    m = eng.matmul(ps_b[:, 0, 0:D], mo_t[:, n, c, :], w1[:, 4 + 2 * n + c, :],
                                   start=n + c == 0, stop=n == 2 and c == KB - 1)
            m.then_inc(m_row, 1)
            loaded(eng, d_cls)
            for n, first in enumerate((0, 2, 10)):
                for c in range(KB):
                    m = eng.matmul(ps_b[0:CLS, 1, 0:D], cls_t[:, n, c, :], w1[:, first + c, :],
                                   start=n + c == 0, stop=n == 2 and c == KB - 1)
            m.then_inc(m_cls, 1)

        @block.vector
        def _(eng):
            link = chain(eng, v_chain)

            def decoded(first, end):
                for n in range(first, end):
                    c, r0, r1 = groups[n]
                    eng.wait_ge(m_dec, n + 1)
                    bias = bdec[:, c, r0:r1].unsqueeze(2).broadcast_to([P, r1 - r0, B])
                    eng.tensor_tensor(u_all[:, c, :, r0:r1].rearrange("p b r -> p r b"),
                                      banks[n % 4][:, 0:(r1 - r0) * B].rearrange("p (r b) -> p r b", b=B), bias,
                                      ALU.add).then_inc(v_dec, 1)

            loaded(eng, d_aw)
            link(eng.reduce_max(aw_c[0][:, :], aw[:, :], AX.X))
            eng.tensor_scalar(aw_s[0][:, :], aw[:, :], aw_c[0][:, 0:1], None, ALU.subtract).then_inc(v_aw, 1)
            loaded(eng, d_l1)
            eng.tensor_tensor(wsq[:, :, :], l1_w[:, :, :], l1_w[:, :, :], ALU.mult)
            eng.wait_ge(c_style, 1)
            eng.tensor_tensor(style2[:, :, :], k["style"][:, :, :], k["style"][:, :, :], ALU.mult).then_inc(v_st2, 1)
            eng.wait_ge(m_dc, 1)
            link(eng.tensor_scalar(dm[0][:, :, :], ps_b[:, 0, 0:KB * P].rearrange("p (k b) -> p k b", k=KB),
                                   DEMOD_EPS, None, ALU.add))
            eng.sem_inc(v_dca, 1)
            loaded(eng, d_dec0)
            decoded(0, 2)
            eng.wait_ge(c_dc, 1)
            eng.reciprocal(dm[2][:, :, :], dm[1][:, :, :]).then_inc(v_rcp, 1)
            decoded(2, per_half)
            eng.wait_ge(c_exp, 1)
            link(eng.reduce_sum(aw_c[1][:, :], aw_s[1][:, :], AX.X))
            link(eng.reciprocal(aw_c[2][:, :], aw_c[1][:, :]))
            eng.tensor_scalar(aw_w[:, :], aw_s[1][:, :], aw_c[2][:, 0:1], None, ALU.mult).then_inc(v_soft, 1)
            eng.wait_ge(m_mo, 1)
            loaded(eng, d_net2)
            link(eng.tensor_tensor(mo[1][:, :, :], rows_b[:, 0:3, :], rown[:, :, 0, :], ALU.add))
            for n in range(3):
                last = eng.bn_stats(mo_bn[:, n, :], mo[1][:, n, :])
            link(last)
            for n in range(3):
                last = eng.bn_aggr(mo_mv[:, n, :], mo_bn[:, n, :])
            last.then_inc(v_mve, 1)
            eng.wait_ge(g_r, 1)
            eng.wait_ge(v_mve, 1)
            for n in range(3):
                last = eng.tensor_scalar(mo[2][:, n, :], mo[1][:, n, :], mo_mv[:, n, 0:1], mo_r[:, n:n + 1],
                                         ALU.subtract, ALU.mult)
            link(last)
            link(eng.tensor_tensor(mo[1][:, :, :], mo[2][:, :, :], rown[:, :, 1, :], ALU.mult))
            eng.tensor_tensor(mo[0][:, :, :], mo[1][:, :, :], rown[:, :, 2, :], ALU.add).then_inc(v_mo, 1)
            loaded(eng, d_dec1)
            decoded(per_half, per_half + 4)
            eng.wait_ge(c_w1, 1)
            link(eng.tensor_tensor(w1x[:, :, :], w1[:, 4:6, :], w1[:, 6:8, :], ALU.add))
            eng.tensor_tensor(w1x[:, :, :], w1x[:, :, :], w1[:, 8:10, :], ALU.add).then_inc(v_w1x, 1)
            decoded(per_half + 4, len(groups))
            eng.wait_ge(c_wh, 1)
            v_low = k["v_st"][RP:2 * RP, :]
            eng.tensor_tensor(v_low, v_rep[RP:2 * RP, :], v_low.bitcast(F32), ALU.subtract)
            eng.wait_ge(g_tab, 1)
            loaded(eng, d_gain)
            masks = cls_const[:, 1:1 + PIECES]
            link(pick(eng, link, k["gain_tab"][:, :], tab[1][:, :], *(p[:, :] for p in tab_p), masks))
            n = len(groups)
            eng.wait_ge(m_dec, n + 1)
            eng.tensor_scalar(k["ub_t"][:, :], banks[n % 4][0:RK, 0:B], bdec_u[:, 0:1], None, ALU.add)
            eng.wait_ge(m_row, 1)
            link(eng.tensor_copy(rowb[0][:, :], ps_b[:, 0, 0:D]))
            split(eng, link, rowb[0][:, :], rowb[1][:, :], rowb[2][:, :], *(rowb_p[:, e, :] for e in range(PIECES)))
            eng.sem_inc(v_rowb, 1)
            eng.wait_ge(m_cls, 1)
            link(eng.tensor_copy(clsb[0][:, :], ps_b[0:CLS, 1, 0:D]))
            pieces = [p[:, :] for p in clsb_p]
            split(eng, link, clsb[0][:, :], clsb[1][:, :], clsb[2][:, :], *pieces)
            pick(eng, link, k["shift"][0][0:CLS, :], clsb[1][:, :], *pieces, masks).then_inc(v_shift, 1)


def conditioned_residuals(nc, t):
    ctx = ExitStack()
    with ctx:
        def sb(name, shape, dt=F32):
            return ctx.enter_context(nc.sbuf_tensor(name, shape, dt))

        def sem(name):
            return ctx.enter_context(nc.semaphore(name))

        ps_a, ps_b, ps_c, ps_d = (
            ctx.enter_context(nc.psum_tensor(f"ps_{n}", [P, KB, CH], F32)) for n in "abcd")

        def rows_of(ps):
            return ps[:, :, :].rearrange("p k (u d) -> p (k u) d", d=D)

        ident = sb("ident", [P, P])
        two_i = sb("two_i", [P, P], F32R)
        mhalf = sb("mhalf", [P, CT])
        cls_neg = sb("cls_neg", [CLS, 1])
        ub_t = sb("ub_t", [RK, B])
        v_st = sb("v_st", [3 * RP, D], F32R)
        style = sb("style", [P, KB, B])
        dcoef = sb("dcoef", [P, KB, B])
        l1_w_h, l1_w_l = (sb(f"l1_w_{e}", [P, KB, D], F32R) for e in "hl")
        bias_cols = sb("bias_cols", [P, 6 * KB])
        l1_b = bias_cols[:, 0:KB]
        b1 = bias_cols[:, KB:2 * KB]
        down_w_h, down_w_l = (sb(f"down_w_{e}", [P, KB, P], F32R) for e in "hl")
        dgdb = sb("dgdb", [P, B])
        up_rep = sb("up_rep", [P, D])
        w1_h, w1_l = (sb(f"w1_{e}", [P, 8, D], F32R) for e in "hl")
        w2_h, w2_l = (sb(f"w2_{e}", [P, KB, D], F32R) for e in "hl")
        b2_row = sb("b2_row", [PIECES, D], BF16)
        ones3 = sb("ones3", [PIECES, P], BF16)
        ln_gb = sb("ln_gb", [P, 2 * D])
        ln_g, ln_be = ln_gb[:, 0:D], ln_gb[:, D:2 * D]
        gain_tab = sb("gain_tab", [CLS, 3 * D], BF16)
        pw_idx = sb("pw_idx", [P, ROWS // P], I32)

        ugub_d = nc.dram_tensor("ugub_scratch", (B, 2 * D), F32, kind="Internal").ap()
        u_d = nc.dram_tensor("u_scratch", (NCH, P, KB, CB, RK), F32, kind="Internal").ap()
        row_d = nc.dram_tensor("row_scratch", (B, PIECES, D), BF16, kind="Internal").ap()

        onehot = [sb(f"onehot{r}", [CLS + BRW, CH], BF16) for r in range(2)]
        shift = [sb(f"shift{r}", [CLS + BRW, D], BF16) for r in range(2)]
        act_bd = sb("act_bd", [P, CT, P])
        t_st = sb("t_st", [3 * RP, CH], F32R)

        setup(nc, locals())

        x_t = [sb(f"x_t{r}", [P, KB, CH]) for r in range(2)]
        u_ch = [sb(f"u_ch{r}", [P, KB, CB, RK]) for r in range(2)]
        ugub = sb("ugub", [P, CT, 2 * D])
        idx_ch = [sb(f"idx_ch{r}", [CLS, CH], I32) for r in range(2)]
        pw_rows = sb("pw_rows", [P, CT, 2 * D])
        gidx = sb("gidx", [P, CT], I32)
        oh_sq = sb("oh_sq", [CLS, CH], BF16)
        t_t = sb("t_t", [RK, CH])
        x1_t = sb("x1_t", [P, KB, CH])
        xm_t = sb("xm_t", [P, KB, CH])
        xm_t_h, xm_t_l = (sb(f"xm_t_{e}", [P, KB, CH], F32R) for e in "hl")
        l1_u = xm_t
        x2_t = x1_t
        x2_t_h, x2_t_l = (sb(f"x2_t_{e}", [P, KB, CH], F32R) for e in "hl")
        dn_u = sb("dn_u", [HID, CH])
        dn_v = sb("dn_v", [HID, CH])
        dn = sb("dn", [HID, CH])
        w_up = sb("w_up", [P, CT, D])
        x3 = sb("x3", [P, CT, D])
        x3be = [sb(f"x3be{r}", [P, CT, D]) for r in range(2)]
        xhat = sb("xhat", [P, CT, D])
        h1 = sb("h1", [P, CT, D])
        x3_t_h, x3_t_l = (sb(f"x3_t_{e}", [P, KB, CH], F32R) for e in "hl")
        xh_t = sb("xh_t", [P, KB, CH])
        hh_t = sb("hh_t", [P, KB, CH])
        tm_t = sb("tm_t", [P, KB, CH])
        tm_t_h, tm_t_l = (sb(f"tm_t_{e}", [P, KB, CH], F32R) for e in "hl")
        ms_t = sb("ms_t", [P, KB, CH])
        ms_t_h, ms_t_l = (sb(f"ms_t_{e}", [P, KB, CH], F32R) for e in "hl")
        h_t = tm_t
        h_t_h, h_t_l = (sb(f"h_t_{e}", [P, KB, CH], F32R) for e in "hl")
        act_t = hh_t
        act_t_h, act_t_l = (sb(f"act_t_{e}", [P, KB, CH], F32R) for e in "hl")
        y_out = [sb(f"y_out{r}", [P, CT, D]) for r in range(2)]
        bn = {k: sb(f"bn_{k}", [P, CT, 6]) for k in "xhy"}
        mv = {k: sb(f"mv_{k}", [P, CT, 2]) for k in "xhy"}
        ve = {k: sb(f"ve_{k}", [P, CT]) for k in "xhy"}
        rstd = {k: sb(f"rstd_{k}", [P, CT]) for k in "xhy"}
        nb = {k: sb(f"nb_{k}", [P, CT]) for k in "xh"}

        s_x = [sem(f"s_x{r}") for r in range(2)]
        s_u = [sem(f"s_u{r}") for r in range(2)]
        s_ug = sem("s_ug")
        s_idx = [sem(f"s_idx{r}") for r in range(2)]
        s_row = [sem(f"s_row{r}") for r in range(2)]
        s_pw = sem("s_pw")
        s_idle = sem("s_idle")
        s_store = [sem(f"s_store{r}") for r in range(2)]
        (p_t, p_x1, p_l1, p_dn, p_up, p_x3t, p_xht, p_tm, p_ms, p_hht, p_cp, p_w1x, p_w1t, p_w1m, p_w1, p_w2) = (
            sem("p_" + n) for n in "t x1 l1 dn up x3t xht tm ms hht cp w1x w1t w1m w1 w2".split())
        (a_relu, a_x3, a_x3h, a_xht, a_hht, a_silu, a_silh, a_xmh, a_x2h, a_tmh, a_msh, a_hh, a_sq, a_oh,
         a_xhat, a_hhat, a_th) = (
            sem("a_" + n) for n in "relu x3 x3h xht hht silu silh xmh x2h tmh msh hh sq oh xhat hhat th".split())
        (v_t, v_x1, v_l1u, v_l1v, v_x2, v_dnu, v_dn, v_bnx, v_mvx, v_xnb, v_bnh, v_mvh, v_hnb,
         v_tm, v_ms, v_h, v_bny, v_mvy, v_y1, v_y, v_xml, v_x2l, v_x3l, v_hl, v_sill,
         v_tl, v_vex, v_veh, v_vey) = (
            sem("v_" + n) for n in
            "t x1 l1u l1v x2 dnu dn bnx mvx xnb bnh mvh hnb tm ms h bny mvy y1 y "
            "xml x2l x3l hl sill tl vex veh vey".split())
        g_gidx, g_xm, g_rx, g_h1m, g_h1, g_rh, g_upm, g_up, g_x3be, g_ry, g_tml, g_msl = (
            sem("g_" + n) for n in "gidx xm rx h1m h1 rh upm up x3be ry tml msl".split())

        x_d = t["x_t"].rearrange("(k p) (c n) -> c p k n", p=P, n=CH)
        out_d = t["out"].rearrange("(c k p) d -> c p k d", k=CT, p=P)
        ug_d = ugub_d.rearrange("(c k h) d -> c h k d", k=CT, h=2)
        tok_d = t["itok4"].rearrange("(c o n) -> c o n", o=1, n=CH)
        mask_d = t["mask"].rearrange("(c o n) -> c o n", o=1, n=CH)
        rowc_d = row_d.rearrange("(c b) e d -> c (b e) d", b=CB)

        def one(ap, c):
            return ap[c.n]

        def cols(table, c):
            k = table.shape[1]
            return table[:, :, bass.ds(c.n * CB, CB)].unsqueeze(3).broadcast_to([P, k, CB, S])

        def by_entry(ap):
            return ap.rearrange("p k (b s) -> p k b s", s=S)

        def load(eng, c):
            r = c.ring
            wait(eng, v_x1, c.n - 1)
            eng.dma_start(x_t[r][:, :, :], one(x_d, c)).then_inc(s_x[r], 16)
            wait(eng, p_t, c.n - 1)
            eng.dma_start(u_ch[r][:, :, :, :],
                          one(u_d, c)).then_inc(s_u[r], 16)
            wait(eng, a_sq, c.n - 1)
            ncp = PIECES * NCP
            eng.dma_start(idx_ch[r][0:ncp, :], one(tok_d, c).broadcast_to([ncp, CH])).then_inc(s_idx[r], 16)
            eng.dma_start(idx_ch[r][ncp:CLS, :],
                          one(mask_d, c).broadcast_to([CLS - ncp, CH])).then_inc(s_idx[r], 16)

        def load_shift(eng, c):
            wait(eng, p_w1, c.n - 1)
            eng.dma_start(shift[c.ring][CLS:CLS + BRW, :], one(rowc_d, c)).then_inc(s_row[c.ring], 16)

        def load_up(eng, c):
            wait(eng, g_up, c.n)
            for h in range(2):
                src = one(ug_d, c)[h:h + 1].broadcast_to([HID, CT, 2 * D])
                eng.dma_start(ugub[h * HID:(h + 1) * HID, :, :], src).then_inc(s_ug, 16)

        def store(eng, c):
            wait(eng, v_y, c.n + 1)
            eng.dma_start(one(out_d, c), y_out[c.ring][:, :, :]).then_inc(s_store[c.ring], 16)

        def product(eng, out, w, act, first, last):
            (wh, wl), (ah, al) = w, act
            eng.matmul(out, wl, ah, start=first, stop=False)
            eng.matmul(out, wh, al, start=False, stop=False)
            return eng.matmul(out, wh, ah, start=False, stop=last)

        def pe_t(eng, c):
            wait(eng, s_x[c.ring], 16 * (c.half + 1))
            wait(eng, v_l1u, c.n)
            wait(eng, s_u[c.ring], 16 * (c.half + 1))
            for b in range(CB):
                for k in range(KB):
                    m = eng.matmul(ps_a[0:RK, 0, b * S:(b + 1) * S], u_ch[c.ring][:, k, b, :],
                                   x_t[c.ring][:, k, b * S:(b + 1) * S], start=k == 0, stop=k == KB - 1)
            m.then_inc(p_t, 1)

        def pe_x1(eng, c):
            wait(eng, v_tl, c.n + 1)
            for k in range(KB):
                m = eng.matmul(ps_a[:, k, :], v_st[:, k * P:(k + 1) * P], t_st[:, :], start=True, stop=True)
            m.then_inc(p_x1, 1)

        def pe_l1(eng, c):
            wait(eng, v_x1, c.n + 1)
            wait(eng, v_xml, c.n + 1)
            for o in range(KB):
                cut = slice(o * P, (o + 1) * P)
                for k in range(KB):
                    m = product(eng, ps_a[:, o, :], (l1_w_h[:, k, cut], l1_w_l[:, k, cut]),
                                (xm_t_h[:, k, :], xm_t_l[:, k, :]), k == 0, k == KB - 1)
            m.then_inc(p_l1, 1)

        def pe_dn(eng, c):
            wait(eng, v_x2l, c.n + 1)
            wait(eng, v_ms, c.n)
            for k in range(KB):
                m = product(eng, ps_b[:, 0, :], (down_w_h[:, k, :], down_w_l[:, k, :]),
                            (x2_t_h[:, k, :], x2_t_l[:, k, :]), k == 0, k == KB - 1)
            m.then_inc(p_dn, 1)

        def pe_up(eng, c):
            wait(eng, a_relu, c.n + 1)
            wait(eng, v_dn, c.n + 1)
            wait(eng, g_up, c.n + 1)
            out = rows_of(ps_b)
            for tiles in ((0, 2), (1, 3)):
                for j in tiles:
                    eng.matmul(out[:, j, :], act_bd[:, j, :], w_up[:, j, :], start=True, stop=False)
                for j in tiles:
                    for k in range(KB):
                        for half in (x2_t_l, x2_t_h):
                            m = eng.matmul(out[:, j, k * P:(k + 1) * P], half[:, k, j * P:(j + 1) * P],
                                           two_i[:, :], start=False, stop=k == KB - 1 and half is x2_t_h)
            m.then_inc(p_up, 1)

        def transposes(eng, out, src):
            for k in range(KB):
                for j in range(CT):
                    m = eng.transpose(out[:, k, j * P:(j + 1) * P], src[:, j, k * P:(k + 1) * P], ident[:, :])
            return m

        def pe_x3t(eng, c):
            wait(eng, a_x3, c.n + 1)
            transposes(eng, ps_b, x3).then_inc(p_x3t, 1)

        def pe_xht(eng, c):
            wait(eng, a_xhat, c.n + 1)
            wait(eng, v_h, c.n)
            transposes(eng, ps_c, xhat).then_inc(p_xht, 1)

        def gains(eng, out, c, first):
            for k in range(KB):
                m = eng.matmul(out[:, k, :], gain_tab[:, first + k * P:first + (k + 1) * P],
                               onehot[c.ring][0:CLS, :], start=True, stop=True)
            return m

        def pe_tm(eng, c):
            wait(eng, a_oh, c.n + 1)
            wait(eng, a_xht, c.n + 1)
            gains(eng, ps_c, c, D).then_inc(p_tm, 1)

        def pe_ms(eng, c):
            wait(eng, a_oh, c.n + 1)
            wait(eng, v_x3l, c.n + 1)
            gains(eng, ps_b, c, 2 * D).then_inc(p_ms, 1)

        def pe_hhat(eng, c):
            wait(eng, a_hhat, c.n + 1)
            wait(eng, v_tm, c.n + 1)
            transposes(eng, ps_c, h1).then_inc(p_hht, 1)

        def pe_cp(eng, c):
            wait(eng, a_hht, c.n + 1)
            gains(eng, ps_c, c, 0).then_inc(p_cp, 1)

        def w1_part(eng, c, first, ah, al, last):
            for o in range(KB):
                cut = slice(o * P, (o + 1) * P)
                for k in range(KB):
                    m = product(eng, ps_d[:, o, :], (w1_h[:, first + k, cut], w1_l[:, first + k, cut]),
                                (ah[:, k, :], al[:, k, :]), False, last and k == KB - 1)
            return m

        def pe_w1_x3(eng, c):
            wait(eng, v_y1, c.n)
            wait(eng, a_oh, c.n + 1)
            wait(eng, s_row[c.ring], 16 * (c.half + 1))
            for o in range(KB):
                eng.matmul(ps_d[:, o, :], shift[c.ring][:, o * P:(o + 1) * P], onehot[c.ring][:, :],
                           start=True, stop=False)
            wait(eng, v_x3l, c.n + 1)
            w1_part(eng, c, 4, x3_t_h, x3_t_l, False).then_inc(p_w1x, 1)

        def pe_w1_tm(eng, c):
            wait(eng, g_tml, c.n + 1)
            w1_part(eng, c, 2, tm_t_h, tm_t_l, False).then_inc(p_w1t, 1)

        def pe_w1_ms(eng, c):
            wait(eng, g_msl, c.n + 1)
            w1_part(eng, c, 6, ms_t_h, ms_t_l, False).then_inc(p_w1m, 1)

        def pe_w1_h(eng, c):
            wait(eng, v_hl, c.n + 1)
            w1_part(eng, c, 0, h_t_h, h_t_l, True).then_inc(p_w1, 1)

        def pe_w2(eng, c):
            wait(eng, v_sill, c.n + 1)
            out = rows_of(ps_d)
            for j in range(CT):
                cut = slice(j * P, (j + 1) * P)
                eng.matmul(out[:, j, :], ones3[:, :], b2_row[:, :], start=True, stop=False)
                for k in range(KB):
                    m = product(eng, out[:, j, :], (act_t_h[:, k, cut], act_t_l[:, k, cut]),
                                (w2_h[:, k, :], w2_l[:, k, :]), False, k == KB - 1)
            m.then_inc(p_w2, 1)

        def act_th(eng, c):
            wait(eng, v_t, c.n + 1)
            wait(eng, p_x1, c.n)
            for n in range(2):
                m = eng.activation(t_st[n * RP:n * RP + RK, :], t_t[:, :], ACT.Copy)
            m.then_inc(a_th, 1)

        def act_relu(eng, c):
            wait(eng, v_dn, c.n + 1)
            wait(eng, p_up, c.n)
            d = dn[:, :].rearrange("h (k e s) -> h k e s", e=2, s=S)
            eng.activation(act_bd[0:HID, :, 0:S], d[:, :, 0, :], ACT.Relu)
            eng.activation(act_bd[HID:P, :, S:P], d[:, :, 1, :], ACT.Relu).then_inc(a_relu, 1)

        def act_x3(eng, c):
            wait(eng, p_up, c.n + 1)
            wait(eng, p_x3t, c.n)
            wait(eng, a_xhat, c.n)
            wait(eng, g_x3be, c.n)
            eng.activation(x3[:, :, :], rows_of(ps_b), ACT.Copy).then_inc(a_x3, 1)

        def act_x3t(eng, c):
            wait(eng, p_x3t, c.n + 1)
            wait(eng, p_w1x, c.n)
            eng.activation(x3_t_h[:, :, :], ps_b[:, :, :], ACT.Copy).then_inc(a_x3h, 1)

        def act_xht(eng, c):
            wait(eng, p_xht, c.n + 1)
            wait(eng, v_ms, c.n)
            eng.activation(xh_t[:, :, :], ps_c[:, :, :], ACT.Copy).then_inc(a_xht, 1)

        def act_hht(eng, c):
            wait(eng, p_hht, c.n + 1)
            wait(eng, v_sill, c.n)
            eng.activation(hh_t[:, :, :], ps_c[:, :, :], ACT.Copy).then_inc(a_hht, 1)

        def normalise(eng, k, out, src):
            for j in range(CT):
                m = eng.activation(out[:, j, :], src[:, j, :], ACT.Identity, bias=nb[k][:, j:j + 1],
                                   scale=rstd[k][:, j:j + 1])
            return m

        def act_xnorm(eng, c):
            wait(eng, v_xnb, c.n + 1)
            wait(eng, p_xht, c.n)
            wait(eng, g_h1m, c.n)
            normalise(eng, "x", xhat, x3).then_inc(a_xhat, 1)

        def act_hnorm(eng, c):
            wait(eng, v_hnb, c.n + 1)
            normalise(eng, "h", h1, h1).then_inc(a_hhat, 1)

        def high(out, src, s_src, s_free, s_done):
            def stage(eng, c):
                wait(eng, s_src, c.n + 1)
                wait(eng, s_free, c.n)
                eng.activation(out[:, :, :], src[:, :, :], ACT.Copy).then_inc(s_done, 1)
            return stage

        act_xmh = high(xm_t_h, xm_t, g_xm, p_l1, a_xmh)
        act_x2h = high(x2_t_h, x2_t, v_x2, p_up, a_x2h)
        act_tmh = high(tm_t_h, tm_t, v_tm, p_w1t, a_tmh)
        act_msh = high(ms_t_h, ms_t, v_ms, p_w1m, a_msh)
        act_hh = high(h_t_h, h_t, v_h, p_w1, a_hh)

        def act_silu(eng, c):
            wait(eng, p_w1, c.n + 1)
            wait(eng, v_sill, c.n)
            for k in range(KB):
                m = eng.activation(act_t[:, k, :], ps_d[:, k, :], ACT.Silu, bias=b1[:, k:k + 1])
            m.then_inc(a_silu, 1)

        def act_silh(eng, c):
            wait(eng, p_w2, c.n)
            wait(eng, a_silu, c.n + 1)
            eng.activation(act_t_h[:, :, :], act_t[:, :, :], ACT.Copy).then_inc(a_silh, 1)

        def act_onehot(eng, c):
            wait(eng, s_idx[c.ring], 32 * (c.half + 1))
            eng.activation(oh_sq[:, :], idx_ch[c.ring][:, :], ACT.Square, bias=cls_neg[:, 0:1]).then_inc(a_sq, 1)
            wait(eng, a_sq, c.n + 1)
            wait(eng, p_w1, c.n - 1)
            eng.activation(onehot[c.ring][0:CLS, :], oh_sq[:, :], ACT.Relu, bias=1.0, scale=-1.0).then_inc(a_oh, 1)

        def v_down(eng, c):
            wait(eng, p_dn, c.n + 1)
            wait(eng, a_relu, c.n)
            def half(ap):
                return ap.rearrange("p (b s) -> p b s", s=S)
            def dtab(lo):
                return dgdb[lo:lo + HID, bass.ds(c.n * CB, CB)].unsqueeze(2).broadcast_to([HID, CB, S])
            eng.tensor_tensor(half(dn_u[:, :]), half(ps_b[0:HID, 0, :]), dtab(0), ALU.mult)
            eng.tensor_tensor(half(dn_v[:, :]), half(ps_b[HID:P, 0, :]), dtab(HID), ALU.mult).then_inc(v_dnu, 1)
            eng.wait_ge(v_dnu, c.n + 1)
            eng.tensor_tensor(dn[:, :], dn_u[:, :], dn_v[:, :], ALU.add).then_inc(v_dn, 1)

        def v_tadd(eng, c):
            wait(eng, p_t, c.n + 1)
            wait(eng, v_tl, c.n)
            ub = ub_t[:, bass.ds(c.n * CB, CB)].unsqueeze(2).broadcast_to([RK, CB, S])
            eng.tensor_tensor(t_t[:, :].rearrange("p (b s) -> p b s", s=S),
                              ps_a[0:RK, 0, :].rearrange("p (b s) -> p b s", s=S), ub, ALU.add).then_inc(v_t, 1)

        def v_tlow(eng, c):
            wait(eng, a_th, c.n + 1)
            eng.tensor_tensor(t_st[2 * RP:2 * RP + RK, :], t_t[:, :], t_st[0:RK, :].bitcast(F32),
                              ALU.subtract).then_inc(v_tl, 1)

        def v_hprod(eng, c):
            wait(eng, a_hht, c.n + 1)
            wait(eng, p_cp, c.n + 1)
            wait(eng, g_tml, c.n + 1)
            eng.tensor_tensor(h_t[:, :, :], ps_c[:, :, :], hh_t[:, :, :], ALU.mult).then_inc(v_h, 1)

        def v_x1add(eng, c):
            wait(eng, p_x1, c.n + 1)
            wait(eng, v_x2l, c.n)
            eng.tensor_tensor(x1_t[:, :, :], ps_a[:, :, :], x_t[c.ring][:, :, :], ALU.add).then_inc(v_x1, 1)

        def stats(eng, c, k, src, s_bn, s_mv, s_ve):
            for j in range(CT):
                m = eng.bn_stats(bn[k][:, j, :], src[:, j, :])
            m.then_inc(s_bn, 1)
            eng.wait_ge(s_bn, c.n + 1)
            settle(eng, s_idle)
            for j in range(CT):
                m = eng.bn_aggr(mv[k][:, j, :], bn[k][:, j, :])
            m.then_inc(s_mv, 1)
            eng.wait_ge(s_mv, c.n + 1)
            eng.tensor_scalar(ve[k][:, :], mv[k][:, :, 1], EPS, None, ALU.add).then_inc(s_ve, 1)

        def offsets(eng, c, k, s_r, s_nb):
            wait(eng, s_r, c.n + 1)
            eng.scalar_tensor_tensor(nb[k][:, :], mv[k][:, :, 0], -1.0, rstd[k][:, :], ALU.mult, ALU.mult)\
               .then_inc(s_nb, 1)

        def v_xstat(eng, c):
            wait(eng, a_x3, c.n + 1)
            wait(eng, g_rx, c.n)
            stats(eng, c, "x", x3, v_bnx, v_mvx, v_vex)

        def v_xoff(eng, c):
            wait(eng, a_xhat, c.n)
            offsets(eng, c, "x", g_rx, v_xnb)

        def v_hstat(eng, c):
            wait(eng, g_h1, c.n + 1)
            wait(eng, g_rh, c.n)
            stats(eng, c, "h", h1, v_bnh, v_mvh, v_veh)

        def v_hoff(eng, c):
            wait(eng, a_hhat, c.n)
            offsets(eng, c, "h", g_rh, v_hnb)

        def v_l1(eng, c):
            wait(eng, p_l1, c.n + 1)
            eng.tensor_tensor(by_entry(l1_u[:, :, :]), by_entry(ps_a[:, :, :]), cols(dcoef, c),
                              ALU.mult).then_inc(v_l1u, 1)
            eng.wait_ge(v_l1u, c.n + 1)
            for k in range(KB):
                m = eng.tensor_scalar(l1_u[:, k, :], l1_u[:, k, :], l1_b[:, k:k + 1], CLAMP, ALU.add, ALU.min)
            m.then_inc(v_l1v, 1)
            eng.wait_ge(v_l1v, c.n + 1)
            wait(eng, g_xm, c.n + 1)
            eng.scalar_tensor_tensor(x2_t[:, :, :], l1_u[:, :, :], -CLAMP, x1_t[:, :, :],
                                     ALU.max, ALU.add).then_inc(v_x2, 1)

        def v_tmprod(eng, c):
            wait(eng, a_xht, c.n + 1)
            wait(eng, v_hl, c.n)
            wait(eng, p_tm, c.n + 1)
            eng.tensor_tensor(tm_t[:, :, :], ps_c[:, :, :], xh_t[:, :, :], ALU.mult).then_inc(v_tm, 1)

        def v_msprod(eng, c):
            wait(eng, a_xht, c.n + 1)
            wait(eng, g_msl, c.n)
            wait(eng, p_ms, c.n + 1)
            eng.tensor_tensor(ms_t[:, :, :], ps_b[:, :, :], xh_t[:, :, :], ALU.mult).then_inc(v_ms, 1)

        def low(out, src, high_half, s_high, s_free, s_done):
            def stage(eng, c):
                wait(eng, s_high, c.n + 1)
                wait(eng, s_free, c.n)
                eng.tensor_tensor(out[:, :, :], src[:, :, :], high_half[:, :, :].bitcast(F32),
                                  ALU.subtract).then_inc(s_done, 1)
            return stage

        v_xml_ = low(xm_t_l, xm_t, xm_t_h, a_xmh, p_l1, v_xml)
        v_x2l_ = low(x2_t_l, x2_t, x2_t_h, a_x2h, p_up, v_x2l)
        v_x3l_ = low(x3_t_l, ps_b, x3_t_h, a_x3h, p_w1x, v_x3l)
        g_tml_ = low(tm_t_l, tm_t, tm_t_h, a_tmh, p_w1t, g_tml)
        g_msl_ = low(ms_t_l, ms_t, ms_t_h, a_msh, p_w1m, g_msl)
        v_hl_ = low(h_t_l, h_t, h_t_h, a_hh, p_w1, v_hl)
        v_sill_ = low(act_t_l, act_t, act_t_h, a_silh, p_w2, v_sill)

        def v_ystat(eng, c):
            wait(eng, p_w2, c.n + 1)
            wait(eng, g_ry, c.n)
            stats(eng, c, "y", rows_of(ps_d), v_bny, v_mvy, v_vey)

        def v_ycentre(eng, c):
            eng.wait_ge(v_mvy, c.n + 1)
            wait(eng, s_store[c.ring], 16 * c.half)
            for j in range(CT):
                m = eng.scalar_tensor_tensor(y_out[c.ring][:, j, :], rows_of(ps_d)[:, j, :], mv["y"][:, j, 0:1],
                                             ln_g[:, :], ALU.subtract, ALU.mult)
            m.then_inc(v_y1, 1)

        def v_ynorm(eng, c):
            wait(eng, v_y1, c.n + 1)
            wait(eng, g_ry, c.n + 1)
            wait(eng, g_x3be, c.n + 1)
            for j in range(CT):
                m = eng.scalar_tensor_tensor(y_out[c.ring][:, j, :], y_out[c.ring][:, j, :], rstd["y"][:, j:j + 1],
                                             x3be[c.ring][:, j, :], ALU.mult, ALU.add)
            m.then_inc(v_y, 1)

        def g_gather(eng, c):
            wait(eng, g_h1, c.n)
            wait(eng, s_pw, 16 * CT * c.n)
            eng.tensor_copy(gidx[:, :], pw_idx[:, bass.ds(c.n * CT, CT)]).then_inc(g_gidx, 1)
            eng.wait_ge(g_gidx, c.n + 1)
            settle(eng, s_idle)
            for j in range(CT):
                eng.indirect_dma_start(pw_rows[:, j, :], None, t["pw"],
                                       bass.IndirectOffsetOnAxis(ap=gidx[:, j:j + 1], axis=0)).then_inc(s_pw, 16)

        def g_style(eng, c):
            wait(eng, v_x1, c.n + 1)
            wait(eng, v_x2, c.n)
            eng.tensor_tensor(by_entry(xm_t[:, :, :]), by_entry(x1_t[:, :, :]), cols(style, c),
                              ALU.mult).then_inc(g_xm, 1)

        def root(eng, c, k, s_ve, s_r):
            wait(eng, s_ve, c.n + 1)
            eng.tensor_tensor(rstd[k][:, :], ve[k][:, :], mhalf[:, :], ALU.pow).then_inc(s_r, 1)

        def g_rootx(eng, c):
            wait(eng, a_xhat, c.n)
            root(eng, c, "x", v_vex, g_rx)

        def g_h(eng, c):
            wait(eng, a_xhat, c.n + 1)
            wait(eng, s_pw, 16 * CT * (c.n + 1))
            wait(eng, p_hht, c.n)
            eng.tensor_tensor(h1[:, :, :], xhat[:, :, :], pw_rows[:, :, 0:D], ALU.mult).then_inc(g_h1m, 1)
            eng.wait_ge(g_h1m, c.n + 1)
            eng.tensor_tensor(h1[:, :, :], h1[:, :, :], pw_rows[:, :, D:2 * D], ALU.add).then_inc(g_h1, 1)

        def g_rooth(eng, c):
            root(eng, c, "h", v_veh, g_rh)

        def g_wup(eng, c):
            wait(eng, s_ug, 32 * (c.n + 1))
            wait(eng, p_up, c.n)
            q = up_rep[:, :].unsqueeze(1).broadcast_to([P, CT, D])
            eng.tensor_tensor(w_up[:, :, :], q, ugub[:, :, 0:D], ALU.mult).then_inc(g_upm, 1)
            eng.wait_ge(g_upm, c.n + 1)
            eng.tensor_tensor(w_up[:, :, :], w_up[:, :, :], ugub[:, :, D:2 * D], ALU.add).then_inc(g_up, 1)

        def g_res(eng, c):
            wait(eng, a_x3, c.n + 1)
            wait(eng, v_y, c.n - 1)
            eng.tensor_tensor(x3be[c.ring][:, :, :], x3[:, :, :], ln_be[:, :].unsqueeze(1).broadcast_to([P, CT, D]),
                              ALU.add).then_inc(g_x3be, 1)

        def g_rooty(eng, c):
            wait(eng, v_y, c.n)
            root(eng, c, "y", v_vey, g_ry)

        block = ctx.enter_context(nc.Block())

        @block.sync
        def _(eng):
            run_slots(eng, [(load_up, 1), (load, 0), (load_shift, 1), (store, 4)])
            for r in range(2):
                eng.wait_ge(s_store[r], 16 * NCH // 2)

        @block.tensor
        def _(eng):
            run_slots(eng, [(pe_ms, 3), (pe_xht, 3), (pe_w1_ms, 4), (pe_w1_h, 4), (pe_tm, 3), (pe_t, 1),
                            (pe_dn, 2), (pe_w2, 4), (pe_hhat, 3), (pe_up, 2), (pe_x1, 1), (pe_cp, 3),
                            (pe_w1_x3, 3), (pe_x3t, 2), (pe_w1_tm, 3), (pe_l1, 1)])

        @block.scalar
        def _(eng):
            run_slots(eng, [(act_silu, 4), (act_silh, 4), (act_onehot, 2), (act_msh, 3), (act_hnorm, 3),
                            (act_relu, 2), (act_th, 1), (act_hht, 3), (act_tmh, 3), (act_x3, 2), (act_xmh, 1),
                            (act_x3t, 2), (act_xnorm, 2), (act_hh, 3), (act_xht, 2), (act_x2h, 1)])

        @block.vector
        def _(eng):
            run_slots(eng, [(v_tadd, 1), (v_ystat, 4), (v_tlow, 1), (v_ycentre, 4), (v_x1add, 1), (v_xstat, 2),
                            (v_hprod, 3), (v_xoff, 2), (v_xml_, 1), (v_x3l_, 2), (v_ynorm, 4), (v_hl_, 3),
                            (v_l1, 1), (v_msprod, 2), (v_hstat, 2), (v_x2l_, 1), (v_tmprod, 2), (v_sill_, 3),
                            (v_hoff, 2), (v_down, 1)])

        @block.gpsimd
        def _(eng):
            run_slots(eng, [(g_style, 2), (g_rootx, 3), (g_wup, 2), (g_h, 3), (g_gather, 2), (g_rooth, 3),
                            (g_res, 3), (g_msl_, 3), (g_rooty, 4), (g_tml_, 3)])


def kernel(**inputs):
    import numpy as np
    import ml_dtypes
    import concourse.bacc as bacc
    from concourse import mybir
    from concourse.bass_utils import run_bass_kernel_spmd

    a = {n: np.asarray(v) for n, v in inputs.items()}
    lay = np.ascontiguousarray

    def by_block(v):
        return lay(v.reshape(KB, P).T)

    ncls = PIECES * (NCP + NMS)
    cls_id = np.concatenate([np.tile(np.arange(NCP), PIECES), np.tile(np.arange(NMS), PIECES)])
    piece = np.concatenate([np.repeat(np.arange(PIECES), NCP), np.repeat(np.arange(PIECES), NMS)])
    entry = np.repeat(np.arange(CB), PIECES)
    arrays = {
        "ident": np.eye(P, dtype=np.float32),
        "cls_const": np.concatenate([-cls_id[:, None], piece[:, None] == np.arange(PIECES)[None, :]],
                                    axis=1).astype(np.float32),
        "entry_rows": (entry[:, None] == np.repeat(np.arange(CB), S)[None, :]).astype(ml_dtypes.bfloat16),
    }
    l3 = {n[len("L3_cond_"):]: v for n, v in a.items() if n.startswith("L3_cond_")}
    nets = ("mem", "noi", "res")
    arrays.update({
        "x_t": lay(a["x"].reshape(ROWS, D).T),
        "itok_t": lay(a["itok_BxS_0_999"].reshape(ROWS // P, P).T),
        "itok4": a["itok_BxS_0_4"].reshape(ROWS),
        "mask": a["mask_BxS_ik0"].reshape(ROWS),
        "cond_side": np.concatenate([a["cond_512"].T, a["L1_cond_affine_w"].T, a["L2_cond_down_gamma"],
                                     a["L2_cond_down_beta"], a["L2_cond_up_gamma"], a["L2_cond_up_beta"]], axis=1),
        "bias_cols": np.concatenate([by_block(v) for v in (
            a["L1_cond_bias"], l3["int_b1"], a["L1_cond_affine_b"], *(l3[n + "_b1"] for n in nets))], axis=1),
        "W_dec": a["L0_cond_W_dec"], "b_dec": a["L0_cond_b_dec"],
        "V3": np.concatenate([a["L0_cond_V"], np.zeros((RP - RK, D), np.float32)] * 3, axis=0),
        "l1_wt": a["L1_cond_weight"].T,
        "down_p": a["L2_cond_down_project"],
        "up_p2": np.concatenate([a["L2_cond_up_project"]] * 2, axis=0),
        "mem_W1": l3["mem_W1"],
        "nr_W1": np.concatenate([l3["noi_W1"], l3["res_W1"]], axis=0),
        "nr_t": np.concatenate([a["cond_64"].T, a["fside_Bx32_0"].T], axis=0),
        "nets_W2": np.concatenate([l3[n + "_W2"] for n in nets], axis=0),
        "nets_rows": np.concatenate([l3[n + part] for n in nets for part in ("_b2", "_g", "_be")]),
        "pw": np.concatenate([l3["pw_g"], l3["pw_b"]], axis=1),
        "cptm_g": np.concatenate([np.concatenate([l3["cp_g"], l3["tm_g"]], axis=1)] * PIECES, axis=0),
        "ms_g": np.concatenate([l3["ms_g"]] * PIECES, axis=0),
        "cp_bt": np.concatenate([l3["cp_b"].T] * PIECES, axis=1),
        "tm_bt": np.concatenate([l3["tm_b"].T] * PIECES, axis=1),
        "ms_bt": np.concatenate([l3["ms_b"].T] * PIECES, axis=1),
        "int_W1": l3["int_W1"], "int_W2": l3["int_W2"], "int_b2": l3["int_b2"],
        "int_gb": np.concatenate([l3["int_g"], l3["int_be"]]),
        "aw": l3["aw"],
    })

    nc = bacc.Bacc("TRN2", target_bir_lowering=False, num_devices=1)
    t, placed = {}, {}
    for name, v in arrays.items():
        v = lay(v)
        placed["in_" + name] = v
        t[name] = nc.dram_tensor("in_" + name, v.shape, mybir.dt.from_np(v.dtype), kind="ExternalInput").ap()
    t["out"] = nc.dram_tensor("out", (ROWS, D), mybir.dt.float32, kind="ExternalOutput").ap()
    conditioned_residuals(nc, t)
    r = run_bass_kernel_spmd(nc, [placed], core_ids=[0])
    return r.results[0]["out"].reshape(B, S, D)
```
